# Optimizing a Trainium2 kernel written in Bass

```python
import numpy as np
import jax
import jax.numpy as jnp

def _softmax(x, axis=-1):
    return jax.nn.softmax(x, axis=axis)

def _gelu(x):
    return jax.nn.gelu(x, approximate=True)

def _silu(x):
    return jax.nn.silu(x)

def _sigmoid(x):
    return jax.nn.sigmoid(x)

def _layernorm(x, axis=-1, eps=1e-05):
    m = jnp.mean(x, axis=axis, keepdims=True)
    v = jnp.var(x, axis=axis, keepdims=True)
    return (x - m) / jnp.sqrt(v + eps)

def _scatter_add(tgt, idx, src, axis=0):
    return tgt.at[idx].add(src)

def _segment_sum(src, seg, n):
    return jax.ops.segment_sum(src, seg, n)
kernel_name = 'mk_sandwich_d2_jaxref_r8_1cc07a'

def setup_inputs(seed: int=0):
    np.random.seed(seed)
    _w = jnp.asarray

    def _L0_attn_setup():
        import jax, jax.numpy as jnp
        import numpy as np
        HIDDEN = 512
        NUM_HEADS = 32
        HEAD_DIM = HIDDEN // NUM_HEADS
        B, S = (2, 128)

        def _alibi_slopes(n):
            start = 2.0 ** (-2.0 ** (-(np.log2(n) - 3)))
            return np.array([start ** (i + 1) for i in range(n)], dtype=np.float32)
        key = jax.random.key(seed)
        k1, k2, k3, k4 = jax.random.split(key, 4)
        hidden_states = jax.random.normal(k1, (B, S, HIDDEN), jnp.float32)
        Wq = jax.random.normal(k2, (HIDDEN, HIDDEN), jnp.float32) * 0.02
        Wkv = jax.random.normal(k3, (HIDDEN, 2 * HEAD_DIM), jnp.float32) * 0.02
        Wo = jax.random.normal(k4, (HIDDEN, HIDDEN), jnp.float32) * 0.02
        return {'hidden_states': hidden_states, 'Wq': Wq, 'Wkv': Wkv, 'Wo': Wo}
    _L0_attn_in = _L0_attn_setup()

    def _L0_ffn_setup():
        import jax, jax.numpy as jnp
        import numpy as np
        BLOCK = 32

        def _dequantize(q_scales, q_vals):
            OUT, n_blocks = q_scales.shape
            codes = q_vals.astype(jnp.float32) - 128.0
            w = q_scales[:, :, None] * codes
            return w.reshape(OUT, n_blocks * BLOCK)
        key = jax.random.key(seed)
        k1, k2, k3, k4 = jax.random.split(key, 4)
        B, S, IN, OUT = (2, 512, 512, 512)
        n_blocks = IN // BLOCK
        x = jax.random.normal(k1, (B, S, IN), dtype=jnp.float32)
        q_scales = jax.random.uniform(k2, (OUT, n_blocks), dtype=jnp.float32) * 0.05
        q_vals = jax.random.randint(k3, (OUT, n_blocks, BLOCK), 0, 32, dtype=jnp.int32)
        bias = jax.random.normal(k4, (OUT,), dtype=jnp.float32)
        return {'x': x, 'q_scales': q_scales, 'q_vals': q_vals, 'bias': bias}
    _L0_ffn_in = _L0_ffn_setup()

    def _L1_attn_setup():
        import jax, jax.numpy as jnp
        import numpy as np
        HIDDEN = 512
        N_HEADS = 32
        KV_HEADS = 8
        HEAD_DIM = 128
        LOW_RANK = 64
        TOP_K_ROPE = 32
        ROPE_THETA = 10000.0
        B, S = (2, 256)
        GROUPS = N_HEADS // KV_HEADS
        _half = HEAD_DIM // 2
        _m = np.ones(_half, dtype=bool)
        _m[:TOP_K_ROPE] = False
        _m = np.concatenate([_m, _m])
        NOPE_MASK = np.tile(_m, KV_HEADS)
        ROPE_IDX = jnp.asarray(np.where(~NOPE_MASK)[0])
        NOPE_IDX = jnp.asarray(np.where(NOPE_MASK)[0])
        R_DIM = int((~NOPE_MASK).sum())
        C_DIM = LOW_RANK * KV_HEADS

        def _rope_tables(seq_len, dtype):
            inv_freq = 1.0 / ROPE_THETA ** (np.arange(0, HEAD_DIM, 2, dtype=np.float32) / HEAD_DIM)
            pos = np.arange(seq_len, dtype=np.float32)
            freqs = np.outer(pos, inv_freq)
            emb = np.concatenate([freqs, freqs], axis=-1)
            return (jnp.asarray(np.cos(emb), dtype), jnp.asarray(np.sin(emb), dtype))

        def _rotate_half(x):
            x1, x2 = (x[..., :HEAD_DIM // 2], x[..., HEAD_DIM // 2:])
            return jnp.concatenate([-x2, x1], axis=-1)
        key = jax.random.key(seed)
        ks = jax.random.split(key, 7)
        s = 0.02
        return {'hidden_states': jax.random.normal(ks[0], (B, S, HIDDEN), jnp.float32), 'Wq': jax.random.normal(ks[1], (N_HEADS * HEAD_DIM, HIDDEN), jnp.float32) * s, 'Wkr': jax.random.normal(ks[2], (R_DIM, HIDDEN), jnp.float32) * s, 'Wdk': jax.random.normal(ks[3], (C_DIM, HIDDEN), jnp.float32) * s, 'Wupk': jax.random.normal(ks[4], (KV_HEADS * HEAD_DIM - R_DIM, C_DIM), jnp.float32) * s, 'Wupv': jax.random.normal(ks[5], (KV_HEADS * HEAD_DIM, C_DIM), jnp.float32) * s, 'Wo': jax.random.normal(ks[6], (HIDDEN, N_HEADS * HEAD_DIM), jnp.float32) * s}
    _L1_attn_in = _L1_attn_setup()

    def _L1_ffn_setup():
        import jax, jax.numpy as jnp
        import numpy as np
        _TRIPLES = [(1, 2, 3), (1, 4, 5), (1, 7, 6), (2, 4, 6), (2, 5, 7), (3, 4, 7), (3, 6, 5)]

        def _oct_struct():
            S = np.zeros((8, 8, 8), np.float32)
            S[0, 0, 0] = 1.0
            for i in range(1, 8):
                S[0, i, i] = 1.0
                S[i, 0, i] = 1.0
                S[i, i, 0] = -1.0
            for a, b, c in _TRIPLES:
                for x, y, z in ((a, b, c), (b, c, a), (c, a, b)):
                    S[x, y, z] = 1.0
                    S[y, x, z] = -1.0
            return jnp.asarray(S)
        S_OCT = _oct_struct()
        N_EMBD = 512
        HIDDEN = 1366

        def ternary_dequant(W):
            scale = jnp.mean(jnp.abs(W))
            Wq = scale * jnp.clip(jnp.round(W / scale), -1.0, 1.0)
            return W + jax.lax.stop_gradient(Wq - W)

        def oct_ternary_linear(xp, W):
            Wq = ternary_dequant(W)
            M = jnp.einsum('jik,jod->koid', S_OCT, Wq)
            return jnp.einsum('...id,koid->...ko', xp, M)
        key = jax.random.key(seed)
        k1, k2, k3, k4 = jax.random.split(key, 4)
        B, T = (2, 256)
        d8, h8 = (N_EMBD // 8, HIDDEN // 8)
        std_in = 1.0 / np.sqrt(N_EMBD)
        std_h = 1.0 / np.sqrt(HIDDEN)
        return {'x': jax.random.normal(k1, (B, T, N_EMBD), jnp.float32), 'w_gate': jax.random.normal(k2, (8, h8, d8), jnp.float32) * std_in, 'w_up': jax.random.normal(k3, (8, h8, d8), jnp.float32) * std_in, 'w_down': jax.random.normal(k4, (8, d8, h8), jnp.float32) * std_h}
    _L1_ffn_in = _L1_ffn_setup()
    _d = {'L0_attn_hidden_states': _L0_attn_in['hidden_states'], 'L0_attn_Wq': _L0_attn_in['Wq'], 'L0_attn_Wkv': _L0_attn_in['Wkv'], 'L0_attn_Wo': _L0_attn_in['Wo'], 'L0_ffn_q_scales': _L0_ffn_in['q_scales'], 'L0_ffn_q_vals': _L0_ffn_in['q_vals'], 'L0_ffn_bias': _L0_ffn_in['bias'], 'L1_attn_Wq': _L1_attn_in['Wq'], 'L1_attn_Wkr': _L1_attn_in['Wkr'], 'L1_attn_Wdk': _L1_attn_in['Wdk'], 'L1_attn_Wupk': _L1_attn_in['Wupk'], 'L1_attn_Wupv': _L1_attn_in['Wupv'], 'L1_attn_Wo': _L1_attn_in['Wo'], 'L1_ffn_w_gate': _L1_ffn_in['w_gate'], 'L1_ffn_w_up': _L1_ffn_in['w_up'], 'L1_ffn_w_down': _L1_ffn_in['w_down']}
    _x0 = _d['L0_attn_hidden_states']
    _d['L0_attn_hidden_states'] = jax.random.normal(jax.random.fold_in(jax.random.key(seed), 1), (4, 512, 512), dtype=_x0.dtype)
    del _x0
    return _d

def reference(L0_attn_hidden_states, L0_attn_Wq, L0_attn_Wkv, L0_attn_Wo, L0_ffn_q_scales, L0_ffn_q_vals, L0_ffn_bias, L1_attn_Wq, L1_attn_Wkr, L1_attn_Wdk, L1_attn_Wupk, L1_attn_Wupv, L1_attn_Wo, L1_ffn_w_gate, L1_ffn_w_up, L1_ffn_w_down):

    def _L0_attn_ref(hidden_states, Wq, Wkv, Wo):
        import jax, jax.numpy as jnp
        import numpy as np
        HIDDEN = 512
        NUM_HEADS = 32
        HEAD_DIM = HIDDEN // NUM_HEADS
        B, S = (2, 128)

        def _alibi_slopes(n):
            start = 2.0 ** (-2.0 ** (-(np.log2(n) - 3)))
            return np.array([start ** (i + 1) for i in range(n)], dtype=np.float32)
        b, s, h = hidden_states.shape
        scale = HEAD_DIM ** (-0.5)
        q = (hidden_states @ Wq).reshape(b, s, NUM_HEADS, HEAD_DIM)
        kv = hidden_states @ Wkv
        k, v = (kv[..., :HEAD_DIM], kv[..., HEAD_DIM:])
        scores = jnp.einsum('bqhd,bkd->bhqk', q, k) * scale
        pos = jnp.arange(s)
        slopes = jnp.asarray(_alibi_slopes(NUM_HEADS))
        bias = slopes[:, None, None] * (pos[None, None, :] - pos[None, :, None]).astype(jnp.float32)
        causal = pos[None, :] <= pos[:, None]
        scores = jnp.where(causal[None, None], scores + bias[None], -jnp.inf)
        attn = jax.nn.softmax(scores, axis=-1)
        out = jnp.einsum('bhqk,bkd->bqhd', attn, v).reshape(b, s, h)
        return out @ Wo

    def _L0_ffn_ref(x, q_scales, q_vals, bias):
        import jax, jax.numpy as jnp
        import numpy as np
        BLOCK = 32

        def _dequantize(q_scales, q_vals):
            OUT, n_blocks = q_scales.shape
            codes = q_vals.astype(jnp.float32) - 128.0
            w = q_scales[:, :, None] * codes
            return w.reshape(OUT, n_blocks * BLOCK)
        W = _dequantize(q_scales, q_vals)
        out = jnp.einsum('bsi,oi->bso', x, W) + bias
        return out

    def _L1_attn_ref(hidden_states, Wq, Wkr, Wdk, Wupk, Wupv, Wo):
        import jax, jax.numpy as jnp
        import numpy as np
        HIDDEN = 512
        N_HEADS = 32
        KV_HEADS = 8
        HEAD_DIM = 128
        LOW_RANK = 64
        TOP_K_ROPE = 32
        ROPE_THETA = 10000.0
        B, S = (2, 256)
        GROUPS = N_HEADS // KV_HEADS
        _half = HEAD_DIM // 2
        _m = np.ones(_half, dtype=bool)
        _m[:TOP_K_ROPE] = False
        _m = np.concatenate([_m, _m])
        NOPE_MASK = np.tile(_m, KV_HEADS)
        ROPE_IDX = jnp.asarray(np.where(~NOPE_MASK)[0])
        NOPE_IDX = jnp.asarray(np.where(NOPE_MASK)[0])
        R_DIM = int((~NOPE_MASK).sum())
        C_DIM = LOW_RANK * KV_HEADS

        def _rope_tables(seq_len, dtype):
            inv_freq = 1.0 / ROPE_THETA ** (np.arange(0, HEAD_DIM, 2, dtype=np.float32) / HEAD_DIM)
            pos = np.arange(seq_len, dtype=np.float32)
            freqs = np.outer(pos, inv_freq)
            emb = np.concatenate([freqs, freqs], axis=-1)
            return (jnp.asarray(np.cos(emb), dtype), jnp.asarray(np.sin(emb), dtype))

        def _rotate_half(x):
            x1, x2 = (x[..., :HEAD_DIM // 2], x[..., HEAD_DIM // 2:])
            return jnp.concatenate([-x2, x1], axis=-1)
        bsz, q_len, _ = hidden_states.shape
        dt = hidden_states.dtype
        q = (hidden_states @ Wq.T).reshape(bsz, q_len, N_HEADS, HEAD_DIM).transpose(0, 2, 1, 3)
        k_r0 = hidden_states @ Wkr.T
        key_flat = jnp.zeros((bsz, q_len, KV_HEADS * HEAD_DIM), dt).at[..., ROPE_IDX].set(k_r0)
        k = key_flat.reshape(bsz, q_len, KV_HEADS, HEAD_DIM).transpose(0, 2, 1, 3)
        cos, sin = _rope_tables(q_len, dt)
        cos, sin = (cos[None, None], sin[None, None])
        q = q * cos + _rotate_half(q) * sin
        k = k * cos + _rotate_half(k) * sin
        k_r = k.transpose(0, 2, 1, 3).reshape(bsz, q_len, KV_HEADS * HEAD_DIM)[..., ROPE_IDX]
        c_kv = hidden_states @ Wdk.T
        k_c = c_kv @ Wupk.T
        v = (c_kv @ Wupv.T).reshape(bsz, q_len, KV_HEADS, HEAD_DIM).transpose(0, 2, 1, 3)
        key_full = jnp.zeros((bsz, q_len, KV_HEADS * HEAD_DIM), dt).at[..., NOPE_IDX].set(k_c).at[..., ROPE_IDX].set(k_r)
        k = key_full.reshape(bsz, q_len, KV_HEADS, HEAD_DIM).transpose(0, 2, 1, 3)
        k = jnp.repeat(k, GROUPS, axis=1)
        v = jnp.repeat(v, GROUPS, axis=1)
        scale = 1.0 / jnp.sqrt(jnp.asarray(HEAD_DIM, dt))
        scores = jnp.einsum('bhqd,bhkd->bhqk', q, k) * scale
        causal = jnp.tril(jnp.ones((q_len, q_len), bool))
        scores = jnp.where(causal[None, None], scores, jnp.asarray(-1000000000.0, dt))
        attn = jax.nn.softmax(scores, axis=-1)
        out = jnp.einsum('bhqk,bhkd->bhqd', attn, v)
        out = out.transpose(0, 2, 1, 3).reshape(bsz, q_len, N_HEADS * HEAD_DIM)
        return out @ Wo.T

    def _L1_ffn_ref(x, w_gate, w_up, w_down):
        import jax, jax.numpy as jnp
        import numpy as np
        _TRIPLES = [(1, 2, 3), (1, 4, 5), (1, 7, 6), (2, 4, 6), (2, 5, 7), (3, 4, 7), (3, 6, 5)]

        def _oct_struct():
            S = np.zeros((8, 8, 8), np.float32)
            S[0, 0, 0] = 1.0
            for i in range(1, 8):
                S[0, i, i] = 1.0
                S[i, 0, i] = 1.0
                S[i, i, 0] = -1.0
            for a, b, c in _TRIPLES:
                for x, y, z in ((a, b, c), (b, c, a), (c, a, b)):
                    S[x, y, z] = 1.0
                    S[y, x, z] = -1.0
            return jnp.asarray(S)
        S_OCT = _oct_struct()
        N_EMBD = 512
        HIDDEN = 1366

        def ternary_dequant(W):
            scale = jnp.mean(jnp.abs(W))
            Wq = scale * jnp.clip(jnp.round(W / scale), -1.0, 1.0)
            return W + jax.lax.stop_gradient(Wq - W)

        def oct_ternary_linear(xp, W):
            Wq = ternary_dequant(W)
            M = jnp.einsum('jik,jod->koid', S_OCT, Wq)
            return jnp.einsum('...id,koid->...ko', xp, M)
        B, T, D = x.shape
        xp = x.reshape(B, T, 8, D // 8)
        gate = oct_ternary_linear(xp, w_gate).reshape(B, T, -1)
        up = oct_ternary_linear(xp, w_up).reshape(B, T, -1)
        h = jax.nn.silu(gate) * up
        hp = h.reshape(B, T, 8, h.shape[-1] // 8)
        out = oct_ternary_linear(hp, w_down).reshape(B, T, D)
        return out
    x = L0_attn_hidden_states
    x = x + _layernorm(_L0_attn_ref(_layernorm(x, axis=-1), L0_attn_Wq, L0_attn_Wkv, L0_attn_Wo), axis=-1)
    x = x + _layernorm(_L0_ffn_ref(_layernorm(x, axis=-1), L0_ffn_q_scales, L0_ffn_q_vals, L0_ffn_bias), axis=-1)
    x = x + _layernorm(_L1_attn_ref(_layernorm(x, axis=-1), L1_attn_Wq, L1_attn_Wkr, L1_attn_Wdk, L1_attn_Wupk, L1_attn_Wupv, L1_attn_Wo), axis=-1)
    x = x + _layernorm(_L1_ffn_ref(_layernorm(x, axis=-1), L1_ffn_w_gate, L1_ffn_w_up, L1_ffn_w_down), axis=-1)
    return x

_drawn_inputs = setup_inputs


def setup_inputs(seed=0):
    import zlib

    import numpy as np

    out = dict(_drawn_inputs(seed))
    spreads = {}
    factors = {}
    for name, (base, spread) in spreads.items():
        noise = np.random.default_rng([zlib.crc32(name.encode()), seed]).standard_normal(out[name].shape)
        drawn = base * np.exp(spread * noise) if base else spread * noise
        out[name] = jnp.asarray(drawn.astype(out[name].dtype))
    for name, factor in factors.items():
        out[name] = (out[name] * factor).astype(out[name].dtype)
    return out
```

```python
from contextlib import ExitStack

import concourse.bass as bass
import numpy as np
from concourse import mybir

ALU = mybir.AluOpType
ACT = mybir.ActivationFunctionType
AX = mybir.AxisListType
F32 = mybir.dt.float32
F16 = mybir.dt.float16
I32 = mybir.dt.int32
RMAX = bass.bass_isa.ReduceOp.max
RADD = bass.bass_isa.ReduceOp.add

P = 128
B, S, D = 4, 512, 512
KT = D // P
TT = S // P
EPS = 1e-5
MASKED = -1e20
TINY = 1e-30

H0, E0 = 32, 16
PAIRS = H0 // 2
SLOPE0 = 2.0 ** (-(2.0 ** (-(np.log2(H0) - 3))))
SLOPES = [float(np.float32(SLOPE0 ** (i + 1))) for i in range(H0)]

H1, G1, E1 = 32, 8, 128
HG = H1 // G1
UP = 64 + E1
WK = E1 + E1

HID = 1360
HT = -(-HID // P)
OH, OD = HID // 8, D // 8

TRI = [P * t * (t + 1) // 2 for t in range(TT)]
TRIW = P * TT * (TT + 1) // 2
COL = [sum(TT - i for i in range(j)) for j in range(TT)]
NBLK = TT * (TT + 1) // 2


class Chain:

    def __init__(self, eng, sem):
        self.eng, self.sem, self.n = eng, sem, 0

    def tick(self, ins):
        ins.then_inc(self.sem, 1)
        self.n += 1

    def settle(self):
        self.eng.wait_ge(self.sem, self.n)


def clear(nc, sems):
    nums = sorted(s.num for s in sems)
    assert nums == list(range(nums[0], nums[-1] + 1))
    nc.all_engine_barrier(sems_to_clear=range(nums[0], nums[-1] + 1))


class Scope:

    def __init__(self, nc, stack):
        self.nc, self.stack, self.sems = nc, stack, []

    def sb(self, name, shape, dt=F32):
        return self.stack.enter_context(self.nc.sbuf_tensor(name, shape, dt))

    def ps(self, name, shape, dt=F32):
        return self.stack.enter_context(self.nc.psum_tensor(name, shape, dt))

    def sem(self, name):
        s = self.stack.enter_context(self.nc.semaphore(name))
        self.sems.append(s)
        return s


def split_matrices(nc, sc, tag, jobs, gm, rg):
    am = sc.sb(f"{tag}_am", [P, len(jobs)])
    s_ld = [sc.sem(f"{tag}_loaded{i}") for i in range(len(jobs))]
    s_dv = sc.sem(f"{tag}_dve_steps")
    s_am = sc.sem(f"{tag}_rowmax")
    s_gm = sc.sem(f"{tag}_globalmax")
    s_rg = sc.sem(f"{tag}_reciprocal")
    s_hi = sc.sem(f"{tag}_hi")
    s_lo = sc.sem(f"{tag}_lo")

    def flat(ap):
        return ap.rearrange("p a b -> p (a b)")

    with nc.Block() as block:

        @block.sync
        def _(sp):
            for i, job in enumerate(jobs):
                for dst, src in job[1]:
                    sp.dma_start(dst, src).then_inc(s_ld[i], 16)

        @block.gpsimd
        def _(pool):
            for i in range(len(jobs)):
                pool.wait_ge(s_am, i + 1)
                pool.partition_all_reduce(gm[:, i:i + 1], am[:, i:i + 1], P, RMAX).then_inc(s_gm, 1)

        @block.vector
        def _(dve):
            ch = Chain(dve, s_dv)
            for i, job in enumerate(jobs):
                raw = flat(job[2])
                dve.wait_ge(s_ld[i], 16 * len(job[1]))
                if len(job) > 5:
                    codes, scales = job[5]
                    ch.tick(dve.tensor_scalar(raw, flat(codes), -128.0, None, ALU.add))
                    ch.settle()
                    ch.tick(dve.tensor_tensor(raw, raw, flat(scales), ALU.mult))
                    ch.settle()
                dve.tensor_reduce(am[:, i:i + 1], raw, AX.X, ALU.max,
                                  apply_absolute_value=True).then_inc(s_am, 1)
            for i, job in enumerate(jobs):
                dve.wait_ge(s_gm, i + 1)
                ch.tick(dve.tensor_scalar(gm[:, i:i + 1], gm[:, i:i + 1], TINY, None, ALU.max))
                ch.settle()
                dve.reciprocal(rg[:, i:i + 1], gm[:, i:i + 1]).then_inc(s_rg, 1)
                dve.wait_ge(s_rg, i + 1)
                dve.wait_ge(s_hi, i + 1)
                dve.scalar_tensor_tensor(flat(job[4]), flat(job[2]), rg[:, i:i + 1], flat(job[3]),
                                         ALU.mult, ALU.subtract).then_inc(s_lo, 1)

        @block.scalar
        def _(act):
            for i, job in enumerate(jobs):
                act.wait_ge(s_rg, i + 1)
                act.activation(flat(job[3]), flat(job[2]), ACT.Copy,
                               scale=rg[:, i:i + 1]).then_inc(s_hi, 1)


def layer0(nc, A, W0, C, xT, x2_dram):
    with ExitStack() as stack:
        sc = Scope(nc, stack)
        xb = sc.sb("xb", [P, TT, D])
        yb = sc.sb("yb", [P, TT, D])
        aT = [sc.sb("aT_hi", [P, KT, S], F16), sc.sb("aT_lo", [P, KT, S], F16)]
        khi = sc.sb("khi", [P, S], F16)
        kst = sc.sb("kst", [P, S], F16)
        kab = sc.sb("kab", [P, 2, S], F16)
        v2 = sc.sb("v2", [P, TT, 2 * E0], F16)
        qT = [sc.sb("qT_hi", [P, KT, S], F16), sc.sb("qT_lo", [P, KT, S], F16)]
        stk = sc.sb("stk", [P, 2, S], F16)
        tab = sc.sb("tab", [P, 4, S])
        xp = sc.sb("xp", [P, 4, TRIW])
        pT = [sc.sb("pT_hi", [P, 3, NBLK, P], F16), sc.sb("pT_lo", [P, 3, NBLK, P], F16)]
        ob = sc.sb("ob", [P, TT, D])
        mx = sc.sb("mx", [P, 4, TT])
        nm = sc.sb("nm", [P, 4, TT])
        lsum = sc.sb("lsum", [P, H0, TT])
        rsum = sc.sb("rsum", [P, H0, TT])
        st = sc.sb("st", [P, TT, 6])
        mv = sc.sb("mv", [P, TT, 2])
        ve = sc.sb("ve", [P, TT])
        rs = sc.sb("rs", [P, TT])
        cs = sc.sb("cs", [P, 1])
        cinv = sc.sb("cinv", [P, 1])
        cy = sc.sb("cy", [P, 1])
        bank_s = [sc.ps(f"bank_s{i}", [P, S]) for i in range(3)]
        bank_t = [sc.ps(f"bank_t{i}", [P, S]) for i in range(3)]
        bank_v = [sc.ps(f"bank_v{i}", [P, S]) for i in range(2)]

        s_x = sc.sem("s_x_loaded")
        s_dv = sc.sem("s_dve_steps")
        s_cs = sc.sem("s_constants")
        s_ve = sc.sem("s_variance")
        s_rs = sc.sem("s_rstd")
        s_xn = sc.sem("s_normed_rows")
        s_tf = sc.sem("s_t_filled")
        s_th = sc.sem("s_t_hi_out")
        s_tl = sc.sem("s_t_lo_out")
        s_sf = sc.sem("s_s_filled")
        s_sh = sc.sem("s_s_hi_out")
        s_sd = sc.sem("s_s_freed_by_dve")
        s_sa = sc.sem("s_stack_ready")
        s_tab = sc.sem("s_table")
        s_nm = sc.sem("s_negmax")
        s_ex = sc.sem("s_exp")
        s_pf = sc.sem("s_pv_filled")
        s_pd = sc.sem("s_pv_out")
        s_on = sc.sem("s_heads_normed")
        s_out = sc.sem("s_x_stored")

        uses = ["K", "V"] + [("q", m) for m in range(KT)] + [("stack", 0)]
        for p in range(PAIRS):
            uses += [("stack", p + 1)] * (p + 1 < PAIRS) + [("s", p, i) for i in range(6)]
        uses += [("y", t) for t in range(TT)] + [("f", t) for t in range(TT)]
        number = {u: n for n, u in enumerate(uses)}
        emptied, by_dve, by_act = [], 0, 0
        for u in uses:
            if u[0] == "stack":
                by_act += 1
                emptied.append((s_sa, by_act))
            else:
                by_dve += 1
                emptied.append((s_sd, by_dve))

        def sbank(u):
            return bank_s[number[u] % 3]

        T_HEADS, T_OUT = TT, TT + TT * H0
        T_NORM2, T_NORM3 = T_OUT + TT, T_OUT + 2 * TT

        wq, wkv, wo, wf = W0["wq"], W0["wkv"], W0["wo"], W0["wf"]
        GQ, GKV, GO, GF = range(4)
        gm = W0["gm"]

        with nc.Fori(0, B) as b:
            with nc.Block() as block:

                @block.sync
                def _(sp):
                    sp.dma_start(xb[:, :, :], A["x"][b].rearrange("(t p) d -> p t d", p=P)).then_inc(s_x, 16)
                    sp.wait_ge(s_xn, 3 * TT)
                    sp.dma_start(x2_dram[b].rearrange("(t p) d -> p t d", p=P), xb[:, :, :]).then_inc(s_out, 16)
                    sp.wait_ge(s_out, 16)

                @block.gpsimd
                def _(pool):
                    def rstd(n):
                        pool.wait_ge(s_ve, n)
                        pool.tensor_tensor(rs[:, :], ve[:, :], C["mhalf"][:, 0:TT], ALU.pow).then_inc(s_rs, 1)

                    rstd(1)
                    pool.wait_ge(s_cs, 2)
                    for h in range(H0):
                        if h >= 4:
                            pool.wait_ge(s_nm, h - 3)
                        pool.tensor_scalar(tab[:, h % 4, :], C["rel"][:, :], 4.0 * SLOPES[h], cinv[:, 0:1],
                                           ALU.mult, ALU.mult).then_inc(s_tab, 1)
                    for n in range(2, 6):
                        rstd(n)

                @block.tensor
                def _(pe):
                    def take(u):
                        n = number[u]
                        if n >= 3:
                            pe.wait_ge(*emptied[n - 3])
                        return sbank(u)

                    def transpose4(n, rows):
                        if n >= 3:
                            pe.wait_ge(s_tl, n - 2)
                        for k in range(KT):
                            last = pe.transpose(bank_t[n % 3][:, k * P:(k + 1) * P],
                                                rows[:, k * P:(k + 1) * P], C["ident"][:, :])
                        last.then_inc(s_tf, 1)

                    def product(out, lhs, rhs, fill):
                        for k in range(KT):
                            for i, (a, c) in enumerate(((0, 0), (1, 0), (0, 1))):
                                last = pe.matmul(out, lhs(a, k), rhs(c, k), start=(k == 0 and i == 0),
                                                 stop=(k == KT - 1 and i == 2))
                        if fill:
                            last.then_inc(s_sf, 1)

                    for t in range(TT):
                        pe.wait_ge(s_xn, t + 1)
                        transpose4(t, yb[:, t, :])
                    pe.wait_ge(s_tl, TT)
                    product(take("K")[:, :], lambda a, k: wkv[a][:, k, 0:P], lambda c, k: aT[c][:, k, :], True)
                    bank = take("V")
                    for t in range(TT):
                        product(bank[:, t * E0:(t + 1) * E0], lambda a, k: aT[a][:, k, t * P:(t + 1) * P],
                                lambda c, k: wkv[c][:, k, P:P + E0], t == TT - 1)
                    for m in range(KT):
                        product(take(("q", m))[:, :], lambda a, k: wq[a][:, k, m * P:(m + 1) * P],
                                lambda c, k: aT[c][:, k, :], True)

                    def stack_queries(p):
                        m, r = p // 4, p % 4
                        bank = take(("stack", p))
                        pe.wait_ge(s_sd, 3 + m)
                        pe.matmul(bank[:, :], C["sel"][:, 2 * r, :], qT[0][:, m, :], start=True, stop=False)
                        pe.matmul(bank[:, :], C["sel"][:, 2 * r + 1, :], qT[1][:, m, :], start=False,
                                  stop=True).then_inc(s_sf, 1)

                    def scores(p):
                        pe.wait_ge(s_sa, p + 1)
                        q = stk[:, p % 2, :]
                        for i, (t, heads) in enumerate(((0, (0, 1)), (1, (0, 1)), (2, (0,)), (2, (1,)), (3, (0,)), (3, (1,)))):
                            bank, w = take(("s", p, i)), P * (t + 1)
                            pe.matmul(bank[:, 0:len(heads) * w].rearrange("p (h k) -> p h k", k=w),
                                      q[:, t * P:(t + 1) * P], kab[:, heads[0]:heads[-1] + 1, 0:w],
                                      start=True, stop=True).then_inc(s_sf, 1)

                    def transpose_probs(h):
                        pe.wait_ge(s_ex, h + 1)
                        for j in range(TT):
                            n = T_HEADS + TT * h + j
                            pe.wait_ge(s_tl, n - 2)
                            for t in range(j, TT):
                                last = pe.transpose(bank_t[n % 3][:, t * P:(t + 1) * P],
                                                    xp[:, h % 4, TRI[t] + j * P:TRI[t] + (j + 1) * P],
                                                    C["ident"][:, :])
                            last.then_inc(s_tf, 1)

                    def weigh_values(h):
                        pe.wait_ge(s_tl, T_HEADS + TT * (h + 1))
                        if h >= 2:
                            pe.wait_ge(s_pd, h - 1)
                        for t in range(TT):
                            for j in range(t + 1):
                                for a in range(2):
                                    last = pe.matmul(bank_v[h % 2][:, t * 2 * E0:(t + 1) * 2 * E0],
                                                     pT[a][:, h % 3, COL[j] + t - j, :], v2[:, j, :],
                                                     start=(j == 0 and a == 0), stop=(j == t and a == 1))
                        last.then_inc(s_pf, 1)

                    stack_queries(0)
                    for p in range(PAIRS + 2):
                        if p + 1 < PAIRS:
                            stack_queries(p + 1)
                        if p < PAIRS:
                            if p == 0:
                                pe.wait_ge(s_cs, 3)
                            scores(p)
                        if 1 <= p <= PAIRS:
                            transpose_probs(2 * p - 2)
                            if p > 1:
                                weigh_values(2 * p - 3)
                            transpose_probs(2 * p - 1)
                            weigh_values(2 * p - 2)
                        if p == PAIRS + 1:
                            weigh_values(H0 - 1)

                    for t in range(TT):
                        pe.wait_ge(s_on, t + 1)
                        transpose4(T_OUT + t, ob[:, t, :])
                    for t in range(TT):
                        pe.wait_ge(s_tl, T_OUT + t + 1)
                        product(take(("y", t))[:, :], lambda a, k: aT[a][:, k, t * P:(t + 1) * P],
                                lambda c, k: wo[c][:, k, :], True)
                    for t in range(TT):
                        pe.wait_ge(s_xn, TT + t + 1)
                        transpose4(T_NORM2 + t, yb[:, t, :])
                    for t in range(TT):
                        pe.wait_ge(s_tl, T_NORM2 + t + 1)
                        product(take(("f", t))[:, :], lambda a, k: aT[a][:, k, t * P:(t + 1) * P],
                                lambda c, k: wf[c][:, k, :], True)
                    for t in range(TT):
                        pe.wait_ge(s_xn, 2 * TT + t + 1)
                        transpose4(T_NORM3 + t, yb[:, t, :])

                @block.scalar
                def _(act):
                    def hi4(n, dst):
                        act.wait_ge(s_tf, n + 1)
                        act.activation(dst, bank_t[n % 3][:, :].rearrange("p (k c) -> p k c", c=P),
                                       ACT.Copy).then_inc(s_th, 1)

                    def hi_s(u, dst, src):
                        act.wait_ge(s_sf, number[u] + 1)
                        act.activation(dst, src, ACT.Copy).then_inc(s_sh, 1)

                    for t in range(TT):
                        hi4(t, aT[0][:, :, t * P:(t + 1) * P])
                    hi_s("K", khi[:, :], sbank("K")[:, :])
                    hi_s("V", v2[:, :, 0:E0], sbank("V")[:, 0:TT * E0].rearrange("p (t e) -> p t e", e=E0))
                    for m in range(KT):
                        hi_s(("q", m), qT[0][:, m, :], sbank(("q", m))[:, :])

                    def copy_stack(p):
                        u = ("stack", p)
                        if p >= 2:
                            act.wait_ge(s_sf, number[("s", p - 2, 5)] + 1)
                        act.wait_ge(s_sf, number[u] + 1)
                        act.activation(stk[:, p % 2, :], sbank(u)[:, :], ACT.Copy).then_inc(s_sa, 1)

                    def probs_hi(h):
                        for j in range(TT):
                            n = T_HEADS + TT * h + j
                            act.wait_ge(s_tf, n + 1)
                            if h >= 3:
                                act.wait_ge(s_pf, h - 2)
                            act.activation(pT[0][:, h % 3, COL[j]:COL[j] + TT - j, :],
                                           bank_t[n % 3][:, j * P:].rearrange("p (t c) -> p t c", c=P),
                                           ACT.Copy).then_inc(s_th, 1)

                    copy_stack(0)
                    for p in range(PAIRS + 1):
                        if p + 1 < PAIRS:
                            copy_stack(p + 1)
                        if p >= 1:
                            probs_hi(2 * p - 2)
                            probs_hi(2 * p - 1)
                        if p < PAIRS:
                            for h in (2 * p, 2 * p + 1):
                                act.wait_ge(s_nm, h + 1)
                                for t in range(TT):
                                    x = xp[:, h % 4, TRI[t]:TRI[t] + P * (t + 1)]
                                    last = act.activation(x, x, ACT.Exp, bias=nm[:, h % 4, t:t + 1],
                                                          accum_out=lsum[:, h, t:t + 1])
                                last.then_inc(s_ex, 1)
                    for t in range(TT):
                        hi4(T_OUT + t, aT[0][:, :, t * P:(t + 1) * P])
                    for t in range(TT):
                        hi4(T_NORM2 + t, aT[0][:, :, t * P:(t + 1) * P])
                    for t in range(TT):
                        hi4(T_NORM3 + t, xT[0][:, :, bass.ds(b * S + t * P, P)])

                @block.vector
                def _(dve):
                    ch = Chain(dve, s_dv)
                    count = {"rs": 0}

                    def statistics(src):
                        for t in range(TT):
                            ch.tick(dve.bn_stats(st[:, t, :], src[:, t, :]))
                        ch.settle()
                        for t in range(TT):
                            ch.tick(dve.bn_aggr(mv[:, t, :], st[:, t, :]))
                        ch.settle()
                        dve.tensor_scalar(ve[:, :], mv[:, :, 1], EPS, None, ALU.add).then_inc(s_ve, 1)
                        count["rs"] += 1
                        dve.wait_ge(s_rs, count["rs"])

                    def norm_rows():
                        statistics(xb)
                        for t in range(TT):
                            dve.tensor_scalar(yb[:, t, :], xb[:, t, :], mv[:, t, 0:1], rs[:, t:t + 1],
                                              ALU.subtract, ALU.mult).then_inc(s_xn, 1)

                    def add_normed():
                        ch.settle()
                        statistics(yb)
                        for t in range(TT):
                            ch.tick(dve.tensor_scalar(yb[:, t, :], yb[:, t, :], mv[:, t, 0:1], rs[:, t:t + 1],
                                                      ALU.subtract, ALU.mult))
                        ch.settle()
                        for t in range(TT):
                            ch.tick(dve.tensor_tensor(xb[:, t, :], xb[:, t, :], yb[:, t, :], ALU.add))
                        ch.settle()

                    def lo4(n, hi, lo):
                        dve.wait_ge(s_th, n + 1)
                        dve.tensor_tensor(lo, bank_t[n % 3][:, :].rearrange("p (k c) -> p k c", c=P), hi,
                                          ALU.subtract).then_inc(s_tl, 1)

                    ch.tick(dve.tensor_scalar(cs[:, :], gm[:, GQ:GQ + 1], gm[:, GKV:GKV + 1], E0 ** -0.5,
                                              ALU.mult, ALU.mult))
                    dve.tensor_scalar(cy[:, :], gm[:, GKV:GKV + 1], gm[:, GO:GO + 1], None,
                                      ALU.mult).then_inc(s_cs, 1)
                    ch.settle()
                    ch.tick(dve.tensor_scalar(cinv[:, :], cs[:, :], 4.0, None, ALU.mult))
                    ch.settle()
                    dve.reciprocal(cinv[:, :], cinv[:, :]).then_inc(s_cs, 1)

                    dve.wait_ge(s_x, 16)
                    norm_rows()
                    for t in range(TT):
                        lo4(t, aT[0][:, :, t * P:(t + 1) * P], aT[1][:, :, t * P:(t + 1) * P])

                    dve.wait_ge(s_sh, 1)
                    dve.tensor_tensor(kst[64:128, :], sbank("K")[64:128, :], khi[64:128, :],
                                      ALU.subtract).then_inc(s_sd, 1)
                    ch.tick(dve.tensor_copy(kst[0:64, :], khi[0:64, :]))
                    dve.wait_ge(s_sh, 2)
                    dve.tensor_tensor(v2[:, :, E0:2 * E0],
                                      sbank("V")[:, 0:TT * E0].rearrange("p (t e) -> p t e", e=E0),
                                      v2[:, :, 0:E0], ALU.subtract).then_inc(s_sd, 1)
                    ch.settle()
                    dve.wait_ge(s_sd, 2)
                    ch.tick(dve.tensor_scalar(kab[:, 0, :], kst[:, :], C["pairmask"][:, 0:1], None, ALU.mult))
                    ch.tick(dve.tensor_scalar(kab[:, 1, :], kst[:, :], C["pairmask"][:, 1:2], None, ALU.mult))
                    ch.settle()
                    dve.memset(ve[:, 0:1], 1.0).then_inc(s_cs, 1)
                    for m in range(KT):
                        dve.wait_ge(s_sh, 3 + m)
                        dve.tensor_tensor(qT[1][:, m, :], sbank(("q", m))[:, :], qT[0][:, m, :],
                                          ALU.subtract).then_inc(s_sd, 1)

                    def biased_scores(p):
                        if p >= 2:
                            dve.wait_ge(s_tf, T_HEADS + TT * (2 * p - 2))
                        dve.wait_ge(s_tab, 2 * p + 2)
                        for i, (t, heads) in enumerate(((0, (0, 1)), (1, (0, 1)), (2, (0,)), (2, (1,)), (3, (0,)), (3, (1,)))):
                            u, w = ("s", p, i), P * (t + 1)
                            dve.wait_ge(s_sf, number[u] + 1)
                            for k, e in enumerate(heads):
                                h = 2 * p + e
                                last = dve.tensor_tensor_reduce(
                                    out=xp[:, h % 4, TRI[t]:TRI[t] + w], in0=sbank(u)[:, k * w:(k + 1) * w],
                                    in1=tab[:, h % 4, S - w:S], scale=cs[:, 0:1], scalar=-3e38,
                                    op0=ALU.add, op1=ALU.max, accum_out=mx[:, h % 4, t:t + 1])
                            last.then_inc(s_sd, 1)
                        dve.wait_ge(s_sd, emptied[number[("s", p, 5)]][1])
                        for h in (2 * p, 2 * p + 1):
                            dve.tensor_scalar(nm[:, h % 4, :], mx[:, h % 4, :], -1.0, None,
                                              ALU.mult).then_inc(s_nm, 1)

                    def probs_lo(h):
                        for j in range(TT):
                            n = T_HEADS + TT * h + j
                            dve.wait_ge(s_th, n + 1)
                            c = slice(COL[j], COL[j] + TT - j)
                            dve.tensor_tensor(pT[1][:, h % 3, c, :],
                                              bank_t[n % 3][:, j * P:].rearrange("p (t c) -> p t c", c=P),
                                              pT[0][:, h % 3, c, :], ALU.subtract).then_inc(s_tl, 1)

                    def head_out(h):
                        dve.wait_ge(s_pf, h + 1)
                        dve.tensor_reduce(ob[:, :, h * E0:(h + 1) * E0],
                                          bank_v[h % 2][:, 0:TT * 2 * E0].rearrange(
                                              "p (t c e) -> p t e c", c=2, e=E0),
                                          AX.X, ALU.add).then_inc(s_pd, 1)

                    for p in range(PAIRS + 2):
                        if p < PAIRS:
                            biased_scores(p)
                        if 1 <= p <= PAIRS:
                            probs_lo(2 * p - 2)
                            if p > 1:
                                head_out(2 * p - 3)
                            probs_lo(2 * p - 1)
                            head_out(2 * p - 2)
                        if p == PAIRS + 1:
                            head_out(H0 - 1)

                    ch.tick(dve.reciprocal(rsum[:, :, :], lsum[:, :, :]))
                    ch.settle()
                    dve.wait_ge(s_pd, H0)
                    for t in range(TT):
                        o = ob[:, t, :].rearrange("p (h e) -> p h e", e=E0)
                        dve.tensor_tensor(o, o, rsum[:, :, t:t + 1].to_broadcast([P, H0, E0]),
                                          ALU.mult).then_inc(s_on, 1)
                    for t in range(TT):
                        lo4(T_OUT + t, aT[0][:, :, t * P:(t + 1) * P], aT[1][:, :, t * P:(t + 1) * P])
                    for t in range(TT):
                        dve.wait_ge(s_sf, number[("y", t)] + 1)
                        dve.tensor_scalar(yb[:, t, :], sbank(("y", t))[:, :], cy[:, 0:1], None,
                                          ALU.mult).then_inc(s_sd, 1)
                    dve.wait_ge(s_sd, emptied[number[("y", TT - 1)]][1])
                    add_normed()
                    norm_rows()
                    for t in range(TT):
                        lo4(T_NORM2 + t, aT[0][:, :, t * P:(t + 1) * P], aT[1][:, :, t * P:(t + 1) * P])
                    for t in range(TT):
                        dve.wait_ge(s_sf, number[("f", t)] + 1)
                        dve.scalar_tensor_tensor(yb[:, t, :], sbank(("f", t))[:, :], gm[:, GF:GF + 1],
                                                 C["bias"][:, :], ALU.mult, ALU.add).then_inc(s_sd, 1)
                    dve.wait_ge(s_sd, emptied[number[("f", TT - 1)]][1])
                    add_normed()
                    norm_rows()
                    for t in range(TT):
                        c = bass.ds(b * S + t * P, P)
                        lo4(T_NORM3 + t, xT[0][:, :, c], xT[1][:, :, c])

            clear(nc, sc.sems)


def fuse_up_projections(nc, A, C, fused_dram, g1):
    with ExitStack() as stack:
        sc = Scope(nc, stack)
        NU = G1 * UP
        raw_d = sc.sb("raw_d", [P, KT, D])
        raw_u = sc.sb("raw_u", [P, KT, NU])
        wd = [sc.sb("wdk_hi", [P, KT, D], F16), sc.sb("wdk_lo", [P, KT, D], F16)]
        wu = [sc.sb("wup_hi", [P, KT, NU], F16), sc.sb("wup_lo", [P, KT, NU], F16)]
        fused = sc.sb("fused", [P, KT, NU])
        gm = sc.sb("fu_gm", [P, 2])
        rg = sc.sb("fu_rg", [P, 2])
        c = sc.sb("fu_c", [P, 1])
        bank = [sc.ps(f"fu_bank{i}", [P, S]) for i in range(4)]
        jobs = [("wdk", [(raw_d[:, :, :], A["wdk1"].rearrange("(k p) n -> p k n", p=P))],
                 raw_d[:, :, :], wd[0][:, :, :], wd[1][:, :, :]),
                ("wup", [(raw_u[:, :, :], A["wup1"].rearrange("(k p) n -> p k n", p=P))],
                 raw_u[:, :, :], wu[0][:, :, :], wu[1][:, :, :])]
        split_matrices(nc, sc, "fu", jobs, gm, rg)
        s_f = sc.sem("s_fu_filled")
        s_e = sc.sem("s_fu_out")
        s_c = sc.sem("s_fu_factor")
        s_o = sc.sem("s_fu_stored")
        tiles = [(m, n) for m in range(KT) for n in range(NU // S)]
        with nc.Block() as block:

            @block.tensor
            def _(pe):
                for i, (m, n) in enumerate(tiles):
                    if i >= 4:
                        pe.wait_ge(s_e, i - 3)
                    for k in range(KT):
                        for q, (a, r) in enumerate(((0, 0), (1, 0), (0, 1))):
                            last = pe.matmul(bank[i % 4][:, :], wd[a][:, k, m * P:(m + 1) * P],
                                             wu[r][:, k, n * S:(n + 1) * S],
                                             start=(k == 0 and q == 0), stop=(k == KT - 1 and q == 2))
                    last.then_inc(s_f, 1)

            @block.vector
            def _(dve):
                dve.tensor_tensor(c[:, :], gm[:, 0:1], gm[:, 1:2], ALU.mult).then_inc(s_c, 1)

            @block.scalar
            def _(act):
                act.wait_ge(s_c, 1)
                for i, (m, n) in enumerate(tiles):
                    act.wait_ge(s_f, i + 1)
                    act.activation(fused[:, m, n * S:(n + 1) * S], bank[i % 4][:, :], ACT.Copy,
                                   scale=c[:, 0:1]).then_inc(s_e, 1)

            @block.sync
            def _(sp):
                for m in range(KT):
                    sp.wait_ge(s_e, (m + 1) * NU // S)
                    sp.dma_start(fused_dram[m * P:(m + 1) * P, :], fused[:, m, :]).then_inc(s_o, 16)
                sp.wait_ge(s_o, 16 * KT)

        clear(nc, sc.sems)


def attention1(nc, A, C, xT, yacc, fused_dram):
    with ExitStack() as stack:
        sc = Scope(nc, stack)
        NH = B * HG
        raw_kv = sc.sb("raw_kv", [P, KT, WK])
        raw_q = sc.sb("raw_q", [P, KT, D])
        raw_o = sc.sb("raw_o", [P, HG, D])
        wkv = [sc.sb("wkv1_hi", [P, KT, WK], F16), sc.sb("wkv1_lo", [P, KT, WK], F16)]
        wq = [sc.sb("wq1_hi", [P, KT, D], F16), sc.sb("wq1_lo", [P, KT, D], F16)]
        wo = [sc.sb("wo1_hi", [P, HG, D], F16), sc.sb("wo1_lo", [P, HG, D], F16)]
        am = sc.sb("am1", [P, 3])
        gm = sc.sb("gm1", [P, 3])
        rg = sc.sb("rg1", [P, 3])
        cs = sc.sb("cs1", [P, 1])
        cy = sc.sb("cy1", [P, 1])
        rope = {n: sc.sb(n, [P, S]) for n in ("cosq", "sinq", "cosk", "sink")}
        mask = sc.sb("mask", [P, S])
        t1 = sc.sb("t1", [P, 2, S])
        t2 = sc.sb("t2", [P, 2, S])
        qf = sc.sb("qf", [P, 2, S])
        kT = [sc.sb("kT_hi", [P, S], F16), sc.sb("kT_lo", [P, S], F16)]
        v = [sc.sb("v_hi", [P, 2, TT, E1], F16), sc.sb("v_lo", [P, 2, TT, E1], F16)]
        qT = [sc.sb("q1T_hi", [P, 2, S], F16), sc.sb("q1T_lo", [P, 2, S], F16)]
        xp = sc.sb("xp1", [P, 3, TRIW])
        pT = [sc.sb("p1T_hi", [P, NBLK, HG, P], F16), sc.sb("p1T_lo", [P, NBLK, HG, P], F16)]
        oT = [sc.sb("o1T_hi", [P, TT, HG, P], F16), sc.sb("o1T_lo", [P, TT, HG, P], F16)]
        mx = sc.sb("mx1", [P, 3, TT])
        nm = sc.sb("nm1", [P, 3, TT])
        ls = sc.sb("ls1", [P, 3, TT])
        rl = sc.sb("rl1", [P, 3, TT])
        bank_r = [sc.ps(f"bank_r{i}", [P, S]) for i in range(2)]
        bank_s = [sc.ps(f"bank1_s{i}", [P, S]) for i in range(2)]
        bank_t = [sc.ps(f"bank1_t{i}", [P, S]) for i in range(2)]
        bank_o = [sc.ps(f"bank_o{i}", [P, S]) for i in range(2)]
        GKV, GQ, GO = range(3)

        def load_kv(g):
            f = fused_dram.rearrange("(k p) (g n) -> g p k n", p=P, n=UP)[g]
            r = A["wkr1"][g]
            return [(raw_kv[:, :, 0:32], r[:, :, 0:32]), (raw_kv[:, :, 64:96], r[:, :, 32:64]),
                    (raw_kv[:, :, 32:64], f[:, :, 0:32]), (raw_kv[:, :, 96:128], f[:, :, 32:64]),
                    (raw_kv[:, :, E1:WK], f[:, :, 64:UP])]

        s_c = sc.sem("s1_tables")
        with nc.Block() as block:

            @block.sync
            def _(sp):
                for n in rope:
                    sp.dma_start(rope[n][:, :], A[n]).then_inc(s_c, 16)
                sp.dma_start(mask[:, :], A["mask"]).then_inc(s_c, 16)
                for n in load_kv(0):
                    sp.dma_start(*n).then_inc(s_c, 16)
                sp.dma_start(raw_q[:, :, :], A["wq1"][0]).then_inc(s_c, 16)
                sp.dma_start(raw_o[:, :, :], A["wo1"][0]).then_inc(s_c, 16)
                sp.wait_ge(s_c, 16 * 12)

            @block.gpsimd
            def _(pool):
                pool.memset(yacc[:, :, :], 0.0)

        s_dv = sc.sem("s1_dve_steps")
        s_am = sc.sem("s1_rowmax")
        s_gm = sc.sem("s1_globalmax")
        s_rg = sc.sem("s1_reciprocal")
        s_wh = sc.sem("s1_weights_hi")
        s_wl = sc.sem("s1_weights_lo")
        s_ld = sc.sem("s1_next_weights")
        s_rf = sc.sem("s1_r_filled")
        s_rh = sc.sem("s1_v_hi_out")
        s_rd = sc.sem("s1_r_freed")
        s_qf = sc.sem("s1_roped")
        s_qh = sc.sem("s1_roped_hi")
        s_ql = sc.sem("s1_roped_lo")
        s_sf = sc.sem("s1_s_filled")
        s_sd = sc.sem("s1_s_freed")
        s_nm = sc.sem("s1_negmax")
        s_ex = sc.sem("s1_exp")
        s_pn = sc.sem("s1_probs_normed")
        s_tf = sc.sem("s1_t_filled")
        s_th = sc.sem("s1_t_hi_out")
        s_tl = sc.sem("s1_t_lo_out")
        s_of = sc.sem("s1_o_filled")
        s_oh = sc.sem("s1_o_hi_out")
        s_od = sc.sem("s1_o_freed")

        r_uses = []
        for n in range(NH):
            if n % HG == 0:
                r_uses += [("k", n // HG), ("v", n // HG)]
            r_uses.append(("q", n))
        r_no = {u: i for i, u in enumerate(r_uses)}
        ropes = [u for u in r_uses if u[0] != "v"]
        rope_no = {u: i for i, u in enumerate(ropes)}
        STEPS = NH + 4

        def pv_batch(n):
            b = (n - 6) // HG
            return b if n >= 6 and (n - 6) % HG == 0 and b < B else None

        def projections(n):
            out = []
            for b in range(B):
                k = n - (HG * b + 7)
                out += {0: [(b, 0), (b, 1)], 1: [(b, 2)], 2: [(b, 3)]}.get(k, [])
            return out

        o_uses = []
        for n in range(STEPS + 2):
            if pv_batch(n) is not None:
                o_uses += [("pv", pv_batch(n), t) for t in range(TT)]
            o_uses += [("wo", b, t) for b, t in projections(n)]
        o_no = {u: i for i, u in enumerate(o_uses)}
        assert len(o_uses) == 2 * B * TT
        STEPS = STEPS + 2

        def flat(ap):
            return ap.rearrange("p a b -> p (a b)")

        raws = [raw_kv, raw_q, raw_o]
        his, los = [wkv[0], wq[0], wo[0]], [wkv[1], wq[1], wo[1]]

        with nc.Fori(0, G1) as g:
            with nc.Block() as block:

                @block.sync
                def _(sp):
                    nxt = (g + 1) % G1
                    sp.wait_ge(s_wl, 1)
                    for n in load_kv(nxt):
                        sp.dma_start(*n).then_inc(s_ld, 16)
                    sp.wait_ge(s_wl, 2)
                    sp.dma_start(raw_q[:, :, :], A["wq1"][nxt]).then_inc(s_ld, 16)
                    sp.wait_ge(s_wl, 3)
                    sp.dma_start(raw_o[:, :, :], A["wo1"][nxt]).then_inc(s_ld, 16)
                    sp.wait_ge(s_ld, 16 * 7)

                @block.gpsimd
                def _(pool):
                    for i in range(3):
                        pool.wait_ge(s_am, i + 1)
                        pool.partition_all_reduce(gm[:, i:i + 1], am[:, i:i + 1], P, RMAX).then_inc(s_gm, 1)
                    for i, u in enumerate(ropes):
                        pool.wait_ge(s_rd, r_no[u] + 1)
                        if i >= 2:
                            pool.wait_ge(s_ql, i - 1)
                        pool.tensor_tensor(qf[:, i % 2, :], t1[:, i % 2, :], t2[:, i % 2, :],
                                           ALU.add).then_inc(s_qf, 1)

                @block.tensor
                def _(pe):
                    def triple(out, lhs, rhs, first, last):
                        for i, (a, c) in enumerate(((0, 0), (1, 0), (0, 1))):
                            ins = pe.matmul(out, lhs(a), rhs(c), start=(first and i == 0),
                                            stop=(last and i == 2))
                        return ins

                    def take_r(u):
                        i = r_no[u]
                        if i >= 2:
                            pe.wait_ge(s_rd, i - 1)
                        return bank_r[i % 2]

                    def project(u, w, col, b):
                        bank = take_r(u)
                        for k in range(KT):
                            ins = triple(bank[:, :], lambda a: w[a][:, k, col:col + P],
                                         lambda c: xT[c][:, k, b * S:(b + 1) * S], k == 0, k == KT - 1)
                        ins.then_inc(s_rf, 1)

                    def values(b):
                        bank = take_r(("v", b))
                        for t in range(TT):
                            for k in range(KT):
                                ins = triple(bank[:, t * P:(t + 1) * P],
                                             lambda a: xT[a][:, k, b * S + t * P:b * S + (t + 1) * P],
                                             lambda c: wkv[c][:, k, E1:WK], k == 0, k == KT - 1)
                        ins.then_inc(s_rf, 1)

                    def scores(n):
                        pe.wait_ge(s_ql, rope_no[("q", n)] + 1)
                        for i, tiles in enumerate(((0, 1), (2,), (3,))):
                            u = 3 * n + i
                            if u >= 2:
                                pe.wait_ge(s_sd, u - 1)
                            col = 0
                            for t in tiles:
                                w = P * (t + 1)
                                ins = triple(bank_s[u % 2][:, col:col + w],
                                             lambda a: qT[a][:, n % 2, t * P:(t + 1) * P],
                                             lambda c: kT[c][:, 0:w], True, True)
                                col += w
                            ins.then_inc(s_sf, 1)

                    def transpose_probs(n):
                        pe.wait_ge(s_pn, n + 1)
                        for j in range(TT):
                            u = TT * n + j
                            if u >= 2:
                                pe.wait_ge(s_tl, u - 1)
                            for t in range(j, TT):
                                ins = pe.transpose(bank_t[u % 2][:, t * P:(t + 1) * P],
                                                   xp[:, n % 3, TRI[t] + j * P:TRI[t] + (j + 1) * P],
                                                   C["ident"][:, :])
                            ins.then_inc(s_tf, 1)

                    def take_o(u):
                        i = o_no[u]
                        if i >= 2:
                            pe.wait_ge(s_od, i - 1)
                        return bank_o[i % 2]

                    def weigh_values(b):
                        pe.wait_ge(s_tl, TT * HG * (b + 1))
                        for t in range(TT):
                            bank = take_o(("pv", b, t))
                            for j in range(t + 1):
                                ins = triple(bank[:, :], lambda a: v[a][:, b % 2, j, :],
                                             lambda c: flat(pT[c][:, COL[j] + t - j, :, :]), j == 0, j == t)
                            ins.then_inc(s_of, 1)

                    def project_out(b, t):
                        pe.wait_ge(s_od, o_no[("pv", b, t)] + 1)
                        pe.wait_ge(s_wl, 3)
                        bank = take_o(("wo", b, t))
                        for h in range(HG):
                            ins = triple(bank[:, :], lambda a: oT[a][:, t, h, :],
                                         lambda c: wo[c][:, h, :], h == 0, h == HG - 1)
                        ins.then_inc(s_of, 1)

                    for n in range(STEPS):
                        if n < NH:
                            b = n // HG
                            if n % HG == 0:
                                pe.wait_ge(s_wl, 1)
                                project(("k", b), wkv, 0, b)
                                values(b)
                                pe.wait_ge(s_wl, 2)
                            project(("q", n), wq, (n % HG) * P, b)
                        if 1 <= n <= NH:
                            scores(n - 1)
                        if pv_batch(n) is not None:
                            weigh_values(pv_batch(n))
                        if 2 <= n <= NH + 1:
                            transpose_probs(n - 2)
                        for b, t in projections(n):
                            project_out(b, t)

                @block.scalar
                def _(act):
                    for i in range(3):
                        act.wait_ge(s_rg, i + 1)
                        act.activation(flat(his[i][:, :, :]), flat(raws[i][:, :, :]), ACT.Copy,
                                       scale=rg[:, i:i + 1]).then_inc(s_wh, 1)

                    def roped_hi(u):
                        i = rope_no[u]
                        act.wait_ge(s_qf, i + 1)
                        if u[0] == "k":
                            if u[1] >= 1:
                                act.wait_ge(s_sf, 3 * HG * u[1])
                            dst = kT[0][:, :]
                        else:
                            if u[1] >= 2:
                                act.wait_ge(s_sf, 3 * (u[1] - 1))
                            dst = qT[0][:, u[1] % 2, :]
                        act.activation(dst, qf[:, i % 2, :], ACT.Copy).then_inc(s_qh, 1)

                    for n in range(STEPS):
                        if n < NH:
                            b = n // HG
                            if n % HG == 0:
                                act.wait_ge(s_rf, r_no[("v", b)] + 1)
                                if b >= 2:
                                    act.wait_ge(s_of, o_no[("pv", b - 2, TT - 1)] + 1)
                                act.activation(flat(v[0][:, b % 2, :, :]), bank_r[r_no[("v", b)] % 2][:, :],
                                               ACT.Copy).then_inc(s_rh, 1)
                        if 1 <= n <= NH:
                            m = n - 1
                            act.wait_ge(s_nm, m + 1)
                            for t in range(TT):
                                x = xp[:, m % 3, TRI[t]:TRI[t] + P * (t + 1)]
                                ins = act.activation(x, x, ACT.Exp, bias=nm[:, m % 3, t:t + 1],
                                                     accum_out=ls[:, m % 3, t:t + 1])
                            ins.then_inc(s_ex, 1)
                        if n < NH:
                            if n % HG == 0:
                                roped_hi(("k", n // HG))
                            roped_hi(("q", n))
                        if pv_batch(n) is not None:
                            for t in range(TT):
                                u = o_no[("pv", pv_batch(n), t)]
                                act.wait_ge(s_of, u + 1)
                                act.activation(oT[0][:, t, :, :].rearrange("p h c -> p (h c)"),
                                               bank_o[u % 2][:, :], ACT.Copy).then_inc(s_oh, 1)
                        if 2 <= n <= NH + 1:
                            m = n - 2
                            for j in range(TT):
                                u = TT * m + j
                                act.wait_ge(s_tf, u + 1)
                                act.activation(pT[0][:, COL[j]:COL[j] + TT - j, m % HG, :],
                                               bank_t[u % 2][:, j * P:].rearrange("p (t c) -> p t c", c=P),
                                               ACT.Copy).then_inc(s_th, 1)

                @block.vector
                def _(dve):
                    ch = Chain(dve, s_dv)

                    def row_max(i):
                        dve.tensor_reduce(am[:, i:i + 1], flat(raws[i][:, :, :]), AX.X, ALU.max,
                                          apply_absolute_value=True).then_inc(s_am, 1)

                    def weights_lo(i):
                        dve.wait_ge(s_wh, i + 1)
                        dve.scalar_tensor_tensor(flat(los[i][:, :, :]), flat(raws[i][:, :, :]), rg[:, i:i + 1],
                                                 flat(his[i][:, :, :]), ALU.mult,
                                                 ALU.subtract).then_inc(s_wl, 1)

                    def reciprocal(i):
                        dve.wait_ge(s_gm, i + 1)
                        ch.tick(dve.tensor_scalar(gm[:, i:i + 1], gm[:, i:i + 1], TINY, None, ALU.max))
                        ch.settle()
                        dve.reciprocal(rg[:, i:i + 1], gm[:, i:i + 1]).then_inc(s_rg, 1)
                        dve.wait_ge(s_rg, i + 1)

                    row_max(0)
                    row_max(1)
                    reciprocal(0)
                    reciprocal(1)
                    row_max(2)
                    weights_lo(0)
                    weights_lo(1)
                    reciprocal(2)
                    weights_lo(2)
                    ch.tick(dve.tensor_scalar(cs[:, :], gm[:, GQ:GQ + 1], gm[:, GKV:GKV + 1], E1 ** -0.5,
                                              ALU.mult, ALU.mult))
                    ch.tick(dve.tensor_scalar(cy[:, :], gm[:, GKV:GKV + 1], gm[:, GO:GO + 1], None, ALU.mult))
                    ch.settle()

                    def rotate(u):
                        i = rope_no[u]
                        cos, sin = (rope["cosk"], rope["sink"]) if u[0] == "k" else (rope["cosq"], rope["sinq"])
                        bank = bank_r[r_no[u] % 2]
                        dve.wait_ge(s_rf, r_no[u] + 1)
                        if i >= 2:
                            dve.wait_ge(s_qf, i - 1)
                        dve.tensor_tensor(t1[0:64, i % 2, :], bank[64:128, :], sin[0:64, :], ALU.mult)
                        dve.tensor_tensor(t1[64:128, i % 2, :], bank[0:64, :], sin[64:128, :], ALU.mult)
                        dve.tensor_tensor(t2[:, i % 2, :], bank[:, :], cos[:, :], ALU.mult).then_inc(s_rd, 1)

                    def roped_lo(u):
                        i = rope_no[u]
                        hi, lo = (x[:, :] for x in kT) if u[0] == "k" else (x[:, u[1] % 2, :] for x in qT)
                        dve.wait_ge(s_qh, i + 1)
                        dve.tensor_tensor(lo, qf[:, i % 2, :], hi, ALU.subtract).then_inc(s_ql, 1)

                    for n in range(STEPS):
                        if 2 <= n <= NH + 1:
                            m = n - 2
                            dve.wait_ge(s_ex, m + 1)
                            ch.tick(dve.reciprocal(rl[:, m % 3, :], ls[:, m % 3, :]))
                            ch.settle()
                            for t in range(TT):
                                x = xp[:, m % 3, TRI[t]:TRI[t] + P * (t + 1)]
                                ins = dve.tensor_scalar(x, x, rl[:, m % 3, t:t + 1], None, ALU.mult)
                            ins.then_inc(s_pn, 1)
                        if n < NH:
                            b = n // HG
                            if n % HG == 0:
                                rotate(("k", b))
                                dve.wait_ge(s_rh, b + 1)
                                dve.tensor_tensor(flat(v[1][:, b % 2, :, :]), bank_r[r_no[("v", b)] % 2][:, :],
                                                  flat(v[0][:, b % 2, :, :]), ALU.subtract).then_inc(s_rd, 1)
                            rotate(("q", n))
                        if 1 <= n <= NH:
                            m = n - 1
                            if m >= 3:
                                dve.wait_ge(s_tf, TT * (m - 2))
                            for i, tiles in enumerate(((0, 1), (2,), (3,))):
                                u, col = 3 * m + i, 0
                                dve.wait_ge(s_sf, u + 1)
                                for t in tiles:
                                    w = P * (t + 1)
                                    ins = dve.tensor_tensor_reduce(
                                        out=xp[:, m % 3, TRI[t]:TRI[t] + w], in0=bank_s[u % 2][:, col:col + w],
                                        in1=mask[:, S - w:S], scale=cs[:, 0:1], scalar=-3e38,
                                        op0=ALU.add, op1=ALU.max, accum_out=mx[:, m % 3, t:t + 1])
                                    col += w
                                ins.then_inc(s_sd, 1)
                            dve.wait_ge(s_sd, 3 * (m + 1))
                            dve.tensor_scalar(nm[:, m % 3, :], mx[:, m % 3, :], -1.0, None,
                                              ALU.mult).then_inc(s_nm, 1)
                        if n < NH:
                            if n % HG == 0:
                                roped_lo(("k", n // HG))
                            roped_lo(("q", n))
                        if pv_batch(n) is not None:
                            for t in range(TT):
                                u = o_no[("pv", pv_batch(n), t)]
                                dve.wait_ge(s_oh, TT * pv_batch(n) + t + 1)
                                dve.tensor_tensor(oT[1][:, t, :, :].rearrange("p h c -> p (h c)"),
                                                  bank_o[u % 2][:, :],
                                                  oT[0][:, t, :, :].rearrange("p h c -> p (h c)"),
                                                  ALU.subtract).then_inc(s_od, 1)
                        if 2 <= n <= NH + 1:
                            m = n - 2
                            for j in range(TT):
                                u = TT * m + j
                                c = slice(COL[j], COL[j] + TT - j)
                                dve.wait_ge(s_th, u + 1)
                                dve.tensor_tensor(pT[1][:, c, m % HG, :],
                                                  bank_t[u % 2][:, j * P:].rearrange("p (t c) -> p t c", c=P),
                                                  pT[0][:, c, m % HG, :], ALU.subtract).then_inc(s_tl, 1)
                        for b, t in projections(n):
                            u = o_no[("wo", b, t)]
                            dve.wait_ge(s_of, u + 1)
                            y = yacc[:, TT * b + t, :]
                            dve.scalar_tensor_tensor(y, bank_o[u % 2][:, :], cy[:, 0:1], y, ALU.mult,
                                                     ALU.add).then_inc(s_od, 1)

            clear(nc, sc.sems)


def feed_forward1(nc, A, C, yacc, x2_dram, out):
    with ExitStack() as stack:
        sc = Scope(nc, stack)
        tg = sc.sb("tern_gate", [P, KT, HID], F16)
        tu = sc.sb("tern_up", [P, KT, HID], F16)
        td = sc.sb("tern_down", [P, HT, D], F16)
        scale = sc.sb("tern_scale", [P, 3])
        kup = sc.sb("kup", [P, 1])
        cdn = sc.sb("cdn", [P, 1])
        GATE, UPW, DOWN = range(3)

        with ExitStack() as inner:
            si = Scope(nc, inner)
            raws = [si.sb("raw_gate", [P, KT, HID]), si.sb("raw_up", [P, KT, HID]),
                    si.sb("raw_down", [P, HT, D])]
            pos = si.sb("pos", [P, HT * D], F16)
            sgn = [si.sb("sgn_in", [P, KT, 8], F16), si.sb("sgn_dn", [P, HT, 8], F16)]
            part = si.sb("part", [P, HT * 8])
            am = si.sb("am2", [P, 3])
            half = si.sb("half", [P, 3])
            nhalf = si.sb("nhalf", [P, 3])
            s_zero = si.sem("s_tail_zeroed")
            s_ld = [si.sem(f"s_tern_loaded{i}") for i in range(3)]
            s_am = si.sem("s_abs_sums")
            s_gm = si.sem("s_total_sums")
            s_dv = si.sem("s_tern_steps")
            tern = [tg, tu, td]
            with nc.Block() as block:

                @block.sync
                def _(sp):
                    for i, n in ((0, "w_gate"), (1, "w_up")):
                        sp.dma_start(raws[i][:, :, :], A[n].rearrange("(k p) n -> p k n", p=P)).then_inc(s_ld[i], 16)
                    full = (HT - 1) * P
                    sp.dma_start(raws[2][:, 0:HT - 1, :],
                                 A["w_down"][0:full, :].rearrange("(k p) n -> p k n", p=P)).then_inc(s_ld[2], 16)
                    sp.dma_start(sgn[0][:, :, :], A["sgn_in"]).then_inc(s_ld[0], 16)
                    sp.dma_start(sgn[1][:, :, :], A["sgn_dn"]).then_inc(s_ld[2], 16)
                    sp.wait_ge(s_zero, 1)
                    sp.dma_start(raws[2][0:HID - full, HT - 1, :], A["w_down"][full:HID, :]).then_inc(s_ld[2], 16)

                @block.gpsimd
                def _(pool):
                    pool.memset(raws[2][:, HT - 1, :], 0.0).then_inc(s_zero, 1)
                    for i in range(3):
                        pool.wait_ge(s_am, i + 1)
                        pool.partition_all_reduce(scale[:, i:i + 1], am[:, i:i + 1], P, RADD).then_inc(s_gm, 1)

                @block.vector
                def _(dve):
                    ch = Chain(dve, s_dv)
                    for i, n in enumerate((KT, KT, HT)):
                        dve.wait_ge(s_ld[i], (32, 16, 48)[i])
                        ch.tick(dve.tensor_reduce(part[:, 0:8 * n], raws[i][:, :, :].rearrange(
                            "p k (c o) -> p (k c) o", c=8), AX.X, ALU.add, apply_absolute_value=True))
                        ch.settle()
                        dve.tensor_reduce(am[:, i:i + 1], part[:, 0:8 * n], AX.X, ALU.add).then_inc(s_am, 1)
                        dve.wait_ge(s_am, i + 1)
                    dve.wait_ge(s_gm, 3)
                    ch.tick(dve.tensor_scalar(scale[:, :], scale[:, :], 1.0 / (D * HID), None, ALU.mult))
                    ch.settle()
                    ch.tick(dve.tensor_scalar(half[:, :], scale[:, :], 0.5, None, ALU.mult))
                    ch.tick(dve.tensor_scalar(nhalf[:, :], scale[:, :], -0.5, None, ALU.mult))
                    ch.tick(dve.tensor_scalar(kup[:, :], scale[:, GATE:GATE + 1], 16.0, TINY, ALU.mult, ALU.max))
                    ch.settle()
                    ch.tick(dve.tensor_tensor(cdn[:, :], kup[:, :], scale[:, UPW:UPW + 1], ALU.mult))
                    ch.settle()
                    ch.tick(dve.reciprocal(kup[:, :], kup[:, :]))
                    ch.tick(dve.tensor_tensor(cdn[:, :], cdn[:, :], scale[:, DOWN:DOWN + 1], ALU.mult))
                    for i, n in enumerate((KT, KT, HT)):
                        w = raws[i][:, :, :].rearrange("p k n -> p (k n)")
                        size = n * (HID if i < 2 else D)
                        t = tern[i][:, :, :].rearrange("p k n -> p (k n)")
                        ch.settle()
                        ch.tick(dve.tensor_scalar(pos[:, 0:size], w, half[:, i:i + 1], None, ALU.is_gt))
                        ch.settle()
                        ch.tick(dve.scalar_tensor_tensor(t, w, nhalf[:, i:i + 1], pos[:, 0:size], ALU.is_lt,
                                                         ALU.subtract))
                        ch.settle()
                        for k in range(n):
                            x = tern[i][:, k, :].rearrange("p (c o) -> p c o", c=8)
                            o = OH if i < 2 else OD
                            ch.tick(dve.tensor_tensor(
                                x, x, sgn[i // 2][:, k, :].unsqueeze(2).to_broadcast([P, 8, o]), ALU.mult))
                    ch.settle()

            clear(nc, si.sems)

        xb = sc.sb("xb2", [P, TT, D])
        yb = sc.sb("yb2", [P, TT, D])
        aT = [sc.sb("a2T_hi", [P, KT, S], F16), sc.sb("a2T_lo", [P, KT, S], F16)]
        sl = sc.sb("silu_gate", [P, 2, S])
        hf = sc.sb("hidden", [P, 2, S])
        hT = [sc.sb("hidden_hi", [P, HT, S], F16), sc.sb("hidden_lo", [P, HT, S], F16)]
        st = sc.sb("st2", [P, TT, 6])
        mv = sc.sb("mv2", [P, TT, 2])
        ve = sc.sb("ve2", [P, TT])
        rs = sc.sb("rs2", [P, TT])
        bank_g = [sc.ps(f"bank_g{i}", [P, S]) for i in range(2)]
        bank_u = [sc.ps(f"bank_u{i}", [P, S]) for i in range(2)]
        bank_t = [sc.ps(f"bank2_t{i}", [P, S]) for i in range(2)]
        bank_y = [sc.ps(f"bank_y{i}", [P, S]) for i in range(2)]

        s_x = sc.sem("s2_x_loaded")
        s_dv = sc.sem("s2_dve_steps")
        s_ve = sc.sem("s2_variance")
        s_rs = sc.sem("s2_rstd")
        s_xn = sc.sem("s2_normed_rows")
        s_tf = sc.sem("s2_t_filled")
        s_th = sc.sem("s2_t_hi_out")
        s_tl = sc.sem("s2_t_lo_out")
        s_gf = sc.sem("s2_gate_filled")
        s_uf = sc.sem("s2_up_filled")
        s_sl = sc.sem("s2_silu")
        s_hf = sc.sem("s2_hidden")
        s_hh = sc.sem("s2_hidden_hi")
        s_hl = sc.sem("s2_hidden_lo")
        s_yf = sc.sem("s2_y_filled")
        s_yd = sc.sem("s2_y_out")
        s_fin = sc.sem("s2_final")
        s_out = sc.sem("s2_stored")

        def width(m):
            return min(P, HID - m * P)

        with nc.Fori(0, B) as b:
            with nc.Block() as block:

                @block.sync
                def _(sp):
                    sp.dma_start(xb[:, :, :], x2_dram[b].rearrange("(t p) d -> p t d", p=P)).then_inc(s_x, 16)
                    sp.wait_ge(s_fin, TT)
                    sp.dma_start(out[b].rearrange("(t p) d -> p t d", p=P), xb[:, :, :]).then_inc(s_out, 16)
                    sp.wait_ge(s_out, 16)

                @block.gpsimd
                def _(pool):
                    for n in range(3):
                        pool.wait_ge(s_ve, n + 1)
                        pool.tensor_tensor(rs[:, :], ve[:, :], C["mhalf"][:, 0:TT], ALU.pow).then_inc(s_rs, 1)

                @block.tensor
                def _(pe):
                    for t in range(TT):
                        pe.wait_ge(s_xn, t + 1)
                        if t >= 2:
                            pe.wait_ge(s_tl, t - 1)
                        for k in range(KT):
                            last = pe.transpose(bank_t[t % 2][:, k * P:(k + 1) * P], yb[:, t, k * P:(k + 1) * P],
                                                C["ident"][:, :])
                        last.then_inc(s_tf, 1)
                    pe.wait_ge(s_tl, TT)
                    for m in range(HT):
                        w = width(m)
                        for bank, tern, filled in ((bank_g, tg, s_gf), (bank_u, tu, s_uf)):
                            if m >= 2:
                                pe.wait_ge(s_hf, m - 1)
                            for k in range(KT):
                                for c in range(2):
                                    last = pe.matmul(bank[m % 2][0:w, :], tern[:, k, m * P:m * P + w],
                                                     aT[c][:, k, :], start=(k == 0 and c == 0),
                                                     stop=(k == KT - 1 and c == 1))
                            last.then_inc(filled, 1)
                    pe.wait_ge(s_hl, HT)
                    for t in range(TT):
                        if t >= 2:
                            pe.wait_ge(s_yd, t - 1)
                        for m in range(HT):
                            w = width(m)
                            for c in range(2):
                                last = pe.matmul(bank_y[t % 2][:, :], hT[c][0:w, m, t * P:(t + 1) * P],
                                                 td[0:w, m, :], start=(m == 0 and c == 0),
                                                 stop=(m == HT - 1 and c == 1))
                        last.then_inc(s_yf, 1)

                @block.scalar
                def _(act):
                    for t in range(TT):
                        act.wait_ge(s_tf, t + 1)
                        act.activation(aT[0][:, :, t * P:(t + 1) * P],
                                       bank_t[t % 2][:, :].rearrange("p (k c) -> p k c", c=P),
                                       ACT.Copy).then_inc(s_th, 1)
                    for m in range(HT + 1):
                        if m < HT:
                            w = width(m)
                            act.wait_ge(s_gf, m + 1)
                            act.activation(sl[0:w, m % 2, :], bank_g[m % 2][0:w, :], ACT.Silu,
                                           scale=scale[0:w, GATE:GATE + 1]).then_inc(s_sl, 1)
                        if m >= 1:
                            w = width(m - 1)
                            act.wait_ge(s_hf, m)
                            act.activation(hT[0][0:w, m - 1, :], hf[0:w, (m - 1) % 2, :],
                                           ACT.Copy).then_inc(s_hh, 1)

                @block.vector
                def _(dve):
                    ch = Chain(dve, s_dv)
                    count = {"rs": 0}

                    def statistics(src):
                        for t in range(TT):
                            ch.tick(dve.bn_stats(st[:, t, :], src(t)))
                        ch.settle()
                        for t in range(TT):
                            ch.tick(dve.bn_aggr(mv[:, t, :], st[:, t, :]))
                        ch.settle()
                        dve.tensor_scalar(ve[:, :], mv[:, :, 1], EPS, None, ALU.add).then_inc(s_ve, 1)
                        count["rs"] += 1
                        dve.wait_ge(s_rs, count["rs"])

                    def add_normed(src, done=None):
                        statistics(src)
                        for t in range(TT):
                            ch.tick(dve.tensor_scalar(yb[:, t, :], src(t), mv[:, t, 0:1], rs[:, t:t + 1],
                                                      ALU.subtract, ALU.mult))
                        ch.settle()
                        for t in range(TT):
                            ins = dve.tensor_tensor(xb[:, t, :], xb[:, t, :], yb[:, t, :], ALU.add)
                            if done is None:
                                ch.tick(ins)
                            else:
                                ins.then_inc(done, 1)
                        ch.settle()

                    dve.wait_ge(s_x, 16)
                    add_normed(lambda t: yacc[:, bass.ds(b * TT + t, 1), :].rearrange("p a n -> p (a n)"))
                    statistics(lambda t: xb[:, t, :])
                    for t in range(TT):
                        dve.tensor_scalar(yb[:, t, :], xb[:, t, :], mv[:, t, 0:1], rs[:, t:t + 1],
                                          ALU.subtract, ALU.mult).then_inc(s_xn, 1)
                    for t in range(TT):
                        dve.wait_ge(s_th, t + 1)
                        dve.tensor_tensor(aT[1][:, :, t * P:(t + 1) * P],
                                          bank_t[t % 2][:, :].rearrange("p (k c) -> p k c", c=P),
                                          aT[0][:, :, t * P:(t + 1) * P], ALU.subtract).then_inc(s_tl, 1)
                    for m in range(HT + 1):
                        if m < HT:
                            w = width(m)
                            dve.wait_ge(s_uf, m + 1)
                            dve.wait_ge(s_sl, m + 1)
                            if m >= 2:
                                dve.wait_ge(s_hh, m - 1)
                                dve.wait_ge(s_hl, m - 1)
                            dve.scalar_tensor_tensor(hf[0:w, m % 2, :], bank_u[m % 2][0:w, :], kup[0:w, 0:1],
                                                     sl[0:w, m % 2, :], ALU.mult, ALU.mult).then_inc(s_hf, 1)
                        if m >= 1:
                            w = width(m - 1)
                            dve.wait_ge(s_hf, m)
                            dve.wait_ge(s_hh, m)
                            dve.tensor_tensor(hT[1][0:w, m - 1, :], hf[0:w, (m - 1) % 2, :],
                                              hT[0][0:w, m - 1, :], ALU.subtract).then_inc(s_hl, 1)
                    for t in range(TT):
                        dve.wait_ge(s_yf, t + 1)
                        dve.tensor_scalar(yb[:, t, :], bank_y[t % 2][:, :], cdn[:, 0:1], None,
                                          ALU.mult).then_inc(s_yd, 1)
                    dve.wait_ge(s_yd, TT)
                    add_normed(lambda t: yb[:, t, :], s_fin)

            clear(nc, sc.sems)


def build(nc, A, out, stages=4):
    x2_dram = nc.dram_tensor("x2_scratch", [B, S, D], F32).ap()
    fused_dram = nc.dram_tensor("fused_scratch", [D, G1 * UP], F32).ap()
    with ExitStack() as stack:
        sc = Scope(nc, stack)
        C = {"ident": sc.sb("ident", [P, P]), "mhalf": sc.sb("mhalf", [P, 8])}
        xT = [sc.sb("xT_hi", [P, KT, B * S], F16), sc.sb("xT_lo", [P, KT, B * S], F16)]
        with ExitStack() as first:
            s0 = Scope(nc, first)
            for n, shape, dt in (("rel", [P, S], F32), ("sel", [P, 8, P], F16), ("pairmask", [P, 2], F32),
                                 ("bias", [P, D], F32)):
                C[n] = s0.sb(n, shape, dt)
            W0 = {n: [s0.sb(f"{n}_hi", [P, KT, w], F16), s0.sb(f"{n}_lo", [P, KT, w], F16)]
                  for n, w in (("wq", D), ("wkv", P + E0), ("wo", D), ("wf", D))}
            W0["gm"] = s0.sb("gm0", [P, 4])
            with ExitStack() as second:
                ss = Scope(nc, second)
                raw = {n: ss.sb(f"raw_{n}", [P, KT, w], F32)
                       for n, w in (("wq", D), ("wkv", P + E0), ("wo", D), ("wf", D))}
                codes = ss.sb("codes", [P, KT, D], I32)
                qsc = ss.sb("qscales", [P, KT, D])
                rg = ss.sb("rg0", [P, 4])
                s_c = ss.sem("s_constants_loaded")
                with nc.Block() as block:

                    @block.sync
                    def _(sp):
                        for n in ("ident", "rel", "pairmask"):
                            sp.dma_start(C[n][:, :], A[n]).then_inc(s_c, 16)
                        sp.dma_start(C["sel"][:, :, :], A["sel"]).then_inc(s_c, 16)
                        sp.dma_start(C["bias"][:, :], A["bias"].partition_broadcast(P)).then_inc(s_c, 16)
                        sp.wait_ge(s_c, 16 * 5)

                    @block.gpsimd
                    def _(pool):
                        pool.memset(C["mhalf"][:, :], -0.5)

                def km(ap):
                    return ap.rearrange("(k p) n -> p k n", p=P)

                jobs = []
                for n, loads in (("wq", [(raw["wq"][:, :, :], km(A["wq0"]))]),
                                 ("wkv", [(raw["wkv"][:, :, 0:P], km(A["wk0"])),
                                          (raw["wkv"][:, :, P:P + E0], km(A["wv0"]))]),
                                 ("wo", [(raw["wo"][:, :, :], km(A["wo0"]))]),
                                 ("wf", [(codes[:, :, :], km(A["codes"])), (qsc[:, :, :], km(A["qscales"]))])):
                    job = [n, loads, raw[n][:, :, :], W0[n][0][:, :, :], W0[n][1][:, :, :]]
                    if n == "wf":
                        job.append((codes[:, :, :], qsc[:, :, :]))
                    jobs.append(job)
                split_matrices(nc, ss, "w0", jobs, W0["gm"], rg)
                clear(nc, ss.sems)
            layer0(nc, A, W0, C, xT, x2_dram)
        if stages < 2:
            return
        fuse_up_projections(nc, A, C, fused_dram, None)
        yacc = sc.sb("yacc", [P, B * TT, D])
        attention1(nc, A, C, xT, yacc, fused_dram)
        if stages < 3:
            return
        feed_forward1(nc, A, C, yacc, x2_dram, out)


def octonion_table():
    table = np.zeros((8, 8, 8), np.float32)
    table[0, 0, 0] = 1.0
    for i in range(1, 8):
        table[0, i, i] = table[i, 0, i] = 1.0
        table[i, i, 0] = -1.0
    for a, b, c in [(1, 2, 3), (1, 4, 5), (1, 7, 6), (2, 4, 6), (2, 5, 7), (3, 4, 7), (3, 6, 5)]:
        for x, y, z in ((a, b, c), (b, c, a), (c, a, b)):
            table[x, y, z] = 1.0
            table[y, x, z] = -1.0
    return np.abs(table).argmax(0), table.sum(0)


def constants():
    out = {"ident": np.eye(P, dtype=np.float32)}
    rel = (np.arange(S)[None, :] - (S - P) - np.arange(P)[:, None]).astype(np.float32)
    out["rel"] = np.where(rel <= 0, rel, np.float32(MASKED)).astype(np.float32)
    out["mask"] = np.where(rel <= 0, 0.0, MASKED).astype(np.float32)
    sel = np.zeros((P, 4, 2, P), np.float16)
    for r in range(4):
        for x in range(32):
            sel[32 * r + x, r, 0, [x, 64 + x]] = 1
            sel[32 * r + x, r, 1, [32 + x, 96 + x]] = 1
    out["sel"] = sel.reshape(P, 8, P)
    low = (np.arange(P) % 32 < 16).astype(np.float32)
    out["pairmask"] = np.stack([low, 1 - low], 1)
    inv_freq = 1.0 / 10000.0 ** (np.arange(0, E1, 2, dtype=np.float32) / E1)
    freqs = np.outer(np.arange(S, dtype=np.float32), inv_freq)
    emb = np.concatenate([freqs, freqs], -1).T
    cos, sin = np.cos(emb).astype(np.float32), np.sin(emb).astype(np.float32)
    sin[:E1 // 2] *= -1
    roped = (np.arange(E1) % (E1 // 2) < 32)[:, None]
    out["cosq"], out["sinq"] = cos, sin
    out["cosk"] = np.where(roped, cos, 1.0).astype(np.float32)
    out["sink"] = np.where(roped, sin, 0.0).astype(np.float32)
    sign = octonion_table()[1]
    rows = np.arange(D).reshape(KT, P) // OD
    out["sgn_in"] = np.ascontiguousarray(-sign[rows].transpose(1, 0, 2)).astype(np.float16)
    rows = np.minimum(np.arange(HT * P), HID - 1).reshape(HT, P) // OH
    out["sgn_dn"] = np.ascontiguousarray(-sign[rows].transpose(1, 0, 2)).astype(np.float16)
    return out


def lay_out(inputs):
    a = {k: np.asarray(v) for k, v in inputs.items()}
    unit = octonion_table()[0]
    i = np.arange(8)[:, None]
    k = np.arange(8)[None, :]
    wkv = a["L0_attn_Wkv"]
    out = {
        "x": a["L0_attn_hidden_states"],
        "wq0": a["L0_attn_Wq"],
        "wk0": np.tile(wkv[:, :E0], (1, P // E0)),
        "wv0": wkv[:, E0:],
        "wo0": a["L0_attn_Wo"],
        "codes": a["L0_ffn_q_vals"].reshape(D, D).T,
        "qscales": np.repeat(a["L0_ffn_q_scales"].T, 32, axis=0),
        "bias": a["L0_ffn_bias"],
        "wq1": a["L1_attn_Wq"].reshape(G1, HG * E1, KT, P).transpose(0, 3, 2, 1),
        "wkr1": a["L1_attn_Wkr"].reshape(G1, 64, KT, P).transpose(0, 3, 2, 1),
        "wdk1": a["L1_attn_Wdk"],
        "wup1": np.concatenate([a["L1_attn_Wupk"].reshape(G1, 64, D), a["L1_attn_Wupv"].reshape(G1, E1, D)],
                               1).reshape(G1 * UP, D).T,
        "wo1": a["L1_attn_Wo"].reshape(D, G1, HG, E1).transpose(1, 3, 2, 0),
        "w_gate": a["L1_ffn_w_gate"][unit[i, k]].transpose(0, 3, 1, 2).reshape(D, HID),
        "w_up": a["L1_ffn_w_up"][unit[i, k]].transpose(0, 3, 1, 2).reshape(D, HID),
        "w_down": a["L1_ffn_w_down"][unit[i, k]].transpose(0, 3, 1, 2).reshape(HID, D),
    }
    out.update(constants())
    return {n: np.ascontiguousarray(v) for n, v in out.items()}


def declare(nc, arrays):
    return {n: nc.dram_tensor(f"in_{n}", v.shape, mybir.dt.from_np(v.dtype), kind="ExternalInput").ap()
            for n, v in arrays.items()}


def kernel(**inputs):
    import concourse.bacc as bacc
    from concourse.bass_utils import run_bass_kernel_spmd

    arrays = lay_out(inputs)
    nc = bacc.Bacc("TRN2", target_bir_lowering=False, num_devices=1)
    A = declare(nc, arrays)
    out = nc.dram_tensor("out_x", [B, S, D], F32, kind="ExternalOutput").ap()
    build(nc, A, out)
    r = run_bass_kernel_spmd(nc, [{f"in_{n}": v for n, v in arrays.items()}], core_ids=[0])
    return r.results[0]["out_x"]
```

```python
from contextlib import ExitStack

import concourse.bass as bass
import numpy as np
from concourse import mybir

ALU = mybir.AluOpType
ACT = mybir.ActivationFunctionType
AX = mybir.AxisListType
F32 = mybir.dt.float32
F16 = mybir.dt.float16
I32 = mybir.dt.int32
RMAX = bass.bass_isa.ReduceOp.max
RADD = bass.bass_isa.ReduceOp.add

P = 128
B, S, D = 4, 512, 512
KT = D // P
TT = S // P
EPS = 1e-5
MASKED = -1e20
TINY = 1e-30

H0, E0 = 32, 16
PAIRS = H0 // 2
SLOPE0 = 2.0 ** (-(2.0 ** (-(np.log2(H0) - 3))))
SLOPES = [float(np.float32(SLOPE0 ** (i + 1))) for i in range(H0)]

H1, G1, E1 = 32, 8, 128
HG = H1 // G1
UP = 64 + E1
WK = E1 + E1

HID = 1360
HT = -(-HID // P)
OH, OD = HID // 8, D // 8

TRI = [P * t * (t + 1) // 2 for t in range(TT)]
TRIW = P * TT * (TT + 1) // 2
COL = [sum(TT - i for i in range(j)) for j in range(TT)]
NBLK = TT * (TT + 1) // 2


class Chain:

    def __init__(self, eng, sem):
        self.eng, self.sem, self.n = eng, sem, 0

    def tick(self, ins):
        ins.then_inc(self.sem, 1)
        self.n += 1

    def settle(self):
        self.eng.wait_ge(self.sem, self.n)


def clear(nc, sems):
    nums = sorted(s.num for s in sems)
    assert nums == list(range(nums[0], nums[-1] + 1))
    nc.all_engine_barrier(sems_to_clear=range(nums[0], nums[-1] + 1))


class Scope:

    def __init__(self, nc, stack):
        self.nc, self.stack, self.sems = nc, stack, []

    def sb(self, name, shape, dt=F32):
        return self.stack.enter_context(self.nc.sbuf_tensor(name, shape, dt))

    def ps(self, name, shape, dt=F32):
        return self.stack.enter_context(self.nc.psum_tensor(name, shape, dt))

    def sem(self, name):
        s = self.stack.enter_context(self.nc.semaphore(name))
        self.sems.append(s)
        return s


def split_matrices(nc, sc, tag, jobs, gm, rg):
    am = sc.sb(f"{tag}_am", [P, len(jobs)])
    s_ld = [sc.sem(f"{tag}_loaded{i}") for i in range(len(jobs))]
    s_dv = sc.sem(f"{tag}_dve_steps")
    s_am = sc.sem(f"{tag}_rowmax")
    s_gm = sc.sem(f"{tag}_globalmax")
    s_rg = sc.sem(f"{tag}_reciprocal")
    s_hi = sc.sem(f"{tag}_hi")
    s_lo = sc.sem(f"{tag}_lo")

    def flat(ap):
        return ap.rearrange("p a b -> p (a b)")

    with nc.Block() as block:

        @block.sync
        def _(sp):
            for i, job in enumerate(jobs):
                for dst, src in job[1]:
                    sp.dma_start(dst, src).then_inc(s_ld[i], 16)

        @block.gpsimd
        def _(pool):
            for i in range(len(jobs)):
                pool.wait_ge(s_am, i + 1)
                pool.partition_all_reduce(gm[:, i:i + 1], am[:, i:i + 1], P, RMAX).then_inc(s_gm, 1)

        @block.vector
        def _(dve):
            ch = Chain(dve, s_dv)
            for i, job in enumerate(jobs):
                raw = flat(job[2])
                dve.wait_ge(s_ld[i], 16 * len(job[1]))
                if len(job) > 5:
                    codes, scales = job[5]
                    ch.tick(dve.tensor_scalar(raw, flat(codes), -128.0, None, ALU.add))
                    ch.settle()
                    ch.tick(dve.tensor_tensor(raw, raw, flat(scales), ALU.mult))
                    ch.settle()
                dve.tensor_reduce(am[:, i:i + 1], raw, AX.X, ALU.max,
                                  apply_absolute_value=True).then_inc(s_am, 1)
            for i, job in enumerate(jobs):
                dve.wait_ge(s_gm, i + 1)
                ch.tick(dve.tensor_scalar(gm[:, i:i + 1], gm[:, i:i + 1], TINY, None, ALU.max))
                ch.settle()
                dve.reciprocal(rg[:, i:i + 1], gm[:, i:i + 1]).then_inc(s_rg, 1)
                dve.wait_ge(s_rg, i + 1)
                dve.wait_ge(s_hi, i + 1)
                dve.scalar_tensor_tensor(flat(job[4]), flat(job[2]), rg[:, i:i + 1], flat(job[3]),
                                         ALU.mult, ALU.subtract).then_inc(s_lo, 1)

        @block.scalar
        def _(act):
            for i, job in enumerate(jobs):
                act.wait_ge(s_rg, i + 1)
                act.activation(flat(job[3]), flat(job[2]), ACT.Copy,
                               scale=rg[:, i:i + 1]).then_inc(s_hi, 1)


def layer0(nc, A, W0, C, xT, x2_dram):
    with ExitStack() as stack:
        sc = Scope(nc, stack)
        xb = sc.sb("xb", [P, TT, D])
        yb = sc.sb("yb", [P, TT, D])
        aT = [sc.sb("aT_hi", [P, KT, S], F16), sc.sb("aT_lo", [P, KT, S], F16)]
        khi = sc.sb("khi", [P, S], F16)
        kst = sc.sb("kst", [P, S], F16)
        kab = sc.sb("kab", [P, 2, S], F16)
        v2 = sc.sb("v2", [P, TT, 2 * E0], F16)
        qT = [sc.sb("qT_hi", [P, KT, S], F16), sc.sb("qT_lo", [P, KT, S], F16)]
        stk = sc.sb("stk", [P, 2, S], F16)
        tab = sc.sb("tab", [P, 4, S])
        xp = sc.sb("xp", [P, 4, TRIW])
        pT = [sc.sb("pT_hi", [P, 3, NBLK, P], F16), sc.sb("pT_lo", [P, 3, NBLK, P], F16)]
        ob = sc.sb("ob", [P, TT, D])
        mx = sc.sb("mx", [P, 4, TT])
        nm = sc.sb("nm", [P, 4, TT])
        lsum = sc.sb("lsum", [P, H0, TT])
        rsum = sc.sb("rsum", [P, H0, TT])
        st = sc.sb("st", [P, TT, 6])
        mv = sc.sb("mv", [P, TT, 2])
        ve = sc.sb("ve", [P, TT])
        rs = sc.sb("rs", [P, TT])
        cs = sc.sb("cs", [P, 1])
        cinv = sc.sb("cinv", [P, 1])
        cy = sc.sb("cy", [P, 1])
        bank_s = [sc.ps(f"bank_s{i}", [P, S]) for i in range(3)]
        bank_t = [sc.ps(f"bank_t{i}", [P, S]) for i in range(3)]
        bank_v = [sc.ps(f"bank_v{i}", [P, S]) for i in range(2)]

        s_x = sc.sem("s_x_loaded")
        s_dv = sc.sem("s_dve_steps")
        s_cs = sc.sem("s_constants")
        s_ve = sc.sem("s_variance")
        s_rs = sc.sem("s_rstd")
        s_xn = sc.sem("s_normed_rows")
        s_tf = sc.sem("s_t_filled")
        s_th = sc.sem("s_t_hi_out")
        s_tl = sc.sem("s_t_lo_out")
        s_sf = sc.sem("s_s_filled")
        s_sh = sc.sem("s_s_hi_out")
        s_sd = sc.sem("s_s_freed_by_dve")
        s_sa = sc.sem("s_stack_ready")
        s_tab = sc.sem("s_table")
        s_nm = sc.sem("s_negmax")
        s_ex = sc.sem("s_exp")
        s_pf = sc.sem("s_pv_filled")
        s_pd = sc.sem("s_pv_out")
        s_on = sc.sem("s_heads_normed")
        s_out = sc.sem("s_x_stored")

        uses = ["K", "V"] + [("q", m) for m in range(KT)] + [("stack", 0)]
        for p in range(PAIRS):
            uses += [("stack", p + 1)] * (p + 1 < PAIRS) + [("s", p, i) for i in range(6)]
        uses += [("y", t) for t in range(TT)] + [("f", t) for t in range(TT)]
        number = {u: n for n, u in enumerate(uses)}
        emptied, by_dve, by_act = [], 0, 0
        for u in uses:
            if u[0] == "stack":
                by_act += 1
                emptied.append((s_sa, by_act))
            else:
                by_dve += 1
                emptied.append((s_sd, by_dve))

        def sbank(u):
            return bank_s[number[u] % 3]

        T_HEADS, T_OUT = TT, TT + TT * H0
        T_NORM2, T_NORM3 = T_OUT + TT, T_OUT + 2 * TT

        wq, wkv, wo, wf = W0["wq"], W0["wkv"], W0["wo"], W0["wf"]
        GQ, GKV, GO, GF = range(4)
        gm = W0["gm"]

        with nc.Fori(0, B) as b:
            with nc.Block() as block:

                @block.sync
                def _(sp):
                    sp.dma_start(xb[:, :, :], A["x"][b].rearrange("(t p) d -> p t d", p=P)).then_inc(s_x, 16)
                    sp.wait_ge(s_xn, 3 * TT)
                    sp.dma_start(x2_dram[b].rearrange("(t p) d -> p t d", p=P), xb[:, :, :]).then_inc(s_out, 16)
                    sp.wait_ge(s_out, 16)

                @block.gpsimd
                def _(pool):
                    def rstd(n):
                        pool.wait_ge(s_ve, n)
                        pool.tensor_tensor(rs[:, :], ve[:, :], C["mhalf"][:, 0:TT], ALU.pow).then_inc(s_rs, 1)

                    rstd(1)
                    pool.wait_ge(s_cs, 2)
                    for h in range(H0):
                        if h >= 4:
                            pool.wait_ge(s_nm, h - 3)
                        pool.tensor_scalar(tab[:, h % 4, :], C["rel"][:, :], 4.0 * SLOPES[h], cinv[:, 0:1],
                                           ALU.mult, ALU.mult).then_inc(s_tab, 1)
                    for n in range(2, 6):
                        rstd(n)

                @block.tensor
                def _(pe):
                    def take(u):
                        n = number[u]
                        if n >= 3:
                            pe.wait_ge(*emptied[n - 3])
                        return sbank(u)

                    def transpose4(n, rows):
                        if n >= 3:
                            pe.wait_ge(s_tl, n - 2)
                        for k in range(KT):
                            last = pe.transpose(bank_t[n % 3][:, k * P:(k + 1) * P],
                                                rows[:, k * P:(k + 1) * P], C["ident"][:, :])
                        last.then_inc(s_tf, 1)

                    def product(out, lhs, rhs, fill):
                        for k in range(KT):
                            for i, (a, c) in enumerate(((0, 0), (1, 0), (0, 1))):
                                last = pe.matmul(out, lhs(a, k), rhs(c, k), start=(k == 0 and i == 0),
                                                 stop=(k == KT - 1 and i == 2))
                        if fill:
                            last.then_inc(s_sf, 1)

                    for t in range(TT):
                        pe.wait_ge(s_xn, t + 1)
                        transpose4(t, yb[:, t, :])
                    pe.wait_ge(s_tl, TT)
                    product(take("K")[:, :], lambda a, k: wkv[a][:, k, 0:P], lambda c, k: aT[c][:, k, :], True)
                    bank = take("V")
                    for t in range(TT):
                        product(bank[:, t * E0:(t + 1) * E0], lambda a, k: aT[a][:, k, t * P:(t + 1) * P],
                                lambda c, k: wkv[c][:, k, P:P + E0], t == TT - 1)
                    for m in range(KT):
                        product(take(("q", m))[:, :], lambda a, k: wq[a][:, k, m * P:(m + 1) * P],
                                lambda c, k: aT[c][:, k, :], True)

                    def stack_queries(p):
                        m, r = p // 4, p % 4
                        bank = take(("stack", p))
                        pe.wait_ge(s_sd, 3 + m)
                        pe.matmul(bank[:, :], C["sel"][:, 2 * r, :], qT[0][:, m, :], start=True, stop=False)
                        pe.matmul(bank[:, :], C["sel"][:, 2 * r + 1, :], qT[1][:, m, :], start=False,
                                  stop=True).then_inc(s_sf, 1)

                    def scores(p):
                        pe.wait_ge(s_sa, p + 1)
                        q = stk[:, p % 2, :]
                        for i, (t, heads) in enumerate(((0, (0, 1)), (1, (0, 1)), (2, (0,)), (2, (1,)), (3, (0,)), (3, (1,)))):
                            bank, w = take(("s", p, i)), P * (t + 1)
                            pe.matmul(bank[:, 0:len(heads) * w].rearrange("p (h k) -> p h k", k=w),
                                      q[:, t * P:(t + 1) * P], kab[:, heads[0]:heads[-1] + 1, 0:w],
                                      start=True, stop=True).then_inc(s_sf, 1)

                    def transpose_probs(h):
                        pe.wait_ge(s_ex, h + 1)
                        for j in range(TT):
                            n = T_HEADS + TT * h + j
                            pe.wait_ge(s_tl, n - 2)
                            for t in range(j, TT):
                                last = pe.transpose(bank_t[n % 3][:, t * P:(t + 1) * P],
                                                    xp[:, h % 4, TRI[t] + j * P:TRI[t] + (j + 1) * P],
                                                    C["ident"][:, :])
                            last.then_inc(s_tf, 1)

                    def weigh_values(h):
                        pe.wait_ge(s_tl, T_HEADS + TT * (h + 1))
                        if h >= 2:
                            pe.wait_ge(s_pd, h - 1)
                        for t in range(TT):
                            for j in range(t + 1):
                                for a in range(2):
                                    last = pe.matmul(bank_v[h % 2][:, t * 2 * E0:(t + 1) * 2 * E0],
                                                     pT[a][:, h % 3, COL[j] + t - j, :], v2[:, j, :],
                                                     start=(j == 0 and a == 0), stop=(j == t and a == 1))
                        last.then_inc(s_pf, 1)

                    stack_queries(0)
                    for p in range(PAIRS + 2):
                        if p + 1 < PAIRS:
                            stack_queries(p + 1)
                        if p < PAIRS:
                            if p == 0:
                                pe.wait_ge(s_cs, 3)
                            scores(p)
                        if 1 <= p <= PAIRS:
                            transpose_probs(2 * p - 2)
                            if p > 1:
                                weigh_values(2 * p - 3)
                            transpose_probs(2 * p - 1)
                            weigh_values(2 * p - 2)
                        if p == PAIRS + 1:
                            weigh_values(H0 - 1)

                    for t in range(TT):
                        pe.wait_ge(s_on, t + 1)
                        transpose4(T_OUT + t, ob[:, t, :])
                    for t in range(TT):
                        pe.wait_ge(s_tl, T_OUT + t + 1)
                        product(take(("y", t))[:, :], lambda a, k: aT[a][:, k, t * P:(t + 1) * P],
                                lambda c, k: wo[c][:, k, :], True)
                    for t in range(TT):
                        pe.wait_ge(s_xn, TT + t + 1)
                        transpose4(T_NORM2 + t, yb[:, t, :])
                    for t in range(TT):
                        pe.wait_ge(s_tl, T_NORM2 + t + 1)
                        product(take(("f", t))[:, :], lambda a, k: aT[a][:, k, t * P:(t + 1) * P],
                                lambda c, k: wf[c][:, k, :], True)
                    for t in range(TT):
                        pe.wait_ge(s_xn, 2 * TT + t + 1)
                        transpose4(T_NORM3 + t, yb[:, t, :])

                @block.scalar
                def _(act):
                    def hi4(n, dst):
                        act.wait_ge(s_tf, n + 1)
                        act.activation(dst, bank_t[n % 3][:, :].rearrange("p (k c) -> p k c", c=P),
                                       ACT.Copy).then_inc(s_th, 1)

                    def hi_s(u, dst, src):
                        act.wait_ge(s_sf, number[u] + 1)
                        act.activation(dst, src, ACT.Copy).then_inc(s_sh, 1)

                    for t in range(TT):
                        hi4(t, aT[0][:, :, t * P:(t + 1) * P])
                    hi_s("K", khi[:, :], sbank("K")[:, :])
                    hi_s("V", v2[:, :, 0:E0], sbank("V")[:, 0:TT * E0].rearrange("p (t e) -> p t e", e=E0))
                    for m in range(KT):
                        hi_s(("q", m), qT[0][:, m, :], sbank(("q", m))[:, :])

                    def copy_stack(p):
                        u = ("stack", p)
                        if p >= 2:
                            act.wait_ge(s_sf, number[("s", p - 2, 5)] + 1)
                        act.wait_ge(s_sf, number[u] + 1)
                        act.activation(stk[:, p % 2, :], sbank(u)[:, :], ACT.Copy).then_inc(s_sa, 1)

                    def probs_hi(h):
                        for j in range(TT):
                            n = T_HEADS + TT * h + j
                            act.wait_ge(s_tf, n + 1)
                            if h >= 3:
                                act.wait_ge(s_pf, h - 2)
                            act.activation(pT[0][:, h % 3, COL[j]:COL[j] + TT - j, :],
                                           bank_t[n % 3][:, j * P:].rearrange("p (t c) -> p t c", c=P),
                                           ACT.Copy).then_inc(s_th, 1)

                    copy_stack(0)
                    for p in range(PAIRS + 1):
                        if p + 1 < PAIRS:
                            copy_stack(p + 1)
                        if p >= 1:
                            probs_hi(2 * p - 2)
                            probs_hi(2 * p - 1)
                        if p < PAIRS:
                            for h in (2 * p, 2 * p + 1):
                                act.wait_ge(s_nm, h + 1)
                                for t in range(TT):
                                    x = xp[:, h % 4, TRI[t]:TRI[t] + P * (t + 1)]
                                    last = act.activation(x, x, ACT.Exp, bias=nm[:, h % 4, t:t + 1],
                                                          accum_out=lsum[:, h, t:t + 1])
                                last.then_inc(s_ex, 1)
                    for t in range(TT):
                        hi4(T_OUT + t, aT[0][:, :, t * P:(t + 1) * P])
                    for t in range(TT):
                        hi4(T_NORM2 + t, aT[0][:, :, t * P:(t + 1) * P])
                    for t in range(TT):
                        hi4(T_NORM3 + t, xT[0][:, :, bass.ds(b * S + t * P, P)])

                @block.vector
                def _(dve):
                    ch = Chain(dve, s_dv)
                    count = {"rs": 0}

                    def statistics(src):
                        for t in range(TT):
                            ch.tick(dve.bn_stats(st[:, t, :], src[:, t, :]))
                        ch.settle()
                        for t in range(TT):
                            ch.tick(dve.bn_aggr(mv[:, t, :], st[:, t, :]))
                        ch.settle()
                        dve.tensor_scalar(ve[:, :], mv[:, :, 1], EPS, None, ALU.add).then_inc(s_ve, 1)
                        count["rs"] += 1
                        dve.wait_ge(s_rs, count["rs"])

                    def norm_rows():
                        statistics(xb)
                        for t in range(TT):
                            dve.tensor_scalar(yb[:, t, :], xb[:, t, :], mv[:, t, 0:1], rs[:, t:t + 1],
                                              ALU.subtract, ALU.mult).then_inc(s_xn, 1)

                    def add_normed():
                        ch.settle()
                        statistics(yb)
                        for t in range(TT):
                            ch.tick(dve.tensor_scalar(yb[:, t, :], yb[:, t, :], mv[:, t, 0:1], rs[:, t:t + 1],
                                                      ALU.subtract, ALU.mult))
                        ch.settle()
                        for t in range(TT):
                            ch.tick(dve.tensor_tensor(xb[:, t, :], xb[:, t, :], yb[:, t, :], ALU.add))
                        ch.settle()

                    def lo4(n, hi, lo):
                        dve.wait_ge(s_th, n + 1)
                        dve.tensor_tensor(lo, bank_t[n % 3][:, :].rearrange("p (k c) -> p k c", c=P), hi,
                                          ALU.subtract).then_inc(s_tl, 1)

                    ch.tick(dve.tensor_scalar(cs[:, :], gm[:, GQ:GQ + 1], gm[:, GKV:GKV + 1], E0 ** -0.5,
                                              ALU.mult, ALU.mult))
                    dve.tensor_scalar(cy[:, :], gm[:, GKV:GKV + 1], gm[:, GO:GO + 1], None,
                                      ALU.mult).then_inc(s_cs, 1)
                    ch.settle()
                    ch.tick(dve.tensor_scalar(cinv[:, :], cs[:, :], 4.0, None, ALU.mult))
                    ch.settle()
                    dve.reciprocal(cinv[:, :], cinv[:, :]).then_inc(s_cs, 1)

                    dve.wait_ge(s_x, 16)
                    norm_rows()
                    for t in range(TT):
                        lo4(t, aT[0][:, :, t * P:(t + 1) * P], aT[1][:, :, t * P:(t + 1) * P])

                    dve.wait_ge(s_sh, 1)
                    dve.tensor_tensor(kst[64:128, :], sbank("K")[64:128, :], khi[64:128, :],
                                      ALU.subtract).then_inc(s_sd, 1)
                    ch.tick(dve.tensor_copy(kst[0:64, :], khi[0:64, :]))
                    dve.wait_ge(s_sh, 2)
                    dve.tensor_tensor(v2[:, :, E0:2 * E0],
                                      sbank("V")[:, 0:TT * E0].rearrange("p (t e) -> p t e", e=E0),
                                      v2[:, :, 0:E0], ALU.subtract).then_inc(s_sd, 1)
                    ch.settle()
                    dve.wait_ge(s_sd, 2)
                    ch.tick(dve.tensor_scalar(kab[:, 0, :], kst[:, :], C["pairmask"][:, 0:1], None, ALU.mult))
                    ch.tick(dve.tensor_scalar(kab[:, 1, :], kst[:, :], C["pairmask"][:, 1:2], None, ALU.mult))
                    ch.settle()
                    dve.memset(ve[:, 0:1], 1.0).then_inc(s_cs, 1)
                    for m in range(KT):
                        dve.wait_ge(s_sh, 3 + m)
                        dve.tensor_tensor(qT[1][:, m, :], sbank(("q", m))[:, :], qT[0][:, m, :],
                                          ALU.subtract).then_inc(s_sd, 1)

                    def biased_scores(p):
                        if p >= 2:
                            dve.wait_ge(s_tf, T_HEADS + TT * (2 * p - 2))
                        dve.wait_ge(s_tab, 2 * p + 2)
                        for i, (t, heads) in enumerate(((0, (0, 1)), (1, (0, 1)), (2, (0,)), (2, (1,)), (3, (0,)), (3, (1,)))):
                            u, w = ("s", p, i), P * (t + 1)
                            dve.wait_ge(s_sf, number[u] + 1)
                            for k, e in enumerate(heads):
                                h = 2 * p + e
                                last = dve.tensor_tensor_reduce(
                                    out=xp[:, h % 4, TRI[t]:TRI[t] + w], in0=sbank(u)[:, k * w:(k + 1) * w],
                                    in1=tab[:, h % 4, S - w:S], scale=cs[:, 0:1], scalar=-3e38,
                                    op0=ALU.add, op1=ALU.max, accum_out=mx[:, h % 4, t:t + 1])
                            last.then_inc(s_sd, 1)
                        dve.wait_ge(s_sd, emptied[number[("s", p, 5)]][1])
                        for h in (2 * p, 2 * p + 1):
                            dve.tensor_scalar(nm[:, h % 4, :], mx[:, h % 4, :], -1.0, None,
                                              ALU.mult).then_inc(s_nm, 1)

                    def probs_lo(h):
                        for j in range(TT):
                            n = T_HEADS + TT * h + j
                            dve.wait_ge(s_th, n + 1)
                            c = slice(COL[j], COL[j] + TT - j)
                            dve.tensor_tensor(pT[1][:, h % 3, c, :],
                                              bank_t[n % 3][:, j * P:].rearrange("p (t c) -> p t c", c=P),
                                              pT[0][:, h % 3, c, :], ALU.subtract).then_inc(s_tl, 1)

                    def head_out(h):
                        dve.wait_ge(s_pf, h + 1)
                        dve.tensor_reduce(ob[:, :, h * E0:(h + 1) * E0],
                                          bank_v[h % 2][:, 0:TT * 2 * E0].rearrange(
                                              "p (t c e) -> p t e c", c=2, e=E0),
                                          AX.X, ALU.add).then_inc(s_pd, 1)

                    for p in range(PAIRS + 2):
                        if p < PAIRS:
                            biased_scores(p)
                        if 1 <= p <= PAIRS:
                            probs_lo(2 * p - 2)
                            if p > 1:
                                head_out(2 * p - 3)
                            probs_lo(2 * p - 1)
                            head_out(2 * p - 2)
                        if p == PAIRS + 1:
                            head_out(H0 - 1)

                    ch.tick(dve.reciprocal(rsum[:, :, :], lsum[:, :, :]))
                    ch.settle()
                    dve.wait_ge(s_pd, H0)
                    for t in range(TT):
                        o = ob[:, t, :].rearrange("p (h e) -> p h e", e=E0)
                        dve.tensor_tensor(o, o, rsum[:, :, t:t + 1].to_broadcast([P, H0, E0]),
                                          ALU.mult).then_inc(s_on, 1)
                    for t in range(TT):
                        lo4(T_OUT + t, aT[0][:, :, t * P:(t + 1) * P], aT[1][:, :, t * P:(t + 1) * P])
                    for t in range(TT):
                        dve.wait_ge(s_sf, number[("y", t)] + 1)
                        dve.tensor_scalar(yb[:, t, :], sbank(("y", t))[:, :], cy[:, 0:1], None,
                                          ALU.mult).then_inc(s_sd, 1)
                    dve.wait_ge(s_sd, emptied[number[("y", TT - 1)]][1])
                    add_normed()
                    norm_rows()
                    for t in range(TT):
                        lo4(T_NORM2 + t, aT[0][:, :, t * P:(t + 1) * P], aT[1][:, :, t * P:(t + 1) * P])
                    for t in range(TT):
                        dve.wait_ge(s_sf, number[("f", t)] + 1)
                        dve.scalar_tensor_tensor(yb[:, t, :], sbank(("f", t))[:, :], gm[:, GF:GF + 1],
                                                 C["bias"][:, :], ALU.mult, ALU.add).then_inc(s_sd, 1)
                    dve.wait_ge(s_sd, emptied[number[("f", TT - 1)]][1])
                    add_normed()
                    norm_rows()
                    for t in range(TT):
                        c = bass.ds(b * S + t * P, P)
                        lo4(T_NORM3 + t, xT[0][:, :, c], xT[1][:, :, c])

            clear(nc, sc.sems)


def fuse_up_projections(nc, A, C, fused_dram, g1):
    with ExitStack() as stack:
        sc = Scope(nc, stack)
        NU = G1 * UP
        raw_d = sc.sb("raw_d", [P, KT, D])
        raw_u = sc.sb("raw_u", [P, KT, NU])
        wd = [sc.sb("wdk_hi", [P, KT, D], F16), sc.sb("wdk_lo", [P, KT, D], F16)]
        wu = [sc.sb("wup_hi", [P, KT, NU], F16), sc.sb("wup_lo", [P, KT, NU], F16)]
        fused = sc.sb("fused", [P, KT, NU])
        gm = sc.sb("fu_gm", [P, 2])
        rg = sc.sb("fu_rg", [P, 2])
        c = sc.sb("fu_c", [P, 1])
        bank = [sc.ps(f"fu_bank{i}", [P, S]) for i in range(4)]
        jobs = [("wdk", [(raw_d[:, :, :], A["wdk1"].rearrange("(k p) n -> p k n", p=P))],
                 raw_d[:, :, :], wd[0][:, :, :], wd[1][:, :, :]),
                ("wup", [(raw_u[:, :, :], A["wup1"].rearrange("(k p) n -> p k n", p=P))],
                 raw_u[:, :, :], wu[0][:, :, :], wu[1][:, :, :])]
        split_matrices(nc, sc, "fu", jobs, gm, rg)
        s_f = sc.sem("s_fu_filled")
        s_e = sc.sem("s_fu_out")
        s_c = sc.sem("s_fu_factor")
        s_o = sc.sem("s_fu_stored")
        tiles = [(m, n) for m in range(KT) for n in range(NU // S)]
        with nc.Block() as block:

            @block.tensor
            def _(pe):
                for i, (m, n) in enumerate(tiles):
                    if i >= 4:
                        pe.wait_ge(s_e, i - 3)
                    for k in range(KT):
                        for q, (a, r) in enumerate(((0, 0), (1, 0), (0, 1))):
                            last = pe.matmul(bank[i % 4][:, :], wd[a][:, k, m * P:(m + 1) * P],
                                             wu[r][:, k, n * S:(n + 1) * S],
                                             start=(k == 0 and q == 0), stop=(k == KT - 1 and q == 2))
                    last.then_inc(s_f, 1)

            @block.vector
            def _(dve):
                dve.tensor_tensor(c[:, :], gm[:, 0:1], gm[:, 1:2], ALU.mult).then_inc(s_c, 1)

            @block.scalar
            def _(act):
                act.wait_ge(s_c, 1)
                for i, (m, n) in enumerate(tiles):
                    act.wait_ge(s_f, i + 1)
                    act.activation(fused[:, m, n * S:(n + 1) * S], bank[i % 4][:, :], ACT.Copy,
                                   scale=c[:, 0:1]).then_inc(s_e, 1)

            @block.sync
            def _(sp):
                for m in range(KT):
                    sp.wait_ge(s_e, (m + 1) * NU // S)
                    sp.dma_start(fused_dram[m * P:(m + 1) * P, :], fused[:, m, :]).then_inc(s_o, 16)
                sp.wait_ge(s_o, 16 * KT)

        clear(nc, sc.sems)


def attention1(nc, A, C, xT, yacc, fused_dram):
    with ExitStack() as stack:
        sc = Scope(nc, stack)
        NH = B * HG
        raw_kv = sc.sb("raw_kv", [P, KT, WK])
        raw_q = sc.sb("raw_q", [P, KT, D])
        raw_o = sc.sb("raw_o", [P, HG, D])
        wkv = [sc.sb("wkv1_hi", [P, KT, WK], F16), sc.sb("wkv1_lo", [P, KT, WK], F16)]
        wq = [sc.sb("wq1_hi", [P, KT, D], F16), sc.sb("wq1_lo", [P, KT, D], F16)]
        wo = [sc.sb("wo1_hi", [P, HG, D], F16), sc.sb("wo1_lo", [P, HG, D], F16)]
        am = sc.sb("am1", [P, 3])
        gm = sc.sb("gm1", [P, 3])
        rg = sc.sb("rg1", [P, 3])
        cs = sc.sb("cs1", [P, 1])
        cy = sc.sb("cy1", [P, 1])
        rope = {n: sc.sb(n, [P, S]) for n in ("cosq", "sinq", "cosk", "sink")}
        mask = sc.sb("mask", [P, S])
        t1 = sc.sb("t1", [P, 2, S])
        t2 = sc.sb("t2", [P, 2, S])
        qf = sc.sb("qf", [P, 2, S])
        kT = [sc.sb("kT_hi", [P, S], F16), sc.sb("kT_lo", [P, S], F16)]
        v = [sc.sb("v_hi", [P, 2, TT, E1], F16), sc.sb("v_lo", [P, 2, TT, E1], F16)]
        qT = [sc.sb("q1T_hi", [P, 2, S], F16), sc.sb("q1T_lo", [P, 2, S], F16)]
        xp = sc.sb("xp1", [P, 3, TRIW])
        pT = [sc.sb("p1T_hi", [P, NBLK, HG, P], F16), sc.sb("p1T_lo", [P, NBLK, HG, P], F16)]
        oT = [sc.sb("o1T_hi", [P, TT, HG, P], F16), sc.sb("o1T_lo", [P, TT, HG, P], F16)]
        mx = sc.sb("mx1", [P, 3, TT])
        nm = sc.sb("nm1", [P, 3, TT])
        ls = sc.sb("ls1", [P, 3, TT])
        rl = sc.sb("rl1", [P, 3, TT])
        bank = [sc.ps(f"bank1_{i}", [P, S]) for i in range(8)]
        GKV, GQ, GO = range(3)

        def load_kv(g):
            f = fused_dram.rearrange("(k p) (g n) -> g p k n", p=P, n=UP)[g]
            r = A["wkr1"][g]
            return [(raw_kv[:, :, 0:32], r[:, :, 0:32]), (raw_kv[:, :, 64:96], r[:, :, 32:64]),
                    (raw_kv[:, :, 32:64], f[:, :, 0:32]), (raw_kv[:, :, 96:128], f[:, :, 32:64]),
                    (raw_kv[:, :, E1:WK], f[:, :, 64:UP])]

        s_c = sc.sem("s1_tables")
        with nc.Block() as block:

            @block.sync
            def _(sp):
                for n in rope:
                    sp.dma_start(rope[n][:, :], A[n]).then_inc(s_c, 16)
                sp.dma_start(mask[:, :], A["mask"]).then_inc(s_c, 16)
                sp.wait_ge(s_c, 16 * 5)

            @block.gpsimd
            def _(pool):
                pool.memset(yacc[:, :, :], 0.0)

        split_matrices(nc, sc, "w1", [
            ("kv", load_kv(0), raw_kv[:, :, :], wkv[0][:, :, :], wkv[1][:, :, :]),
            ("q", [(raw_q[:, :, :], A["wq1"][0])], raw_q[:, :, :], wq[0][:, :, :], wq[1][:, :, :])], gm, rg)

        s_dv = sc.sem("s1_dve_steps")
        s_am = sc.sem("s1_rowmax")
        s_gm = sc.sem("s1_globalmax")
        s_rg = sc.sem("s1_reciprocal")
        s_wh = sc.sem("s1_weights_hi")
        s_wl = sc.sem("s1_weights_lo")
        s_lo = sc.sem("s1_output_weights_loaded")
        s_ld = sc.sem("s1_next_weights_loaded")
        s_rf = sc.sem("s1_projection_filled")
        s_vh = sc.sem("s1_v_hi_out")
        s_rd = sc.sem("s1_projection_out")
        s_qf = sc.sem("s1_roped")
        s_qh = sc.sem("s1_roped_hi")
        s_ql = sc.sem("s1_roped_lo")
        s_sf = sc.sem("s1_scores_filled")
        s_sd = sc.sem("s1_scores_out")
        s_nm = sc.sem("s1_negmax")
        s_ex = sc.sem("s1_exp")
        s_rl = sc.sem("s1_sum_reciprocal")
        s_pn = sc.sem("s1_probs_normed")
        s_tf = sc.sem("s1_transpose_filled")
        s_th = sc.sem("s1_transpose_hi_out")
        s_tl = sc.sem("s1_transpose_lo_out")
        s_of = sc.sem("s1_output_filled")
        s_oh = sc.sem("s1_output_hi_out")
        s_od = sc.sem("s1_output_out")

        STEPS = NH + 6
        TILES = ((0, 1), (2,), (3,))

        def pv_batch(n):
            b = (n - 6) // HG
            return b if n >= 6 and (n - 6) % HG == 0 and b < B else None

        def projections(n):
            out = []
            for b in range(B):
                out += {0: [(b, 0), (b, 1)], 1: [(b, 2)], 2: [(b, 3)]}.get(n - (HG * b + 7), [])
            return out

        kinds = {"r": [], "s": [], "t": [], "o": []}
        fillings = []

        def plan(kind, what):
            fillings.append((kind, len(kinds[kind])))
            kinds[kind].append(what)

        for n in range(STEPS):
            if n < NH:
                if n % HG == 0:
                    plan("r", ("k", n // HG))
                    plan("r", ("v", n // HG))
                plan("r", ("q", n))
            if 1 <= n <= NH:
                for i in range(3):
                    plan("s", (n - 1, i))
            if pv_batch(n) is not None:
                for t in range(TT):
                    plan("o", ("pv", pv_batch(n), t))
            for b, t in projections(n):
                plan("o", ("wo", b, t))
            if 2 <= n <= NH + 1:
                for i in range(3):
                    plan("t", (n - 2, i))
        assert len(kinds["o"]) == 2 * B * TT
        place = {f: i for i, f in enumerate(fillings)}
        out_of = {"r": s_rd, "s": s_sd, "t": s_tl, "o": s_od}
        no = {kind: {u: i for i, u in enumerate(us)} for kind, us in kinds.items()}
        ropes = [u for u in kinds["r"] if u[0] != "v"]
        rope_no = {u: i for i, u in enumerate(ropes)}

        def bank_of(kind, u):
            return bank[place[(kind, no[kind][u])] % 8]

        def blocks(js):
            return slice(COL[js[0]], COL[js[-1]] + TT - js[-1])

        def flat(ap):
            return ap.rearrange("p a b -> p (a b)")

        raws = {GKV: raw_kv, GQ: raw_q, GO: raw_o}
        splits = {GKV: wkv, GQ: wq, GO: wo}
        ORDER = (GO, GKV, GQ)

        with nc.Fori(0, G1) as g:
            with nc.Block() as block:

                @block.sync
                def _(sp):
                    nxt = (g + 1) % G1
                    sp.dma_start(raw_o[:, :, :], A["wo1"][g]).then_inc(s_lo, 16)
                    for n in load_kv(nxt):
                        sp.dma_start(*n).then_inc(s_ld, 16)
                    sp.dma_start(raw_q[:, :, :], A["wq1"][nxt]).then_inc(s_ld, 16)
                    sp.wait_ge(s_lo, 16)
                    sp.wait_ge(s_ld, 16 * 6)

                @block.gpsimd
                def _(pool):
                    def global_max(k):
                        i = ORDER[k]
                        pool.wait_ge(s_am, k + 1)
                        pool.partition_all_reduce(gm[:, i:i + 1], am[:, i:i + 1], P, RMAX).then_inc(s_gm, 1)

                    for i, u in enumerate(ropes):
                        pool.wait_ge(s_rd, no["r"][u] + 1)
                        if i >= 2:
                            pool.wait_ge(s_ql, i - 1)
                        pool.tensor_tensor(qf[:, i % 2, :], t1[:, i % 2, :], t2[:, i % 2, :],
                                           ALU.add).then_inc(s_qf, 1)
                        if u == ("q", 2):
                            global_max(0)
                        if u == ("q", 14):
                            global_max(1)
                    global_max(2)

                @block.tensor
                def _(pe):
                    def triple(out, lhs, rhs, first, last):
                        for i, (a, c) in enumerate(((0, 0), (1, 0), (0, 1))):
                            ins = pe.matmul(out, lhs(a), rhs(c), start=(first and i == 0),
                                            stop=(last and i == 2))
                        return ins

                    def take(kind, u):
                        i = place[(kind, no[kind][u])]
                        if i >= 8:
                            k, c = fillings[i - 8]
                            pe.wait_ge(out_of[k], c + 1)
                        return bank[i % 8]

                    def project(u, w, col, b):
                        out = take("r", u)
                        for k in range(KT):
                            ins = triple(out[:, :], lambda a: w[a][:, k, col:col + P],
                                         lambda c: xT[c][:, k, b * S:(b + 1) * S], k == 0, k == KT - 1)
                        ins.then_inc(s_rf, 1)

                    def values(b):
                        out = take("r", ("v", b))
                        for t in range(TT):
                            for k in range(KT):
                                ins = triple(out[:, t * P:(t + 1) * P],
                                             lambda a: xT[a][:, k, b * S + t * P:b * S + (t + 1) * P],
                                             lambda c: wkv[c][:, k, E1:WK], k == 0, k == KT - 1)
                        ins.then_inc(s_rf, 1)

                    def scores(n):
                        pe.wait_ge(s_ql, rope_no[("q", n)] + 1)
                        for i, tiles in enumerate(TILES):
                            out, col = take("s", (n, i)), 0
                            for t in tiles:
                                w = P * (t + 1)
                                ins = triple(out[:, col:col + w], lambda a: qT[a][:, n % 2, t * P:(t + 1) * P],
                                             lambda c: kT[c][:, 0:w], True, True)
                                col += w
                            ins.then_inc(s_sf, 1)

                    def transpose_probs(n):
                        pe.wait_ge(s_pn, n + 1)
                        for i, js in enumerate(((0,), (1,), (2, 3))):
                            out, col = take("t", (n, i)), 0
                            for j in js:
                                for t in range(j, TT):
                                    ins = pe.transpose(out[:, col:col + P],
                                                       xp[:, n % 3, TRI[t] + j * P:TRI[t] + (j + 1) * P],
                                                       C["ident"][:, :])
                                    col += P
                            ins.then_inc(s_tf, 1)

                    def weigh_values(b):
                        pe.wait_ge(s_tl, 3 * HG * (b + 1))
                        for t in range(TT):
                            out = take("o", ("pv", b, t))
                            for j in range(t + 1):
                                ins = triple(out[:, :], lambda a: v[a][:, b % 2, j, :],
                                             lambda c: flat(pT[c][:, COL[j] + t - j, :, :]), j == 0, j == t)
                            ins.then_inc(s_of, 1)

                    def project_out(b, t):
                        pe.wait_ge(s_od, no["o"][("pv", b, t)] + 1)
                        if (b, t) == (0, 0):
                            pe.wait_ge(s_wl, 1)
                        out = take("o", ("wo", b, t))
                        for h in range(HG):
                            ins = triple(out[:, :], lambda a: oT[a][:, t, h, :],
                                         lambda c: wo[c][:, h, :], h == 0, h == HG - 1)
                        ins.then_inc(s_of, 1)

                    for n in range(STEPS):
                        if n < NH:
                            b = n // HG
                            if n % HG == 0:
                                project(("k", b), wkv, 0, b)
                                values(b)
                            project(("q", n), wq, (n % HG) * P, b)
                        if 1 <= n <= NH:
                            scores(n - 1)
                        if pv_batch(n) is not None:
                            weigh_values(pv_batch(n))
                        for b, t in projections(n):
                            project_out(b, t)
                        if 2 <= n <= NH + 1:
                            transpose_probs(n - 2)

                @block.scalar
                def _(act):
                    def weights_hi(k):
                        i = ORDER[k]
                        act.wait_ge(s_rg, k + 1)
                        act.activation(flat(splits[i][0][:, :, :]), flat(raws[i][:, :, :]), ACT.Copy,
                                       scale=rg[:, i:i + 1]).then_inc(s_wh, 1)

                    def roped_hi(u):
                        i = rope_no[u]
                        act.wait_ge(s_qf, i + 1)
                        if u[0] == "k":
                            if u[1] >= 1:
                                act.wait_ge(s_sf, 3 * HG * u[1])
                            dst = kT[0][:, :]
                        else:
                            if u[1] >= 2:
                                act.wait_ge(s_sf, 3 * (u[1] - 1))
                            dst = qT[0][:, u[1] % 2, :]
                        act.activation(dst, qf[:, i % 2, :], ACT.Copy).then_inc(s_qh, 1)

                    for n in range(STEPS):
                        if 3 <= n <= NH + 2:
                            m = n - 3
                            for i, js in enumerate(((0,), (1,), (2, 3))):
                                dst = pT[0][:, blocks(js), m % HG, :]
                                act.wait_ge(s_tf, 3 * m + i + 1)
                                act.activation(dst, bank_of("t", (m, i))[:, 0:P * dst.shape[1]].rearrange(
                                    "p (t c) -> p t c", c=P), ACT.Copy).then_inc(s_th, 1)
                        if 2 <= n <= NH + 1:
                            m = n - 2
                            act.wait_ge(s_rl, m + 1)
                            for t in range(TT):
                                x = xp[:, m % 3, TRI[t]:TRI[t] + P * (t + 1)]
                                ins = act.activation(x, x, ACT.Copy, scale=rl[:, m % 3, t:t + 1])
                            ins.then_inc(s_pn, 1)
                        if n < NH and n % HG == 0:
                            b = n // HG
                            act.wait_ge(s_rf, no["r"][("v", b)] + 1)
                            if b >= 2:
                                act.wait_ge(s_of, no["o"][("pv", b - 2, TT - 1)] + 1)
                            act.activation(flat(v[0][:, b % 2, :, :]), bank_of("r", ("v", b))[:, :],
                                           ACT.Copy).then_inc(s_vh, 1)
                        if 1 <= n <= NH:
                            m = n - 1
                            act.wait_ge(s_nm, m + 1)
                            for t in range(TT):
                                x = xp[:, m % 3, TRI[t]:TRI[t] + P * (t + 1)]
                                ins = act.activation(x, x, ACT.Exp, bias=nm[:, m % 3, t:t + 1],
                                                     accum_out=ls[:, m % 3, t:t + 1])
                            ins.then_inc(s_ex, 1)
                        if n < NH:
                            if n % HG == 0:
                                roped_hi(("k", n // HG))
                            roped_hi(("q", n))
                        if pv_batch(n) is not None:
                            for t in range(TT):
                                u = ("pv", pv_batch(n), t)
                                act.wait_ge(s_of, no["o"][u] + 1)
                                act.activation(flat(oT[0][:, t, :, :]), bank_of("o", u)[:, :],
                                               ACT.Copy).then_inc(s_oh, 1)
                        if n == 3:
                            weights_hi(0)
                        if n == NH - 1:
                            weights_hi(1)
                    weights_hi(2)

                @block.vector
                def _(dve):
                    ch = Chain(dve, s_dv)

                    def row_max(k):
                        i = ORDER[k]
                        dve.tensor_reduce(am[:, i:i + 1], flat(raws[i][:, :, :]), AX.X, ALU.max,
                                          apply_absolute_value=True).then_inc(s_am, 1)

                    def reciprocal(k):
                        i = ORDER[k]
                        dve.wait_ge(s_gm, k + 1)
                        ch.tick(dve.tensor_scalar(gm[:, i:i + 1], gm[:, i:i + 1], TINY, None, ALU.max))
                        ch.settle()
                        dve.reciprocal(rg[:, i:i + 1], gm[:, i:i + 1]).then_inc(s_rg, 1)
                        dve.wait_ge(s_rg, k + 1)

                    def weights_lo(k):
                        i = ORDER[k]
                        dve.wait_ge(s_wh, k + 1)
                        dve.scalar_tensor_tensor(flat(splits[i][1][:, :, :]), flat(raws[i][:, :, :]),
                                                 rg[:, i:i + 1], flat(splits[i][0][:, :, :]), ALU.mult,
                                                 ALU.subtract).then_inc(s_wl, 1)

                    def rotate(u):
                        i = rope_no[u]
                        cos, sin = (rope["cosk"], rope["sink"]) if u[0] == "k" else (rope["cosq"], rope["sinq"])
                        q = bank_of("r", u)
                        dve.wait_ge(s_rf, no["r"][u] + 1)
                        if i >= 2:
                            dve.wait_ge(s_qf, i - 1)
                        dve.tensor_tensor(t1[0:64, i % 2, :], q[64:128, :], sin[0:64, :], ALU.mult)
                        dve.tensor_tensor(t1[64:128, i % 2, :], q[0:64, :], sin[64:128, :], ALU.mult)
                        dve.tensor_tensor(t2[:, i % 2, :], q[:, :], cos[:, :], ALU.mult).then_inc(s_rd, 1)

                    def roped_lo(u):
                        i = rope_no[u]
                        hi, lo = (x[:, :] for x in kT) if u[0] == "k" else (x[:, u[1] % 2, :] for x in qT)
                        dve.wait_ge(s_qh, i + 1)
                        dve.tensor_tensor(lo, qf[:, i % 2, :], hi, ALU.subtract).then_inc(s_ql, 1)

                    ch.tick(dve.tensor_scalar(cs[:, :], gm[:, GQ:GQ + 1], gm[:, GKV:GKV + 1], E1 ** -0.5,
                                              ALU.mult, ALU.mult))
                    ch.settle()
                    for n in range(STEPS):
                        if 3 <= n <= NH + 2:
                            m = n - 3
                            for i, js in enumerate(((0,), (1,), (2, 3))):
                                hi = pT[0][:, blocks(js), m % HG, :]
                                dve.wait_ge(s_th, 3 * m + i + 1)
                                dve.tensor_tensor(pT[1][:, blocks(js), m % HG, :],
                                                  bank_of("t", (m, i))[:, 0:P * hi.shape[1]].rearrange(
                                                      "p (t c) -> p t c", c=P), hi,
                                                  ALU.subtract).then_inc(s_tl, 1)
                        if n < NH:
                            b = n // HG
                            if n % HG == 0:
                                rotate(("k", b))
                                dve.wait_ge(s_vh, b + 1)
                                dve.tensor_tensor(flat(v[1][:, b % 2, :, :]), bank_of("r", ("v", b))[:, :],
                                                  flat(v[0][:, b % 2, :, :]), ALU.subtract).then_inc(s_rd, 1)
                            rotate(("q", n))
                        if 1 <= n <= NH:
                            m = n - 1
                            if m >= 3:
                                dve.wait_ge(s_tf, 3 * (m - 2))
                            for i, tiles in enumerate(TILES):
                                col = 0
                                dve.wait_ge(s_sf, 3 * m + i + 1)
                                for t in tiles:
                                    w = P * (t + 1)
                                    ins = dve.tensor_tensor_reduce(
                                        out=xp[:, m % 3, TRI[t]:TRI[t] + w],
                                        in0=bank_of("s", (m, i))[:, col:col + w],
                                        in1=mask[:, S - w:S], scale=cs[:, 0:1], scalar=-3e38,
                                        op0=ALU.add, op1=ALU.max, accum_out=mx[:, m % 3, t:t + 1])
                                    col += w
                                ins.then_inc(s_sd, 1)
                            dve.wait_ge(s_sd, 3 * (m + 1))
                            dve.tensor_scalar(nm[:, m % 3, :], mx[:, m % 3, :], -1.0, None,
                                              ALU.mult).then_inc(s_nm, 1)
                        if pv_batch(n) is not None:
                            for t in range(TT):
                                u = ("pv", pv_batch(n), t)
                                dve.wait_ge(s_oh, TT * pv_batch(n) + t + 1)
                                dve.tensor_tensor(flat(oT[1][:, t, :, :]), bank_of("o", u)[:, :],
                                                  flat(oT[0][:, t, :, :]), ALU.subtract).then_inc(s_od, 1)
                        for b, t in projections(n):
                            u = ("wo", b, t)
                            dve.wait_ge(s_of, no["o"][u] + 1)
                            y = yacc[:, TT * b + t, :]
                            dve.scalar_tensor_tensor(y, bank_of("o", u)[:, :], cy[:, 0:1], y, ALU.mult,
                                                     ALU.add).then_inc(s_od, 1)
                        if n < NH:
                            if n % HG == 0:
                                roped_lo(("k", n // HG))
                            roped_lo(("q", n))
                        if 1 <= n <= NH:
                            m = n - 1
                            dve.wait_ge(s_ex, m + 1)
                            dve.reciprocal(rl[:, m % 3, :], ls[:, m % 3, :]).then_inc(s_rl, 1)
                        if n == 2:
                            dve.wait_ge(s_lo, 16)
                            row_max(0)
                        if n == 3:
                            reciprocal(0)
                            ch.tick(dve.tensor_scalar(cy[:, :], gm[:, GKV:GKV + 1], gm[:, GO:GO + 1], None,
                                                      ALU.mult))
                            weights_lo(0)
                            ch.settle()
                        if n == NH - 2:
                            dve.wait_ge(s_ld, 16 * 6)
                            row_max(1)
                        if n == NH - 1:
                            reciprocal(1)
                            weights_lo(1)
                        if n == NH:
                            row_max(2)
                        if n == NH + 1:
                            reciprocal(2)
                    weights_lo(2)

            clear(nc, sc.sems)


def feed_forward1(nc, A, C, yacc, x2_dram, out):
    with ExitStack() as stack:
        sc = Scope(nc, stack)
        tg = sc.sb("tern_gate", [P, KT, HID], F16)
        tu = sc.sb("tern_up", [P, KT, HID], F16)
        td = sc.sb("tern_down", [P, HT, D], F16)
        scale = sc.sb("tern_scale", [P, 3])
        kup = sc.sb("kup", [P, 1])
        cdn = sc.sb("cdn", [P, 1])
        GATE, UPW, DOWN = range(3)

        with ExitStack() as inner:
            si = Scope(nc, inner)
            raws = [si.sb("raw_gate", [P, KT, HID]), si.sb("raw_up", [P, KT, HID]),
                    si.sb("raw_down", [P, HT, D])]
            pos = si.sb("pos", [P, HT * D], F16)
            sgn = [si.sb("sgn_in", [P, KT, 8], F16), si.sb("sgn_dn", [P, HT, 8], F16)]
            part = si.sb("part", [P, HT * 8])
            am = si.sb("am2", [P, 3])
            half = si.sb("half", [P, 3])
            nhalf = si.sb("nhalf", [P, 3])
            s_zero = si.sem("s_tail_zeroed")
            s_ld = [si.sem(f"s_tern_loaded{i}") for i in range(3)]
            s_am = si.sem("s_abs_sums")
            s_gm = si.sem("s_total_sums")
            s_dv = si.sem("s_tern_steps")
            tern = [tg, tu, td]
            with nc.Block() as block:

                @block.sync
                def _(sp):
                    for i, n in ((0, "w_gate"), (1, "w_up")):
                        sp.dma_start(raws[i][:, :, :], A[n].rearrange("(k p) n -> p k n", p=P)).then_inc(s_ld[i], 16)
                    full = (HT - 1) * P
                    sp.dma_start(raws[2][:, 0:HT - 1, :],
                                 A["w_down"][0:full, :].rearrange("(k p) n -> p k n", p=P)).then_inc(s_ld[2], 16)
                    sp.dma_start(sgn[0][:, :, :], A["sgn_in"]).then_inc(s_ld[0], 16)
                    sp.dma_start(sgn[1][:, :, :], A["sgn_dn"]).then_inc(s_ld[2], 16)
                    sp.wait_ge(s_zero, 1)
                    sp.dma_start(raws[2][0:HID - full, HT - 1, :], A["w_down"][full:HID, :]).then_inc(s_ld[2], 16)

                @block.gpsimd
                def _(pool):
                    pool.memset(raws[2][:, HT - 1, :], 0.0).then_inc(s_zero, 1)
                    for i in range(3):
                        pool.wait_ge(s_am, i + 1)
                        pool.partition_all_reduce(scale[:, i:i + 1], am[:, i:i + 1], P, RADD).then_inc(s_gm, 1)

                @block.vector
                def _(dve):
                    ch = Chain(dve, s_dv)
                    for i, n in enumerate((KT, KT, HT)):
                        dve.wait_ge(s_ld[i], (32, 16, 48)[i])
                        ch.tick(dve.tensor_reduce(part[:, 0:8 * n], raws[i][:, :, :].rearrange(
                            "p k (c o) -> p (k c) o", c=8), AX.X, ALU.add, apply_absolute_value=True))
                        ch.settle()
                        dve.tensor_reduce(am[:, i:i + 1], part[:, 0:8 * n], AX.X, ALU.add).then_inc(s_am, 1)
                        dve.wait_ge(s_am, i + 1)
                    dve.wait_ge(s_gm, 3)
                    ch.tick(dve.tensor_scalar(scale[:, :], scale[:, :], 1.0 / (D * HID), None, ALU.mult))
                    ch.settle()
                    ch.tick(dve.tensor_scalar(half[:, :], scale[:, :], 0.5, None, ALU.mult))
                    ch.tick(dve.tensor_scalar(nhalf[:, :], scale[:, :], -0.5, None, ALU.mult))
                    ch.tick(dve.tensor_scalar(kup[:, :], scale[:, GATE:GATE + 1], 16.0, TINY, ALU.mult, ALU.max))
                    ch.settle()
                    ch.tick(dve.tensor_tensor(cdn[:, :], kup[:, :], scale[:, UPW:UPW + 1], ALU.mult))
                    ch.settle()
                    ch.tick(dve.reciprocal(kup[:, :], kup[:, :]))
                    ch.tick(dve.tensor_tensor(cdn[:, :], cdn[:, :], scale[:, DOWN:DOWN + 1], ALU.mult))
                    for i, n in enumerate((KT, KT, HT)):
                        w = raws[i][:, :, :].rearrange("p k n -> p (k n)")
                        size = n * (HID if i < 2 else D)
                        t = tern[i][:, :, :].rearrange("p k n -> p (k n)")
                        ch.settle()
                        ch.tick(dve.tensor_scalar(pos[:, 0:size], w, half[:, i:i + 1], None, ALU.is_gt))
                        ch.settle()
                        ch.tick(dve.scalar_tensor_tensor(t, w, nhalf[:, i:i + 1], pos[:, 0:size], ALU.is_lt,
                                                         ALU.subtract))
                        ch.settle()
                        for k in range(n):
                            x = tern[i][:, k, :].rearrange("p (c o) -> p c o", c=8)
                            o = OH if i < 2 else OD
                            ch.tick(dve.tensor_tensor(
                                x, x, sgn[i // 2][:, k, :].unsqueeze(2).to_broadcast([P, 8, o]), ALU.mult))
                    ch.settle()

            clear(nc, si.sems)

        xb = sc.sb("xb2", [P, TT, D])
        yb = sc.sb("yb2", [P, TT, D])
        aT = [sc.sb("a2T_hi", [P, KT, S], F16), sc.sb("a2T_lo", [P, KT, S], F16)]
        sl = sc.sb("silu_gate", [P, 2, S])
        hf = sc.sb("hidden", [P, 2, S])
        hT = [sc.sb("hidden_hi", [P, HT, S], F16), sc.sb("hidden_lo", [P, HT, S], F16)]
        st = sc.sb("st2", [P, TT, 6])
        mv = sc.sb("mv2", [P, TT, 2])
        ve = sc.sb("ve2", [P, TT])
        rs = sc.sb("rs2", [P, TT])
        bank_g = [sc.ps(f"bank_g{i}", [P, S]) for i in range(2)]
        bank_u = [sc.ps(f"bank_u{i}", [P, S]) for i in range(2)]
        bank_t = [sc.ps(f"bank2_t{i}", [P, S]) for i in range(2)]
        bank_y = [sc.ps(f"bank_y{i}", [P, S]) for i in range(2)]

        s_x = sc.sem("s2_x_loaded")
        s_dv = sc.sem("s2_dve_steps")
        s_ve = sc.sem("s2_variance")
        s_rs = sc.sem("s2_rstd")
        s_xn = sc.sem("s2_normed_rows")
        s_tf = sc.sem("s2_t_filled")
        s_th = sc.sem("s2_t_hi_out")
        s_tl = sc.sem("s2_t_lo_out")
        s_gf = sc.sem("s2_gate_filled")
        s_uf = sc.sem("s2_up_filled")
        s_sl = sc.sem("s2_silu")
        s_hf = sc.sem("s2_hidden")
        s_hh = sc.sem("s2_hidden_hi")
        s_hl = sc.sem("s2_hidden_lo")
        s_yf = sc.sem("s2_y_filled")
        s_yd = sc.sem("s2_y_out")
        s_fin = sc.sem("s2_final")
        s_out = sc.sem("s2_stored")

        def width(m):
            return min(P, HID - m * P)

        with nc.Fori(0, B) as b:
            with nc.Block() as block:

                @block.sync
                def _(sp):
                    sp.dma_start(xb[:, :, :], x2_dram[b].rearrange("(t p) d -> p t d", p=P)).then_inc(s_x, 16)
                    sp.wait_ge(s_fin, TT)
                    sp.dma_start(out[b].rearrange("(t p) d -> p t d", p=P), xb[:, :, :]).then_inc(s_out, 16)
                    sp.wait_ge(s_out, 16)

                @block.gpsimd
                def _(pool):
                    for n in range(3):
                        pool.wait_ge(s_ve, n + 1)
                        pool.tensor_tensor(rs[:, :], ve[:, :], C["mhalf"][:, 0:TT], ALU.pow).then_inc(s_rs, 1)

                @block.tensor
                def _(pe):
                    for t in range(TT):
                        pe.wait_ge(s_xn, t + 1)
                        if t >= 2:
                            pe.wait_ge(s_tl, t - 1)
                        for k in range(KT):
                            last = pe.transpose(bank_t[t % 2][:, k * P:(k + 1) * P], yb[:, t, k * P:(k + 1) * P],
                                                C["ident"][:, :])
                        last.then_inc(s_tf, 1)
                    pe.wait_ge(s_tl, TT)
                    for m in range(HT):
                        w = width(m)
                        for bank, tern, filled in ((bank_g, tg, s_gf), (bank_u, tu, s_uf)):
                            if m >= 2:
                                pe.wait_ge(s_hf, m - 1)
                            for k in range(KT):
                                for c in range(2):
                                    last = pe.matmul(bank[m % 2][0:w, :], tern[:, k, m * P:m * P + w],
                                                     aT[c][:, k, :], start=(k == 0 and c == 0),
                                                     stop=(k == KT - 1 and c == 1))
                            last.then_inc(filled, 1)
                    pe.wait_ge(s_hl, HT)
                    for t in range(TT):
                        if t >= 2:
                            pe.wait_ge(s_yd, t - 1)
                        for m in range(HT):
                            w = width(m)
                            for c in range(2):
                                last = pe.matmul(bank_y[t % 2][:, :], hT[c][0:w, m, t * P:(t + 1) * P],
                                                 td[0:w, m, :], start=(m == 0 and c == 0),
                                                 stop=(m == HT - 1 and c == 1))
                        last.then_inc(s_yf, 1)

                @block.scalar
                def _(act):
                    for t in range(TT):
                        act.wait_ge(s_tf, t + 1)
                        act.activation(aT[0][:, :, t * P:(t + 1) * P],
                                       bank_t[t % 2][:, :].rearrange("p (k c) -> p k c", c=P),
                                       ACT.Copy).then_inc(s_th, 1)
                    for m in range(HT + 1):
                        if m < HT:
                            w = width(m)
                            act.wait_ge(s_gf, m + 1)
                            act.activation(sl[0:w, m % 2, :], bank_g[m % 2][0:w, :], ACT.Silu,
                                           scale=scale[0:w, GATE:GATE + 1]).then_inc(s_sl, 1)
                        if m >= 1:
                            w = width(m - 1)
                            act.wait_ge(s_hf, m)
                            act.activation(hT[0][0:w, m - 1, :], hf[0:w, (m - 1) % 2, :],
                                           ACT.Copy).then_inc(s_hh, 1)

                @block.vector
                def _(dve):
                    ch = Chain(dve, s_dv)
                    count = {"rs": 0}

                    def statistics(src):
                        for t in range(TT):
                            ch.tick(dve.bn_stats(st[:, t, :], src(t)))
                        ch.settle()
                        for t in range(TT):
                            ch.tick(dve.bn_aggr(mv[:, t, :], st[:, t, :]))
                        ch.settle()
                        dve.tensor_scalar(ve[:, :], mv[:, :, 1], EPS, None, ALU.add).then_inc(s_ve, 1)
                        count["rs"] += 1
                        dve.wait_ge(s_rs, count["rs"])

                    def add_normed(src, done=None):
                        statistics(src)
                        for t in range(TT):
                            ch.tick(dve.tensor_scalar(yb[:, t, :], src(t), mv[:, t, 0:1], rs[:, t:t + 1],
                                                      ALU.subtract, ALU.mult))
                        ch.settle()
                        for t in range(TT):
                            ins = dve.tensor_tensor(xb[:, t, :], xb[:, t, :], yb[:, t, :], ALU.add)
                            if done is None:
                                ch.tick(ins)
                            else:
                                ins.then_inc(done, 1)
                        ch.settle()

                    dve.wait_ge(s_x, 16)
                    add_normed(lambda t: yacc[:, bass.ds(b * TT + t, 1), :].rearrange("p a n -> p (a n)"))
                    statistics(lambda t: xb[:, t, :])
                    for t in range(TT):
                        dve.tensor_scalar(yb[:, t, :], xb[:, t, :], mv[:, t, 0:1], rs[:, t:t + 1],
                                          ALU.subtract, ALU.mult).then_inc(s_xn, 1)
                    for t in range(TT):
                        dve.wait_ge(s_th, t + 1)
                        dve.tensor_tensor(aT[1][:, :, t * P:(t + 1) * P],
                                          bank_t[t % 2][:, :].rearrange("p (k c) -> p k c", c=P),
                                          aT[0][:, :, t * P:(t + 1) * P], ALU.subtract).then_inc(s_tl, 1)
                    for m in range(HT + 1):
                        if m < HT:
                            w = width(m)
                            dve.wait_ge(s_uf, m + 1)
                            dve.wait_ge(s_sl, m + 1)
                            if m >= 2:
                                dve.wait_ge(s_hh, m - 1)
                                dve.wait_ge(s_hl, m - 1)
                            dve.scalar_tensor_tensor(hf[0:w, m % 2, :], bank_u[m % 2][0:w, :], kup[0:w, 0:1],
                                                     sl[0:w, m % 2, :], ALU.mult, ALU.mult).then_inc(s_hf, 1)
                        if m >= 1:
                            w = width(m - 1)
                            dve.wait_ge(s_hf, m)
                            dve.wait_ge(s_hh, m)
                            dve.tensor_tensor(hT[1][0:w, m - 1, :], hf[0:w, (m - 1) % 2, :],
                                              hT[0][0:w, m - 1, :], ALU.subtract).then_inc(s_hl, 1)
                    for t in range(TT):
                        dve.wait_ge(s_yf, t + 1)
                        dve.tensor_scalar(yb[:, t, :], bank_y[t % 2][:, :], cdn[:, 0:1], None,
                                          ALU.mult).then_inc(s_yd, 1)
                    dve.wait_ge(s_yd, TT)
                    add_normed(lambda t: yb[:, t, :], s_fin)

            clear(nc, sc.sems)


def build(nc, A, out, stages=4):
    x2_dram = nc.dram_tensor("x2_scratch", [B, S, D], F32).ap()
    fused_dram = nc.dram_tensor("fused_scratch", [D, G1 * UP], F32).ap()
    with ExitStack() as stack:
        sc = Scope(nc, stack)
        C = {"ident": sc.sb("ident", [P, P]), "mhalf": sc.sb("mhalf", [P, 8])}
        xT = [sc.sb("xT_hi", [P, KT, B * S], F16), sc.sb("xT_lo", [P, KT, B * S], F16)]
        with ExitStack() as first:
            s0 = Scope(nc, first)
            for n, shape, dt in (("rel", [P, S], F32), ("sel", [P, 8, P], F16), ("pairmask", [P, 2], F32),
                                 ("bias", [P, D], F32)):
                C[n] = s0.sb(n, shape, dt)
            W0 = {n: [s0.sb(f"{n}_hi", [P, KT, w], F16), s0.sb(f"{n}_lo", [P, KT, w], F16)]
                  for n, w in (("wq", D), ("wkv", P + E0), ("wo", D), ("wf", D))}
            W0["gm"] = s0.sb("gm0", [P, 4])
            with ExitStack() as second:
                ss = Scope(nc, second)
                raw = {n: ss.sb(f"raw_{n}", [P, KT, w], F32)
                       for n, w in (("wq", D), ("wkv", P + E0), ("wo", D), ("wf", D))}
                codes = ss.sb("codes", [P, KT, D], I32)
                qsc = ss.sb("qscales", [P, KT, D])
                rg = ss.sb("rg0", [P, 4])
                s_c = ss.sem("s_constants_loaded")
                with nc.Block() as block:

                    @block.sync
                    def _(sp):
                        for n in ("ident", "rel", "pairmask"):
                            sp.dma_start(C[n][:, :], A[n]).then_inc(s_c, 16)
                        sp.dma_start(C["sel"][:, :, :], A["sel"]).then_inc(s_c, 16)
                        sp.dma_start(C["bias"][:, :], A["bias"].partition_broadcast(P)).then_inc(s_c, 16)
                        sp.wait_ge(s_c, 16 * 5)

                    @block.gpsimd
                    def _(pool):
                        pool.memset(C["mhalf"][:, :], -0.5)

                def km(ap):
                    return ap.rearrange("(k p) n -> p k n", p=P)

                jobs = []
                for n, loads in (("wq", [(raw["wq"][:, :, :], km(A["wq0"]))]),
                                 ("wkv", [(raw["wkv"][:, :, 0:P], km(A["wk0"])),
                                          (raw["wkv"][:, :, P:P + E0], km(A["wv0"]))]),
                                 ("wo", [(raw["wo"][:, :, :], km(A["wo0"]))]),
                                 ("wf", [(codes[:, :, :], km(A["codes"])), (qsc[:, :, :], km(A["qscales"]))])):
                    job = [n, loads, raw[n][:, :, :], W0[n][0][:, :, :], W0[n][1][:, :, :]]
                    if n == "wf":
                        job.append((codes[:, :, :], qsc[:, :, :]))
                    jobs.append(job)
                split_matrices(nc, ss, "w0", jobs, W0["gm"], rg)
                clear(nc, ss.sems)
            layer0(nc, A, W0, C, xT, x2_dram)
        if stages < 2:
            return
        fuse_up_projections(nc, A, C, fused_dram, None)
        yacc = sc.sb("yacc", [P, B * TT, D])
        attention1(nc, A, C, xT, yacc, fused_dram)
        if stages < 3:
            return
        feed_forward1(nc, A, C, yacc, x2_dram, out)


def octonion_table():
    table = np.zeros((8, 8, 8), np.float32)
    table[0, 0, 0] = 1.0
    for i in range(1, 8):
        table[0, i, i] = table[i, 0, i] = 1.0
        table[i, i, 0] = -1.0
    for a, b, c in [(1, 2, 3), (1, 4, 5), (1, 7, 6), (2, 4, 6), (2, 5, 7), (3, 4, 7), (3, 6, 5)]:
        for x, y, z in ((a, b, c), (b, c, a), (c, a, b)):
            table[x, y, z] = 1.0
            table[y, x, z] = -1.0
    return np.abs(table).argmax(0), table.sum(0)


def constants():
    out = {"ident": np.eye(P, dtype=np.float32)}
    rel = (np.arange(S)[None, :] - (S - P) - np.arange(P)[:, None]).astype(np.float32)
    out["rel"] = np.where(rel <= 0, rel, np.float32(MASKED)).astype(np.float32)
    out["mask"] = np.where(rel <= 0, 0.0, MASKED).astype(np.float32)
    sel = np.zeros((P, 4, 2, P), np.float16)
    for r in range(4):
        for x in range(32):
            sel[32 * r + x, r, 0, [x, 64 + x]] = 1
            sel[32 * r + x, r, 1, [32 + x, 96 + x]] = 1
    out["sel"] = sel.reshape(P, 8, P)
    low = (np.arange(P) % 32 < 16).astype(np.float32)
    out["pairmask"] = np.stack([low, 1 - low], 1)
    inv_freq = 1.0 / 10000.0 ** (np.arange(0, E1, 2, dtype=np.float32) / E1)
    freqs = np.outer(np.arange(S, dtype=np.float32), inv_freq)
    emb = np.concatenate([freqs, freqs], -1).T
    cos, sin = np.cos(emb).astype(np.float32), np.sin(emb).astype(np.float32)
    sin[:E1 // 2] *= -1
    roped = (np.arange(E1) % (E1 // 2) < 32)[:, None]
    out["cosq"], out["sinq"] = cos, sin
    out["cosk"] = np.where(roped, cos, 1.0).astype(np.float32)
    out["sink"] = np.where(roped, sin, 0.0).astype(np.float32)
    sign = octonion_table()[1]
    rows = np.arange(D).reshape(KT, P) // OD
    out["sgn_in"] = np.ascontiguousarray(-sign[rows].transpose(1, 0, 2)).astype(np.float16)
    rows = np.minimum(np.arange(HT * P), HID - 1).reshape(HT, P) // OH
    out["sgn_dn"] = np.ascontiguousarray(-sign[rows].transpose(1, 0, 2)).astype(np.float16)
    return out


def lay_out(inputs):
    a = {k: np.asarray(v) for k, v in inputs.items()}
    unit = octonion_table()[0]
    i = np.arange(8)[:, None]
    k = np.arange(8)[None, :]
    wkv = a["L0_attn_Wkv"]
    out = {
        "x": a["L0_attn_hidden_states"],
        "wq0": a["L0_attn_Wq"],
        "wk0": np.tile(wkv[:, :E0], (1, P // E0)),
        "wv0": wkv[:, E0:],
        "wo0": a["L0_attn_Wo"],
        "codes": a["L0_ffn_q_vals"].reshape(D, D).T,
        "qscales": np.repeat(a["L0_ffn_q_scales"].T, 32, axis=0),
        "bias": a["L0_ffn_bias"],
        "wq1": a["L1_attn_Wq"].reshape(G1, HG * E1, KT, P).transpose(0, 3, 2, 1),
        "wkr1": a["L1_attn_Wkr"].reshape(G1, 64, KT, P).transpose(0, 3, 2, 1),
        "wdk1": a["L1_attn_Wdk"],
        "wup1": np.concatenate([a["L1_attn_Wupk"].reshape(G1, 64, D), a["L1_attn_Wupv"].reshape(G1, E1, D)],
                               1).reshape(G1 * UP, D).T,
        "wo1": a["L1_attn_Wo"].reshape(D, G1, HG, E1).transpose(1, 3, 2, 0),
        "w_gate": a["L1_ffn_w_gate"][unit[i, k]].transpose(0, 3, 1, 2).reshape(D, HID),
        "w_up": a["L1_ffn_w_up"][unit[i, k]].transpose(0, 3, 1, 2).reshape(D, HID),
        "w_down": a["L1_ffn_w_down"][unit[i, k]].transpose(0, 3, 1, 2).reshape(HID, D),
    }
    out.update(constants())
    return {n: np.ascontiguousarray(v) for n, v in out.items()}


def declare(nc, arrays):
    return {n: nc.dram_tensor(f"in_{n}", v.shape, mybir.dt.from_np(v.dtype), kind="ExternalInput").ap()
            for n, v in arrays.items()}


def kernel(**inputs):
    import concourse.bacc as bacc
    from concourse.bass_utils import run_bass_kernel_spmd

    arrays = lay_out(inputs)
    nc = bacc.Bacc("TRN2", target_bir_lowering=False, num_devices=1)
    A = declare(nc, arrays)
    out = nc.dram_tensor("out_x", [B, S, D], F32, kind="ExternalOutput").ap()
    build(nc, A, out)
    r = run_bass_kernel_spmd(nc, [{f"in_{n}": v for n, v in arrays.items()}], core_ids=[0])
    return r.results[0]["out_x"]
```

```python
from contextlib import ExitStack

import concourse.bass as bass
import numpy as np
from concourse import mybir

ALU = mybir.AluOpType
ACT = mybir.ActivationFunctionType
AX = mybir.AxisListType
F32 = mybir.dt.float32
F16 = mybir.dt.float16
I32 = mybir.dt.int32
RMAX = bass.bass_isa.ReduceOp.max
RADD = bass.bass_isa.ReduceOp.add

P = 128
B, S, D = 4, 512, 512
KT = D // P
TT = S // P
EPS = 1e-5
MASKED = -1e20
TINY = 1e-30

H0, E0 = 32, 16
PAIRS = H0 // 2
SLOPE0 = 2.0 ** (-(2.0 ** (-(np.log2(H0) - 3))))
SLOPES = [float(np.float32(SLOPE0 ** (i + 1))) for i in range(H0)]

EV = E0 + 1
KEYS = ((2, 3), (1,), (0,))
COLD = {2: 0, 3: 2, 1: 3, 0: 6}

H1, G1, E1 = 32, 8, 128
HG = H1 // G1
UP = 64 + E1
WK = E1 + E1

HID = 1360
HT = -(-HID // P)
OH, OD = HID // 8, D // 8

TRI = [P * t * (t + 1) // 2 for t in range(TT)]
TRIW = P * TT * (TT + 1) // 2
COL = [sum(TT - i for i in range(j)) for j in range(TT)]
NBLK = TT * (TT + 1) // 2


class Chain:

    def __init__(self, eng, sem):
        self.eng, self.sem, self.n = eng, sem, 0

    def tick(self, ins):
        ins.then_inc(self.sem, 1)
        self.n += 1

    def settle(self):
        self.eng.wait_ge(self.sem, self.n)


def clear(nc, sems):
    nums = sorted(s.num for s in sems)
    assert nums == list(range(nums[0], nums[-1] + 1))
    nc.all_engine_barrier(sems_to_clear=range(nums[0], nums[-1] + 1))


class Scope:

    def __init__(self, nc, stack):
        self.nc, self.stack, self.sems = nc, stack, []

    def sb(self, name, shape, dt=F32):
        return self.stack.enter_context(self.nc.sbuf_tensor(name, shape, dt))

    def ps(self, name, shape, dt=F32):
        return self.stack.enter_context(self.nc.psum_tensor(name, shape, dt))

    def sem(self, name):
        s = self.stack.enter_context(self.nc.semaphore(name))
        self.sems.append(s)
        return s


def split_matrices(nc, sc, tag, jobs, gm, rg, before={}, after={}):

    def nothing(eng):
        pass

    am = sc.sb(f"{tag}_am", [P, len(jobs)])
    s_ld = [sc.sem(f"{tag}_loaded{i}") for i in range(len(jobs))]
    s_dv = sc.sem(f"{tag}_dve_steps")
    s_am = sc.sem(f"{tag}_rowmax")
    s_gm = sc.sem(f"{tag}_globalmax")
    s_rg = sc.sem(f"{tag}_reciprocal")
    s_hi = sc.sem(f"{tag}_hi")
    s_lo = sc.sem(f"{tag}_lo")

    def flat(ap):
        return ap.rearrange("p a b -> p (a b)")

    with nc.Block() as block:

        @block.sync
        def _(sp):
            before.get("sync", nothing)(sp)
            for i, job in enumerate(jobs):
                for dst, src in job[1]:
                    sp.dma_start(dst, src).then_inc(s_ld[i], 16)
            after.get("sync", nothing)(sp)

        @block.tensor
        def _(pe):
            after.get("tensor", nothing)(pe)

        @block.gpsimd
        def _(pool):
            before.get("gpsimd", nothing)(pool)
            for i in range(len(jobs)):
                pool.wait_ge(s_am, i + 1)
                pool.partition_all_reduce(gm[:, i:i + 1], am[:, i:i + 1], P, RMAX).then_inc(s_gm, 1)

        @block.vector
        def _(dve):
            before.get("vector", nothing)(dve)
            ch = Chain(dve, s_dv)
            for i, job in enumerate(jobs):
                raw = flat(job[2])
                dve.wait_ge(s_ld[i], 16 * len(job[1]))
                if len(job) > 5:
                    codes, scales = job[5]
                    ch.tick(dve.tensor_scalar(raw, flat(codes), -128.0, None, ALU.add))
                    ch.settle()
                    ch.tick(dve.tensor_tensor(raw, raw, flat(scales), ALU.mult))
                    ch.settle()
                dve.tensor_reduce(am[:, i:i + 1], raw, AX.X, ALU.max,
                                  apply_absolute_value=True).then_inc(s_am, 1)
            for i, job in enumerate(jobs):
                dve.wait_ge(s_gm, i + 1)
                ch.tick(dve.tensor_scalar(gm[:, i:i + 1], gm[:, i:i + 1], TINY, None, ALU.max))
                ch.settle()
                dve.reciprocal(rg[:, i:i + 1], gm[:, i:i + 1]).then_inc(s_rg, 1)
                dve.wait_ge(s_rg, i + 1)
                dve.wait_ge(s_hi, i + 1)
                dve.scalar_tensor_tensor(flat(job[4]), flat(job[2]), rg[:, i:i + 1], flat(job[3]),
                                         ALU.mult, ALU.subtract).then_inc(s_lo, 1)

        @block.scalar
        def _(act):
            for i, job in enumerate(jobs):
                act.wait_ge(s_rg, i + 1)
                act.activation(flat(job[3]), flat(job[2]), ACT.Copy,
                               scale=rg[:, i:i + 1]).then_inc(s_hi, 1)
            after.get("scalar", nothing)(act)


def layer0(nc, A, W0, C, xT, x2_dram):
    with ExitStack() as stack:
        sc = Scope(nc, stack)
        xb = sc.sb("xb", [P, TT, D])
        yb = sc.sb("yb", [P, TT, D])
        xf = sc.sb("x_front", [P, TT, D])
        aT = [sc.sb("front_T_hi", [P, KT, S], F16), sc.sb("front_T_lo", [P, KT, S], F16)]
        bT = [sc.sb("back_T_hi", [P, KT, S], F16), sc.sb("back_T_lo", [P, KT, S], F16)]
        khi = sc.sb("khi", [P, S], F16)
        kst = sc.sb("kst", [P, S], F16)
        kab = sc.sb("kab", [P, 2, S], F16)
        v2 = sc.sb("v2", [P, TT, 2 * EV], F16)
        qT = [sc.sb("qT_hi", [P, KT, S], F16), sc.sb("qT_lo", [P, KT, S], F16)]
        stk = sc.sb("stk", [P, 2, S], F16)
        tab = sc.sb("tab", [P, 4, S])
        xp = sc.sb("xp", [P, 4, TRIW])
        pT = [sc.sb("pT_hi", [P, 3, NBLK, P], F16), sc.sb("pT_lo", [P, 3, NBLK, P], F16)]
        ob = sc.sb("ob", [P, TT, H0, EV])
        nm = sc.sb("nm", [P, 4, TT])
        rsum = sc.sb("rsum", [P, TT, H0])
        st = sc.sb("st", [P, TT, 6])
        mv = sc.sb("mv", [P, TT, 2])
        ve = sc.sb("ve", [P, TT])
        rs = sc.sb("rs", [P, TT])
        cs = sc.sb("cs", [P, 1])
        cinv = sc.sb("cinv", [P, 1])
        cy = sc.sb("cy", [P, 1])
        banks = [sc.ps(f"bank{i}", [P, S]) for i in range(8)]

        s_x = sc.sem("s_x_loaded")
        s_dv = sc.sem("s_dve_steps")
        s_ya = sc.sem("s_y_out")
        s_yf = sc.sem("s_y_filled")
        s_xf = sc.sem("s_front_loaded")
        s_nf = sc.sem("s_front_normed")
        s_kv = sc.sem("s_keys_values_ready")
        s_ve = sc.sem("s_variance")
        s_rs = sc.sem("s_rstd")
        s_xn = sc.sem("s_normed_rows")
        s_tf = sc.sem("s_t_filled")
        s_th = sc.sem("s_t_hi_out")
        s_tl = sc.sem("s_t_lo_out")
        s_sf = sc.sem("s_s_filled")
        s_sh = sc.sem("s_s_hi_out")
        s_kf = sc.sem("s_stack_filled")
        s_sd = sc.sem("s_s_freed_by_dve")
        s_sa = sc.sem("s_stack_ready")
        s_tab = sc.sem("s_table")
        s_ex = sc.sem("s_exp")
        s_pf = sc.sem("s_pv_filled")
        s_pd = sc.sem("s_pv_out")
        s_on = sc.sem("s_heads_normed")
        s_out = sc.sem("s_x_stored")

        def score_fills(h):
            return [("s", h, i) for i in range(3 - h % 2)]

        def score_fill(h, t):
            return ("s", h - h % 2, 2) if t == 1 else ("s", h, 0 if t == 3 else 1)

        Q_AT = {0: 1, 9: 2, 11: 3}
        Y_AT, N2_AT = (1, 3, 5, 7), (12, 13, 14, 15)
        F_AT, N3_AT = (17, 19, 21, 23), (28, 29, 30, 31)
        N1_AT = (16, 18, 20, 22)

        wq, wkv, wo, wf = W0["wq"], W0["wkv"], W0["wo"], W0["wf"]
        GQ, GKV, GO, GF = range(4)
        gm = W0["gm"]

        def run(b, attend, back, front):
            extra = {}
            if attend:
                extra.update({h: [("q", m)] for h, m in Q_AT.items()})
                if back:
                    for kind, at in (("y", Y_AT), ("n2", N2_AT), ("f", F_AT), ("n3", N3_AT)):
                        extra.update({h: [(kind, t)] for t, h in enumerate(at)})
                if front:
                    extra.update({h: [("n1", t)] for t, h in enumerate(N1_AT)})
                front_pieces = {2: (0,)}
                back_pieces = {8: (0,), 9: (1,), 10: (2,), 24: (3,), 25: (4,), 26: (5,)}
                pool_pieces = {2: ["n1"]} if front else {}
                if back:
                    pool_pieces.update({8: ["rstd"], 9: ["rstd"], 24: ["rstd"], 25: ["rstd"]})
                steps = H0 + 2
            else:
                for h, kind in enumerate(("y", "n2", "f", "n3") * back + ("n1",) * front):
                    extra[2 * h] = [(kind, t) for t in range(TT)]
                front_pieces = {-1: (0,)}
                back_pieces = {1: (0, 1, 2), 5: (3, 4, 5)}
                pool_pieces = {0: ["rstd"] * (front + 4 * back)}
                steps = 8 if back else 2

            uses = [("K",), ("V",), ("q", 0)] * attend + [("o", t) for t in range(TT)] * back
            uses += ([("stack", 0)] + score_fills(0)) * attend
            for h in range(steps):
                if attend:
                    uses += [("T", h - 1, i) for i in range(3)] * (1 <= h <= H0)
                    uses += [("stack", h // 2 + 1)] * (h % 2 == 0 and h // 2 + 1 < PAIRS)
                    uses += [("pv", h - 2)] * (h >= 2)
                    uses += score_fills(h + 1) if h + 1 < H0 else []
                uses += extra.get(h, [])
            slot = {u: n for n, u in enumerate(uses)}
            signals = {k: (s_tf, s_tl) for k in ("n1", "T", "o", "n2", "n3")}
            signals.update({"pv": (s_pf, s_pd), "stack": (s_kf, s_sa), "y": (s_yf, s_ya)})
            filled, emptied, counted = {}, {}, {}
            for u in uses:
                full, empty = signals.get(u[0], (s_sf, s_sd))
                counted[full] = counted.get(full, 0) + 1
                filled[u], emptied[u] = (full, counted[full]), (empty, counted[full])

            def bank_of(u):
                return banks[slot[u] % 8]

            his = [u for u in uses if u[0] in ("K", "V", "q")]
            hi_no = {u: i + 1 for i, u in enumerate(his)}

            def transposed(u, half):
                t = u[1]
                if u[0] == "n3":
                    return xT[half][:, :, bass.ds((b - 1) * S + t * P, P)]
                return (aT if u[0] == "n1" else bT)[half][:, :, t * P:(t + 1) * P]

            def evacuations(h, kinds):
                return [u for u in extra.get(h - 1, []) if u[0] in kinds]

            with nc.Block() as block:

                @block.sync
                def _(sp):
                    if front:
                        sp.dma_start(xf[:, :, :], A["x"][b + 1].rearrange("(t p) d -> p t d", p=P)).then_inc(s_xf, 16)
                    if back:
                        sp.dma_start(xb[:, :, :], A["x"][b - 1].rearrange("(t p) d -> p t d", p=P)).then_inc(s_x, 16)
                        sp.wait_ge(s_xn, 2 * TT)
                        sp.dma_start(x2_dram[b - 1].rearrange("(t p) d -> p t d", p=P),
                                     xb[:, :, :]).then_inc(s_out, 16)
                        sp.wait_ge(s_out, 16)

                @block.gpsimd
                def _(pool):
                    count = {"rs": 0}

                    def piece(kind):
                        count["rs"] += 1
                        pool.wait_ge(s_ve, count["rs"])
                        pool.tensor_tensor(rs[:, :], ve[:, :], C["mhalf"][:, 0:TT], ALU.pow).then_inc(s_rs, 1)
                        if kind == "n1":
                            pool.wait_ge(s_rs, count["rs"])
                            for t in range(TT):
                                pool.tensor_scalar(xf[:, t, :], xf[:, t, :], mv[:, t, 0:1], rs[:, t:t + 1],
                                                   ALU.subtract, ALU.mult).then_inc(s_nf, 1)

                    for h in range(H0 if attend else 0):
                        if h >= 4:
                            pool.wait_ge(*emptied[score_fills(h - 4)[-1]])
                        pool.tensor_scalar(tab[:, h % 4, :], C["rel"][:, :], 4.0 * SLOPES[h], cinv[:, 0:1],
                                           ALU.mult, ALU.mult).then_inc(s_tab, 1)
                        for p in pool_pieces.get(h - 3, []):
                            piece(p)
                    for p in [] if attend else pool_pieces[0]:
                        piece(p)

                @block.tensor
                def _(pe):
                    def take(u):
                        if slot[u] >= 8:
                            pe.wait_ge(*emptied[uses[slot[u] - 8]])
                        return bank_of(u)

                    def transpose4(u, rows):
                        bank = take(u)
                        for k in range(KT):
                            last = pe.transpose(bank[:, k * P:(k + 1) * P],
                                                rows[:, k * P:(k + 1) * P], C["ident"][:, :])
                        last.then_inc(s_tf, 1)

                    def product(out, lhs, rhs, fill, full=s_sf):
                        for k in range(KT):
                            for i, (a, c) in enumerate(((0, 0), (1, 0), (0, 1))):
                                last = pe.matmul(out, lhs(a, k), rhs(c, k), start=(k == 0 and i == 0),
                                                 stop=(k == KT - 1 and i == 2))
                        if fill:
                            last.then_inc(full, 1)

                    def project(m):
                        product(take(("q", m))[:, :], lambda a, k: wq[a][:, k, m * P:(m + 1) * P],
                                lambda c, k: aT[c][:, k, :], True)

                    def fill(u):
                        kind, t = u
                        if kind == "q":
                            project(t)
                        elif kind in ("y", "f"):
                            pe.wait_ge(*emptied[("o" if kind == "y" else "n2", t)])
                            w = wo if kind == "y" else wf
                            product(take(u)[:, :], lambda a, k: bT[a][:, k, t * P:(t + 1) * P],
                                    lambda c, k: w[c][:, k, :], True, s_yf if kind == "y" else s_sf)
                        elif kind == "n1":
                            pe.wait_ge(s_nf, t + 1)
                            transpose4(u, xf[:, t, :])
                        else:
                            pe.wait_ge(s_xn, (TT if kind == "n3" else 0) + t + 1)
                            transpose4(u, yb[:, t, :])

                    if attend:
                        product(take(("K",))[:, :], lambda a, k: wkv[a][:, k, 0:P],
                                lambda c, k: aT[c][:, k, :], True)
                        bank = take(("V",))
                        for t in range(TT):
                            product(bank[:, t * E0:(t + 1) * E0], lambda a, k: aT[a][:, k, t * P:(t + 1) * P],
                                    lambda c, k: wkv[c][:, k, P:P + E0], t == TT - 1)
                        project(0)
                    if back:
                        for t in range(TT):
                            pe.wait_ge(s_on, t + 1)
                            transpose4(("o", t), yb[:, t, :])

                    def stack_queries(p):
                        m, r = p // 4, p % 4
                        bank = take(("stack", p))
                        pe.wait_ge(*emptied[("q", m)])
                        pe.matmul(bank[:, :], C["sel"][:, 2 * r, :], qT[0][:, m, :], start=True, stop=False)
                        pe.matmul(bank[:, :], C["sel"][:, 2 * r + 1, :], qT[1][:, m, :], start=False,
                                  stop=True).then_inc(s_kf, 1)

                    def scores(h):
                        if h == 0:
                            pe.wait_ge(s_kv, 1)
                        pe.wait_ge(s_sa, h // 2 + 1)
                        e = h % 2
                        for u in score_fills(h):
                            bank = take(u)
                            pieces = (((3, e, e + 1),), ((2, e, e + 1), (0, e, e + 1)), ((1, 0, 2),))[u[2]]
                            at = 0
                            for t, e0, e1 in pieces:
                                w = P * (t + 1)
                                last = pe.matmul(
                                    bank[:, at:at + (e1 - e0) * w].rearrange("p (h k) -> p h k", k=w),
                                    stk[:, h // 2 % 2, t * P:(t + 1) * P], kab[:, e0:e1, 0:w],
                                    start=True, stop=True)
                                at += w
                            last.then_inc(s_sf, 1)

                    def transpose_probs(h):
                        for i, js in enumerate(KEYS):
                            bank, at = take(("T", h, i)), 0
                            pe.wait_ge(s_ex, TT * h + TT - js[0])
                            for j in js:
                                for t in range(j, TT):
                                    last = pe.transpose(bank[:, at:at + P],
                                                        xp[:, h % 4, TRI[t] + j * P:TRI[t] + (j + 1) * P],
                                                        C["ident"][:, :])
                                    at += P
                            last.then_inc(s_tf, 1)

                    def weigh_values(h):
                        bank = take(("pv", h))
                        pe.wait_ge(*emptied[("T", h, 2)])
                        for t in range(TT):
                            for j in range(t + 1):
                                for i, (a, c) in enumerate(((0, 0), (1, 0), (0, 1))):
                                    last = pe.matmul(bank[:, t * EV:(t + 1) * EV],
                                                     pT[a][:, h % 3, COLD[j] + t - j, :],
                                                     v2[:, j, c * EV:(c + 1) * EV],
                                                     start=(j == 0 and i == 0), stop=(j == t and i == 2))
                        last.then_inc(s_pf, 1)

                    if attend:
                        stack_queries(0)
                        scores(0)
                    for h in range(steps):
                        if attend:
                            if 1 <= h <= H0:
                                transpose_probs(h - 1)
                            if h % 2 == 0 and h // 2 + 1 < PAIRS:
                                stack_queries(h // 2 + 1)
                            if h >= 2:
                                weigh_values(h - 2)
                            if h + 1 < H0:
                                scores(h + 1)
                        for u in extra.get(h, []):
                            fill(u)

                @block.scalar
                def _(act):
                    def hi4(u):
                        act.wait_ge(*filled[u])
                        act.activation(transposed(u, 0), bank_of(u)[:, :].rearrange("p (k c) -> p k c", c=P),
                                       ACT.Copy).then_inc(s_th, 1)

                    def hi_s(u, dst, src):
                        act.wait_ge(*filled[u])
                        act.activation(dst, src, ACT.Copy).then_inc(s_sh, 1)

                    def q_hi(u):
                        hi_s(u, qT[0][:, u[1], :], bank_of(u)[:, :])

                    if attend:
                        hi_s(("K",), khi[:, :], bank_of(("K",))[:, :])
                        hi_s(("V",), v2[:, :, 0:E0],
                             bank_of(("V",))[:, 0:TT * E0].rearrange("p (t e) -> p t e", e=E0))
                        q_hi(("q", 0))
                    if back:
                        for t in range(TT):
                            hi4(("o", t))

                    def copy_stack(p):
                        if p >= 2:
                            act.wait_ge(*filled[("s", 2 * p - 3, 1)])
                        act.wait_ge(*filled[("stack", p)])
                        act.activation(stk[:, p % 2, :], bank_of(("stack", p))[:, :], ACT.Copy).then_inc(s_sa, 1)

                    def probs_hi(h):
                        for i, js in enumerate(KEYS):
                            n = sum(TT - j for j in js)
                            act.wait_ge(*filled[("T", h, i)])
                            if h >= 3:
                                act.wait_ge(s_pf, h - 2)
                            act.activation(pT[0][:, h % 3, COLD[js[0]]:COLD[js[0]] + n, :],
                                           bank_of(("T", h, i))[:, 0:n * P].rearrange("p (t c) -> p t c", c=P),
                                           ACT.Copy).then_inc(s_th, 1)

                    def copy_head(h):
                        act.wait_ge(*filled[("pv", h)])
                        act.activation(ob[:, :, h, :],
                                       bank_of(("pv", h))[:, 0:TT * EV].rearrange("p (t e) -> p t e", e=EV),
                                       ACT.Copy).then_inc(s_pd, 1)

                    if attend:
                        copy_stack(0)
                    for h in range(steps):
                        for u in evacuations(h, ("n1", "n2", "n3")):
                            hi4(u)
                        for u in evacuations(h, ("y",)):
                            act.wait_ge(*filled[u])
                            if u[1] == 0:
                                act.wait_ge(s_tl, TT)
                            act.activation(yb[:, u[1], :], bank_of(u)[:, :], ACT.Copy,
                                           scale=cy[:, 0:1]).then_inc(s_ya, 1)
                        if not attend:
                            continue
                        if 1 <= h <= H0:
                            probs_hi(h - 1)
                        if h % 2 == 0 and h // 2 + 1 < PAIRS:
                            copy_stack(h // 2 + 1)
                        if h < H0:
                            for t in reversed(range(TT)):
                                act.wait_ge(*emptied[score_fill(h, t)])
                                x = xp[:, h % 4, TRI[t]:TRI[t] + P * (t + 1)]
                                act.activation(x, x, ACT.Exp, scale=-1.0,
                                               bias=nm[:, h % 4, t:t + 1]).then_inc(s_ex, 1)
                        if h >= 2:
                            if h == 2 and back:
                                act.wait_ge(s_on, TT)
                            copy_head(h - 2)
                        for u in evacuations(h, ("q",)):
                            q_hi(u)

                @block.vector
                def _(dve):
                    ch = Chain(dve, s_dv)
                    count = {"rs": 0}

                    def statistics(src):
                        for t in range(TT):
                            ch.tick(dve.bn_stats(st[:, t, :], src[:, t, :]))
                        ch.settle()
                        for t in range(TT):
                            ch.tick(dve.bn_aggr(mv[:, t, :], st[:, t, :]))
                        ch.settle()
                        dve.tensor_scalar(ve[:, :], mv[:, :, 1], EPS, None, ALU.add).then_inc(s_ve, 1)
                        count["rs"] += 1

                    def normalise(dst, src, done):
                        dve.wait_ge(s_rs, count["rs"])
                        for t in range(TT):
                            done(dve.tensor_scalar(dst[:, t, :], src[:, t, :], mv[:, t, 0:1], rs[:, t:t + 1],
                                                   ALU.subtract, ALU.mult))

                    def add_normed():
                        normalise(yb, yb, ch.tick)
                        dve.wait_ge(s_x, 16)
                        ch.settle()
                        for t in range(TT):
                            ch.tick(dve.tensor_tensor(xb[:, t, :], xb[:, t, :], yb[:, t, :], ALU.add))
                        ch.settle()
                        statistics(xb)

                    def front_piece():
                        dve.wait_ge(s_xf, 16)
                        statistics(xf)
                        if not attend:
                            normalise(xf, xf, lambda ins: ins.then_inc(s_nf, 1))

                    def back_piece(i):
                        if i == 0:
                            if front:
                                dve.wait_ge(s_nf, TT)
                            dve.wait_ge(s_ya, TT)
                            statistics(yb)
                        elif i == 3:
                            dve.wait_ge(*emptied[("f", TT - 1)])
                            statistics(yb)
                        elif i % 3 == 1:
                            add_normed()
                        else:
                            normalise(yb, xb, lambda ins: ins.then_inc(s_xn, 1))

                    def lo4(u):
                        dve.wait_ge(s_th, filled[u][1])
                        dve.tensor_tensor(transposed(u, 1), bank_of(u)[:, :].rearrange("p (k c) -> p k c", c=P),
                                          transposed(u, 0), ALU.subtract).then_inc(s_tl, 1)

                    def q_lo(m):
                        dve.wait_ge(s_sh, hi_no[("q", m)])
                        dve.tensor_tensor(qT[1][:, m, :], bank_of(("q", m))[:, :], qT[0][:, m, :],
                                          ALU.subtract).then_inc(s_sd, 1)

                    if back:
                        ch.tick(dve.reciprocal(rsum[:, :, :], ob[:, :, :, E0]))
                        ch.settle()
                        for t in range(TT):
                            dve.tensor_tensor(yb[:, t, :].rearrange("p (h e) -> p h e", e=E0), ob[:, t, :, 0:E0],
                                              rsum[:, t, :].unsqueeze(2).to_broadcast([P, H0, E0]),
                                              ALU.mult).then_inc(s_on, 1)
                    if attend:
                        dve.wait_ge(s_sh, 1)
                        dve.tensor_tensor(kst[64:128, :], bank_of(("K",))[64:128, :], khi[64:128, :],
                                          ALU.subtract).then_inc(s_sd, 1)
                        ch.tick(dve.tensor_copy(kst[0:64, :], khi[0:64, :]))
                        dve.wait_ge(s_sh, 2)
                        dve.tensor_tensor(v2[:, :, EV:EV + E0],
                                          bank_of(("V",))[:, 0:TT * E0].rearrange("p (t e) -> p t e", e=E0),
                                          v2[:, :, 0:E0], ALU.subtract).then_inc(s_sd, 1)
                        ch.settle()
                        dve.wait_ge(s_sd, 2)
                        ch.tick(dve.tensor_scalar(kab[:, 0, :], kst[:, :], C["pairmask"][:, 0:1], None, ALU.mult))
                        ch.tick(dve.tensor_scalar(kab[:, 1, :], kst[:, :], C["pairmask"][:, 1:2], None, ALU.mult))
                        ch.settle()
                        dve.nop().then_inc(s_kv, 1)
                        q_lo(0)
                    if back:
                        for t in range(TT):
                            lo4(("o", t))

                    def biased(h, t, u, at, signal):
                        w = P * (t + 1)
                        ins = dve.tensor_tensor_reduce(
                            out=xp[:, h % 4, TRI[t]:TRI[t] + w], in0=bank_of(u)[:, at:at + w],
                            in1=tab[:, h % 4, S - w:S], scale=cs[:, 0:1], scalar=3e38,
                            op0=ALU.add, op1=ALU.min, accum_out=nm[:, h % 4, t:t + 1])
                        if signal:
                            ins.then_inc(s_sd, 1)

                    def biased_scores(h):
                        last_head = h + 1 - h % 2
                        if last_head >= 4:
                            dve.wait_ge(*filled[("T", last_head - 4, 2)])
                        dve.wait_ge(s_tab, last_head + 1)
                        dve.wait_ge(*filled[("s", h, 0)])
                        biased(h, 3, ("s", h, 0), 0, True)
                        dve.wait_ge(*filled[("s", h, 1)])
                        biased(h, 2, ("s", h, 1), 0, False)
                        biased(h, 0, ("s", h, 1), 3 * P, True)
                        if h % 2 == 0:
                            dve.wait_ge(*filled[("s", h, 2)])
                            biased(h, 1, ("s", h, 2), 0, False)
                            biased(h + 1, 1, ("s", h, 2), 2 * P, True)

                    def probs_lo(h):
                        for i, js in enumerate(KEYS):
                            u, n = ("T", h, i), sum(TT - j for j in js)
                            dve.wait_ge(s_th, filled[u][1])
                            c = slice(COLD[js[0]], COLD[js[0]] + n)
                            dve.tensor_tensor(pT[1][:, h % 3, c, :],
                                              bank_of(u)[:, 0:n * P].rearrange("p (t c) -> p t c", c=P),
                                              pT[0][:, h % 3, c, :], ALU.subtract).then_inc(s_tl, 1)

                    if front and -1 in front_pieces:
                        front_piece()
                    for h in range(steps):
                        if attend and h < H0:
                            biased_scores(h)
                        for u in evacuations(h, ("n1", "n2", "n3")):
                            lo4(u)
                        if attend and 1 <= h <= H0:
                            probs_lo(h - 1)
                        for kind, t in evacuations(h, ("q", "f")):
                            if kind == "q":
                                q_lo(t)
                                continue
                            out = bank_of((kind, t))
                            dve.wait_ge(*filled[(kind, t)])
                            dve.scalar_tensor_tensor(yb[:, t, :], out[:, :], gm[:, GF:GF + 1],
                                                     C["bias"][:, :], ALU.mult, ALU.add).then_inc(s_sd, 1)
                        if front and h in front_pieces:
                            front_piece()
                        for i in back_pieces.get(h, ()) if back else ():
                            back_piece(i)

            clear(nc, sc.sems)

        with nc.Block() as block:

            @block.vector
            def _(dve):
                ch = Chain(dve, s_dv)
                ch.tick(dve.tensor_scalar(cs[:, :], gm[:, GQ:GQ + 1], gm[:, GKV:GKV + 1], -E0 ** -0.5,
                                          ALU.mult, ALU.mult))
                ch.tick(dve.tensor_scalar(cy[:, :], gm[:, GKV:GKV + 1], gm[:, GO:GO + 1], None, ALU.mult))
                ch.settle()
                ch.tick(dve.tensor_scalar(cinv[:, :], cs[:, :], -4.0, None, ALU.mult))
                ch.settle()
                ch.tick(dve.reciprocal(cinv[:, :], cinv[:, :]))
                ch.tick(dve.memset(v2[:, :, E0:EV], 1.0))
                ch.tick(dve.memset(v2[:, :, EV + E0:2 * EV], 0.0))
                ch.settle()

        clear(nc, sc.sems)
        run(-1, False, False, True)
        run(0, True, False, True)
        with nc.Fori(1, B - 1) as b:
            run(b, True, True, True)
        run(B - 1, True, True, False)
        run(B, False, True, False)


class FusedUpProjections:

    def __init__(self, nc, sc, A, fused_dram):
        self.A, self.dram = A, fused_dram
        self.NU = G1 * UP
        self.wd = sc.sb("wdk", [P, KT, D])
        self.wu = sc.sb("wup", [P, KT, self.NU])
        self.fused = sc.sb("fused", [P, KT * self.NU // S, S])
        self.bank = [sc.ps(f"fu_bank{i}", [P, S]) for i in range(8)]
        self.s_ld = [sc.sem(f"s_fu_loaded{i}") for i in range(1 + self.NU // S)]
        self.s_f = sc.sem("s_fu_filled")
        self.s_e = sc.sem("s_fu_out")
        self.s_o = sc.sem("s_fu_stored")
        self.tiles = [(m, n) for n in range(self.NU // S) for m in range(KT)]

    def load(self, sp, part):
        if part == 0:
            sp.dma_start(self.wd[:, :, :], self.A["wdk1"].rearrange("(k p) n -> p k n", p=P)).then_inc(self.s_ld[0], 16)
        else:
            c = slice((part - 1) * S, part * S)
            sp.dma_start(self.wu[:, :, c], self.A["wup1"][:, c].rearrange("(k p) n -> p k n", p=P)).then_inc(
                self.s_ld[part], 16)

    def multiply(self, pe):
        pe.wait_ge(self.s_ld[0], 16)
        for i, (m, n) in enumerate(self.tiles):
            pe.wait_ge(self.s_ld[n + 1], 16)
            if i >= 8:
                pe.wait_ge(self.s_e, i - 7)
            for k in range(KT):
                last = pe.matmul(self.bank[i % 8][:, :], self.wd[:, k, m * P:(m + 1) * P],
                                 self.wu[:, k, n * S:(n + 1) * S], start=(k == 0), stop=(k == KT - 1))
            last.then_inc(self.s_f, 1)

    def copy(self, act):
        for i in range(len(self.tiles)):
            act.wait_ge(self.s_f, i + 1)
            act.activation(self.fused[:, i, :], self.bank[i % 8][:, :], ACT.Copy).then_inc(self.s_e, 1)

    def store(self, sp):
        for i, (m, n) in enumerate(self.tiles):
            sp.wait_ge(self.s_e, i + 1)
            sp.dma_start(self.dram[m * P:(m + 1) * P, n * S:(n + 1) * S], self.fused[:, i, :]).then_inc(self.s_o, 16)
        sp.wait_ge(self.s_o, 16 * len(self.tiles))


def attention1(nc, A, C, xT, yacc, fused_dram, load_down):
    with ExitStack() as stack:
        sc = Scope(nc, stack)
        NH = B * HG
        raw_kv = sc.sb("raw_kv", [P, KT, WK])
        raw_q = sc.sb("raw_q", [P, KT, D])
        raw_o = sc.sb("raw_o", [P, HG, D])
        wkv = [sc.sb("wkv1_hi", [P, KT, WK], F16), sc.sb("wkv1_lo", [P, KT, WK], F16)]
        wq = [sc.sb("wq1_hi", [P, KT, D], F16), sc.sb("wq1_lo", [P, KT, D], F16)]
        wo = [sc.sb("wo1_hi", [P, HG, D], F16), sc.sb("wo1_lo", [P, HG, D], F16)]
        am = sc.sb("am1", [P, 3])
        gm = sc.sb("gm1", [P, 3])
        rg = sc.sb("rg1", [P, 3])
        cs = sc.sb("cs1", [P, 1])
        cy = sc.sb("cy1", [P, 1])
        rope = {n: sc.sb(n, [P, S]) for n in ("cosq", "sinq", "cosk", "sink")}
        mask = sc.sb("mask", [P, S])
        t2 = sc.sb("t2", [P, 2, S])
        qf = sc.sb("qf", [P, 2, S])
        qs = sc.sb("q_in_sbuf", [P, 2, S])
        kT = [sc.sb("kT_hi", [P, S], F16), sc.sb("kT_lo", [P, S], F16)]
        v = [sc.sb("v_hi", [P, 2, TT, E1], F16), sc.sb("v_lo", [P, 2, TT, E1], F16)]
        qT = [sc.sb("q1T_hi", [P, 2, S], F16), sc.sb("q1T_lo", [P, 2, S], F16)]
        xp = sc.sb("xp1", [P, 4, TRIW])
        pT = [sc.sb("p1T_hi", [P, NBLK, HG, P], F16), sc.sb("p1T_lo", [P, NBLK, HG, P], F16)]
        oT = [sc.sb("o1T_hi", [P, TT, HG, P], F16), sc.sb("o1T_lo", [P, TT, HG, P], F16)]
        nm = sc.sb("nm1", [P, 4, TT])
        ls = sc.sb("ls1", [P, 4, TT])
        rl = sc.sb("rl1", [P, 4, TT])
        bank = [sc.ps(f"bank1_{i}", [P, S]) for i in range(8)]
        GKV, GQ, GO = range(3)

        def load_kv(g):
            f = fused_dram.rearrange("(k p) (g n) -> g p k n", p=P, n=UP)[g]
            r = A["wkr1"][g]
            return [(raw_kv[:, :, 0:32], r[:, :, 0:32]), (raw_kv[:, :, 64:96], r[:, :, 32:64]),
                    (raw_kv[:, :, 32:64], f[:, :, 0:32]), (raw_kv[:, :, 96:128], f[:, :, 32:64]),
                    (raw_kv[:, :, E1:WK], f[:, :, 64:UP])]


        s_dv = sc.sem("s1_dve_steps")
        s_am = sc.sem("s1_rowmax")
        s_gm = sc.sem("s1_globalmax")
        s_rg = sc.sem("s1_reciprocal")
        s_wh = sc.sem("s1_weights_hi")
        s_wl = sc.sem("s1_weights_lo")
        s_lo = sc.sem("s1_output_weights_loaded")
        s_ld = sc.sem("s1_next_weights_loaded")
        s_rf = sc.sem("s1_projection_filled")
        s_vh = sc.sem("s1_v_hi_out")
        s_rd = sc.sem("s1_projection_out")
        s_qf = sc.sem("s1_roped")
        s_qh = sc.sem("s1_roped_hi")
        s_ql = sc.sem("s1_roped_lo")
        s_sf = sc.sem("s1_scores_filled")
        s_sd = sc.sem("s1_scores_out")
        s_qc = sc.sem("s1_product_copied")
        s_rot = sc.sem("s1_rotated")
        s_ex = sc.sem("s1_exp")
        s_rl = sc.sem("s1_sum_reciprocal")
        s_pn = sc.sem("s1_probs_normed")
        s_tf = sc.sem("s1_transpose_filled")
        s_th = sc.sem("s1_transpose_hi_out")
        s_tl = sc.sem("s1_transpose_lo_out")
        s_of = sc.sem("s1_output_filled")
        s_oh = sc.sem("s1_output_hi_out")
        s_od = sc.sem("s1_output_out")

        DRAIN = 6
        TILES = ((0, 1), (2,), (3,))
        KEYS1 = ((0,), (1,), (2, 3))

        def pv_batch(n):
            return (n - 6) // HG if (n - 6) % HG == 0 else None

        def projections(n):
            out = []
            for b in range(-2, B - 1):
                out += {0: [(b, 0), (b, 1)], 1: [(b, 2)], 2: [(b, 3)]}.get(n - (HG * b + 7), [])
            return out

        def plan(turn):
            out = []
            for n in range(NH if turn else DRAIN):
                if turn:
                    if n % HG == 0:
                        out += [("r", ("k", n // HG)), ("r", ("v", n // HG))]
                    out.append(("r", ("q", n)))
                if turn or n < 1:
                    out += [("s", (n - 1, i)) for i in range(3)]
                if pv_batch(n) is not None and (turn or n < DRAIN):
                    out += [("o", ("pv", pv_batch(n), t)) for t in range(TT)]
                projected = [("o", ("wo", b, t)) for b, t in projections(n)]
                transposed = [("t", (n - 2, i)) for i in range(3) if turn or n < 2]
                out += transposed + projected if n == NH - 1 else projected + transposed
            return out

        full_turn = plan(True)
        assert len(full_turn) % 8 == 0
        s_out_of = {"r": s_rd, "s": s_sd, "t": s_tl, "o": s_od}

        s_c = sc.sem("s1_tables")

        def load_tables(sp):
            for n in rope:
                sp.dma_start(rope[n][:, :], A[n]).then_inc(s_c, 16)
            sp.dma_start(mask[:, :], A["mask"]).then_inc(s_c, 16)
            load_down(sp)
            sp.wait_ge(s_c, 16 * 5)

        def clear_past_outputs(pool):
            for half in range(2):
                pool.memset(oT[half][:, 2:TT, :, :], 0.0)
                pool.memset(wo[half][:, :, :], 0.0)

        def clear_past(dve):
            for half in range(2):
                dve.memset(kT[half][:, :], 0.0)
                dve.memset(qT[half][:, 1, :], 0.0)
                dve.memset(v[half][:, 1, :, :], 0.0)
                dve.memset(pT[half][:, :, 0, :], 0.0)
            dve.memset(xp[:, 2, :], 0.0)
            dve.memset(rl[:, 2, :], 0.0)
            dve.memset(cs[:, :], 0.0)
            dve.memset(cy[:, :], 0.0)
            for i in range(3):
                dve.memset(bank[full_turn.index(("t", (NH - 3, i))) % 8][:, :], 0.0)

        split_matrices(nc, sc, "w1", [
            ("kv", load_kv(0), raw_kv[:, :, :], wkv[0][:, :, :], wkv[1][:, :, :]),
            ("q", [(raw_q[:, :, :], A["wq1"][0])], raw_q[:, :, :], wq[0][:, :, :], wq[1][:, :, :])],
            gm, rg, {"vector": clear_past, "gpsimd": clear_past_outputs}, {"sync": load_tables})

        def blocks(js):
            return slice(COL[js[0]], COL[js[-1]] + TT - js[-1])

        def flat(ap):
            return ap.rearrange("p a b -> p (a b)")

        raws = {GKV: raw_kv, GQ: raw_q, GO: raw_o}
        splits = {GKV: wkv, GQ: wq, GO: wo}

        def run_steps(g):
            turn = g is not None
            steps = NH if turn else DRAIN
            fillings = plan(turn)
            no, counts = {}, {"r": 0, "s": 0, "t": 3, "o": 0}
            for kind, u in fillings:
                no[kind, u] = counts[kind]
                counts[kind] += 1
            place = {f: i for i, f in enumerate(fillings)}
            for i in range(3):
                no["t", (-3, i)] = i
                place["t", (-3, i)] = full_turn.index(("t", (NH - 3, i)))
            ropes = [u for kind, u in fillings if kind == "r" and u[0] != "v"]
            rope_no = {u: i for i, u in enumerate(ropes)}

            def bank_of(kind, u):
                return bank[place[kind, u] % 8]


            with nc.Block() as block:

                @block.sync
                def _(sp):
                    if turn:
                        nxt = (g + 1) % G1
                        sp.dma_start(raw_o[:, :, :], A["wo1"][g]).then_inc(s_lo, 16)
                        for n in load_kv(nxt):
                            sp.dma_start(*n).then_inc(s_ld, 16)
                        sp.wait_ge(s_wl, 1)
                        sp.dma_start(raw_q[:, :, :], A["wq1"][nxt]).then_inc(s_ld, 16)
                        sp.wait_ge(s_lo, 16)
                        sp.wait_ge(s_ld, 16 * 6)

                @block.gpsimd
                def _(pool):
                    def global_max(k, i):
                        pool.wait_ge(s_am, k + 1)
                        pool.partition_all_reduce(gm[:, i:i + 1], am[:, i:i + 1], P, RMAX).then_inc(s_gm, 1)

                    for i, u in enumerate(ropes):
                        pool.wait_ge(s_qc, i + 1)
                        pool.tensor_tensor(qs[:, i % 2, :], qs[:, i % 2, :],
                                           rope["sink" if u[0] == "k" else "sinq"][:, :],
                                           ALU.mult).then_inc(s_rot, 1)
                        pool.wait_ge(s_rot, i + 1)
                        pool.wait_ge(s_rd, no["r", u] + 1)
                        if i >= 2:
                            pool.wait_ge(s_ql, i - 1)
                        pool.tensor_tensor(qf[:, i % 2, :], qs[:, i % 2, :], t2[:, i % 2, :],
                                           ALU.add).then_inc(s_qf, 1)
                        if u == ("q", 2):
                            global_max(0, GO)
                        if u == ("q", 11):
                            global_max(1, GKV)
                            global_max(2, GQ)

                @block.tensor
                def _(pe):
                    def triple(out, lhs, rhs, first, last):
                        for i, (a, c) in enumerate(((0, 0), (1, 0), (0, 1))):
                            ins = pe.matmul(out, lhs(a), rhs(c), start=(first and i == 0),
                                            stop=(last and i == 2))
                        return ins

                    def take(kind, u):
                        i = place[kind, u]
                        f = fillings[i - 8] if i >= 8 else full_turn[i - 8]
                        if i < 8 and f[0] == "t" and f[1][0] == NH - 3:
                            f = ("t", (-3, f[1][1]))
                        if i >= 8 or f in no and f[1][0] == -3:
                            pe.wait_ge(s_out_of[f[0]], no[f] + 1)
                        return bank[i % 8]

                    def project(u, w, col, b):
                        out = take("r", u)
                        for k in range(KT):
                            ins = triple(out[:, :], lambda a: w[a][:, k, col:col + P],
                                         lambda c: xT[c][:, k, b * S:(b + 1) * S], k == 0, k == KT - 1)
                        ins.then_inc(s_rf, 1)

                    def values(b):
                        out = take("r", ("v", b))
                        for t in range(TT):
                            for k in range(KT):
                                ins = triple(out[:, t * P:(t + 1) * P],
                                             lambda a: xT[a][:, k, b * S + t * P:b * S + (t + 1) * P],
                                             lambda c: wkv[c][:, k, E1:WK], k == 0, k == KT - 1)
                        ins.then_inc(s_rf, 1)

                    def scores(n):
                        if n >= 0:
                            pe.wait_ge(s_ql, rope_no[("q", n)] + 1)
                        for i, tiles in enumerate(TILES):
                            out, col = take("s", (n, i)), 0
                            for t in tiles:
                                w = P * (t + 1)
                                ins = triple(out[:, col:col + w], lambda a: qT[a][:, n % 2, t * P:(t + 1) * P],
                                             lambda c: kT[c][:, 0:w], True, True)
                                col += w
                            ins.then_inc(s_sf, 1)

                    def transpose_probs(n):
                        pe.wait_ge(s_pn, n + 3)
                        for i, js in enumerate(KEYS1):
                            out, col = take("t", (n, i)), 0
                            for j in js:
                                for t in range(j, TT):
                                    ins = pe.transpose(out[:, col:col + P],
                                                       xp[:, n % 4, TRI[t] + j * P:TRI[t] + (j + 1) * P],
                                                       C["ident"][:, :])
                                    col += P
                            ins.then_inc(s_tf, 1)

                    def weigh_values(b):
                        pe.wait_ge(s_tl, no["t", (HG * b + 3, 2)] + 1)
                        for t in range(TT):
                            out = take("o", ("pv", b, t))
                            for j in range(t + 1):
                                ins = triple(out[:, :], lambda a: v[a][:, b % 2, j, :],
                                             lambda c: flat(pT[c][:, COL[j] + t - j, :, :]), j == 0, j == t)
                            ins.then_inc(s_of, 1)

                    def project_out(b, t):
                        if b >= -1:
                            pe.wait_ge(s_od, no["o", ("pv", b, t)] + 1)
                        if (b, t) == (0, 0):
                            pe.wait_ge(s_wl, 2)
                        out = take("o", ("wo", b, t))
                        for h in range(HG):
                            ins = triple(out[:, :], lambda a: oT[a][:, t, h, :],
                                         lambda c: wo[c][:, h, :], h == 0, h == HG - 1)
                        ins.then_inc(s_of, 1)

                    for n in range(steps):
                        if turn:
                            b = n // HG
                            if n % HG == 0:
                                project(("k", b), wkv, 0, b)
                                values(b)
                            if n == HG - 1:
                                pe.wait_ge(s_wl, 1)
                            project(("q", n), wq, (n % HG) * P, b)
                        if turn or n < 1:
                            scores(n - 1)
                        if pv_batch(n) is not None:
                            weigh_values(pv_batch(n))
                        if n == NH - 1:
                            transpose_probs(n - 2)
                        for b, t in projections(n):
                            project_out(b, t)
                        if n != NH - 1 and (turn or n < 2):
                            transpose_probs(n - 2)

                @block.scalar
                def _(act):
                    def weights_hi(i, cols):
                        act.activation(splits[i][0][:, :, cols], raws[i][:, :, cols], ACT.Copy,
                                       scale=rg[:, i:i + 1]).then_inc(s_wh, 1)

                    def copy_product(u):
                        i = rope_no[u]
                        act.wait_ge(s_rf, no["r", u] + 1)
                        if i >= 2:
                            act.wait_ge(s_qf, i - 1)
                        q = bank_of("r", u)
                        act.activation(qs[0:64, i % 2, :], q[64:128, :], ACT.Copy)
                        act.activation(qs[64:128, i % 2, :], q[0:64, :], ACT.Copy).then_inc(s_qc, 1)

                    def roped_hi(u):
                        i = rope_no[u]
                        act.wait_ge(s_qf, i + 1)
                        if u[0] == "k":
                            act.wait_ge(s_sf, 3 * (HG * u[1] + 1))
                            dst = kT[0][:, :]
                        else:
                            if u[1] >= 1:
                                act.wait_ge(s_sf, 3 * u[1])
                            dst = qT[0][:, u[1] % 2, :]
                        act.activation(dst, qf[:, i % 2, :], ACT.Copy).then_inc(s_qh, 1)

                    for n in range(steps):
                        m = n - 3
                        if turn or m < 0:
                            for i, js in enumerate(KEYS1):
                                dst = pT[0][:, blocks(js), m % HG, :]
                                if m >= -2:
                                    act.wait_ge(s_tf, 3 * (m + 2) + i + 1)
                                act.activation(dst, bank_of("t", (m, i))[:, 0:P * dst.shape[1]].rearrange(
                                    "p (t c) -> p t c", c=P), ACT.Copy).then_inc(s_th, 1)
                        m = n - 2
                        if turn or m < 0:
                            if m >= -1:
                                act.wait_ge(s_rl, m + 2)
                            for t in range(TT):
                                x = xp[:, m % 4, TRI[t]:TRI[t] + P * (t + 1)]
                                ins = act.activation(x, x, ACT.Copy, scale=rl[:, m % 4, t:t + 1])
                            ins.then_inc(s_pn, 1)
                        if turn:
                            if n % HG == 0:
                                copy_product(("k", n // HG))
                            copy_product(("q", n))
                        if turn and n % HG == 0:
                            b = n // HG
                            act.wait_ge(s_rf, no["r", ("v", b)] + 1)
                            if b >= 1:
                                act.wait_ge(s_of, no["o", ("pv", b - 2, TT - 1)] + 1)
                            act.activation(flat(v[0][:, b % 2, :, :]), bank_of("r", ("v", b))[:, :],
                                           ACT.Copy).then_inc(s_vh, 1)
                        m = n - 1
                        if turn or m < 0:
                            for t in range(TT):
                                act.wait_ge(s_sd, 3 * (m + 1) + max(t, 1))
                                x = xp[:, m % 4, TRI[t]:TRI[t] + P * (t + 1)]
                                ins = act.activation(x, x, ACT.Exp, scale=-1.0, bias=nm[:, m % 4, t:t + 1],
                                                     accum_out=ls[:, m % 4, t:t + 1])
                            ins.then_inc(s_ex, 1)
                        if turn:
                            if n % HG == 0:
                                roped_hi(("k", n // HG))
                            roped_hi(("q", n))
                        if pv_batch(n) is not None:
                            for t in range(TT):
                                u = ("pv", pv_batch(n), t)
                                act.wait_ge(s_of, no["o", u] + 1)
                                act.activation(flat(oT[0][:, t, :, :]), bank_of("o", u)[:, :],
                                               ACT.Copy).then_inc(s_oh, 1)
                        if turn and n == 0:
                            weights_hi(GQ, slice(3 * P, D))
                        if turn and n == 6:
                            act.wait_ge(s_rg, 1)
                            act.wait_ge(s_of, no["o", ("wo", -1, TT - 1)] + 1)
                            weights_hi(GO, slice(0, D))
                        if turn and n == 13:
                            act.wait_ge(s_rg, 3)
                            act.wait_ge(s_rf, no["r", ("q", 12)] + 1)
                            weights_hi(GKV, slice(0, WK))
                            weights_hi(GQ, slice(0, P))
                        if turn and n >= 14:
                            act.wait_ge(s_rf, no["r", ("q", n - 1)] + 1)
                            weights_hi(GQ, slice((n - 13) * P, (n - 12) * P))

                @block.vector
                def _(dve):
                    ch = Chain(dve, s_dv)

                    def add_projections(n):
                        for b, t in projections(n):
                            u = ("wo", b, t)
                            dve.wait_ge(s_of, no["o", u] + 1)
                            y = yacc[:, TT * (b % B) + t, :]
                            dve.scalar_tensor_tensor(y, bank_of("o", u)[:, :], cy[:, 0:1], y, ALU.mult,
                                                     ALU.add).then_inc(s_od, 1)

                    def row_max(i):
                        dve.tensor_reduce(am[:, i:i + 1], flat(raws[i][:, :, :]), AX.X, ALU.max,
                                          apply_absolute_value=True).then_inc(s_am, 1)

                    def reciprocal(k, i):
                        dve.wait_ge(s_gm, k + 1)
                        ch.tick(dve.tensor_scalar(gm[:, i:i + 1], gm[:, i:i + 1], TINY, None, ALU.max))
                        ch.settle()
                        dve.reciprocal(rg[:, i:i + 1], gm[:, i:i + 1]).then_inc(s_rg, 1)
                        dve.wait_ge(s_rg, k + 1)

                    def weights_lo(k, i, cols):
                        dve.wait_ge(s_wh, k + 1)
                        dve.scalar_tensor_tensor(splits[i][1][:, :, cols], raws[i][:, :, cols],
                                                 rg[:, i:i + 1], splits[i][0][:, :, cols], ALU.mult,
                                                 ALU.subtract).then_inc(s_wl, 1)

                    def times_cos(u):
                        i = rope_no[u]
                        cos = rope["cosk" if u[0] == "k" else "cosq"]
                        dve.wait_ge(s_rf, no["r", u] + 1)
                        dve.wait_ge(s_qc, i + 1)
                        if i >= 2:
                            dve.wait_ge(s_qf, i - 1)
                        dve.tensor_tensor(t2[:, i % 2, :], bank_of("r", u)[:, :], cos[:, :],
                                          ALU.mult).then_inc(s_rd, 1)

                    def roped_lo(u):
                        i = rope_no[u]
                        hi, lo = (x[:, :] for x in kT) if u[0] == "k" else (x[:, u[1] % 2, :] for x in qT)
                        dve.wait_ge(s_qh, i + 1)
                        dve.tensor_tensor(lo, qf[:, i % 2, :], hi, ALU.subtract).then_inc(s_ql, 1)

                    for n in range(steps):
                        m = n - 3
                        if turn or m < 0:
                            for i, js in enumerate(KEYS1):
                                hi = pT[0][:, blocks(js), m % HG, :]
                                dve.wait_ge(s_th, 3 * (m + 3) + i + 1)
                                dve.tensor_tensor(pT[1][:, blocks(js), m % HG, :],
                                                  bank_of("t", (m, i))[:, 0:P * hi.shape[1]].rearrange(
                                                      "p (t c) -> p t c", c=P), hi,
                                                  ALU.subtract).then_inc(s_tl, 1)
                        if turn:
                            b = n // HG
                            if n % HG == 0:
                                times_cos(("k", b))
                                dve.wait_ge(s_vh, b + 1)
                                dve.tensor_tensor(flat(v[1][:, b % 2, :, :]), bank_of("r", ("v", b))[:, :],
                                                  flat(v[0][:, b % 2, :, :]), ALU.subtract).then_inc(s_rd, 1)
                            times_cos(("q", n))
                        m = n - 1
                        if turn or m < 0:
                            if m >= 2:
                                dve.wait_ge(s_tf, 3 * (m - 1))
                            for i, tiles in enumerate(TILES):
                                col = 0
                                dve.wait_ge(s_sf, 3 * (m + 1) + i + 1)
                                for t in tiles:
                                    w = P * (t + 1)
                                    ins = dve.tensor_tensor_reduce(
                                        out=xp[:, m % 4, TRI[t]:TRI[t] + w],
                                        in0=bank_of("s", (m, i))[:, col:col + w],
                                        in1=mask[:, S - w:S], scale=cs[:, 0:1], scalar=3e38,
                                        op0=ALU.add, op1=ALU.min, accum_out=nm[:, m % 4, t:t + 1])
                                    col += w
                                ins.then_inc(s_sd, 1)
                        if turn and n == 0:
                            dve.wait_ge(s_sd, 3)
                            ch.tick(dve.tensor_scalar(cs[:, :], gm[:, GQ:GQ + 1], gm[:, GKV:GKV + 1],
                                                      -E1 ** -0.5, ALU.mult, ALU.mult))
                            ch.settle()
                        if pv_batch(n) is not None:
                            for t in range(TT):
                                u = ("pv", pv_batch(n), t)
                                dve.wait_ge(s_oh, TT * (pv_batch(n) + 1) + t + 1)
                                dve.tensor_tensor(flat(oT[1][:, t, :, :]), bank_of("o", u)[:, :],
                                                  flat(oT[0][:, t, :, :]), ALU.subtract).then_inc(s_od, 1)
                        if n != NH - 1:
                            add_projections(n)
                        if turn:
                            if n % HG == 0:
                                roped_lo(("k", n // HG))
                            roped_lo(("q", n))
                        m = n - 1
                        if turn or m < 0:
                            dve.wait_ge(s_ex, m + 2)
                            dve.reciprocal(rl[:, m % 4, :], ls[:, m % 4, :]).then_inc(s_rl, 1)
                        if turn and n == 0:
                            weights_lo(0, GQ, slice(3 * P, D))
                        if turn and n == 2:
                            dve.wait_ge(s_lo, 16)
                            row_max(GO)
                        if turn and n == 3:
                            reciprocal(0, GO)
                        if turn and n == 6:
                            weights_lo(1, GO, slice(0, D))
                            dve.wait_ge(s_od, no["o", ("wo", -1, TT - 1)] + 1)
                            ch.tick(dve.tensor_scalar(cy[:, :], gm[:, GKV:GKV + 1], gm[:, GO:GO + 1], None,
                                                      ALU.mult))
                            ch.settle()
                        if turn and n == 11:
                            dve.wait_ge(s_ld, 16 * 6)
                            row_max(GKV)
                            row_max(GQ)
                        if turn and n == 12:
                            reciprocal(1, GKV)
                            reciprocal(2, GQ)
                        if turn and n == 13:
                            weights_lo(2, GKV, slice(0, WK))
                            weights_lo(3, GQ, slice(0, P))
                        if turn and n >= 14:
                            weights_lo(n - 10, GQ, slice((n - 13) * P, (n - 12) * P))
                        if n == NH - 1:
                            add_projections(n)

            clear(nc, sc.sems)

        with nc.Fori(0, G1) as g:
            run_steps(g)
        run_steps(None)


def feed_forward1(nc, A, C, raw_down, yacc, x2_dram, out):
    with ExitStack() as stack:
        sc = Scope(nc, stack)
        tg = sc.sb("tern_gate", [P, KT, HID], F16)
        tu = sc.sb("tern_up", [P, KT, HID], F16)
        td = sc.sb("tern_down", [P, HT, D], F16)
        R = {"gate": sc.sb("raw_gate", [P, 8 * OH]), "up": sc.sb("raw_up", [P, 8 * OH]),
             "sum": sc.sb("raw_down_once", [P, OH * D // P])}
        compact = sc.sb("tern_compact", [P, 2, 8, OH], F16)
        pos = sc.sb("above_half", [P, 8 * OH], F16)
        sgn = sc.sb("sgn_dn", [P, HT, 8], F16)
        am = sc.sb("abs_sums", [P, 3])
        scale = sc.sb("tern_scale", [P, 3])
        half = sc.sb("half", [P, 3])
        nhalf = sc.sb("nhalf", [P, 3])
        kup = sc.sb("kup", [P, 1])
        cdn = sc.sb("cdn", [P, 1])
        GATE, UPW, DOWN = range(3)
        xb = sc.sb("x_before", [P, TT, D])
        nb = sc.sb("normed", [P, TT, D])
        yb = sc.sb("y_out", [P, TT, D])
        aT = [sc.sb("a2T_hi", [P, KT, S], F16), sc.sb("a2T_lo", [P, KT, S], F16)]
        sl = sc.sb("silu_gate", [P, 2, S])
        hf = sc.sb("hidden", [P, 2, S])
        hT = [sc.sb("hidden_hi", [P, HT, S], F16), sc.sb("hidden_lo", [P, HT, S], F16)]
        st = sc.sb("st2", [P, TT, 6])
        mv = sc.sb("mv2", [P, TT, 2])
        ve = sc.sb("ve2", [P, TT])
        rs = sc.sb("rs2", [P, TT])
        bank_g = [sc.ps(f"bank_g{i}", [P, S]) for i in range(2)]
        bank_u = [sc.ps(f"bank_u{i}", [P, S]) for i in range(2)]
        bank_t = [sc.ps(f"bank2_t{i}", [P, S]) for i in range(2)]
        bank_y = [sc.ps(f"bank_y{i}", [P, S]) for i in range(2)]

        s_sg = sc.sem("s2_signs_loaded")
        s_ld = [sc.sem(f"s2_raw_{n}_loaded") for n in R]
        s_x = sc.sem("s2_x_loaded")
        s_xu = sc.sem("s2_x_used")
        s_dv = sc.sem("s2_dve_steps")
        s_am = sc.sem("s2_abs_sums")
        s_gm = sc.sem("s2_total_sums")
        s_cp = sc.sem("s2_compact_ternary")
        s_ev = sc.sem("s2_blocks_by_dve")
        s_ea = sc.sem("s2_blocks_by_act")
        s_td = sc.sem("s2_down_ternary")
        s_ve = sc.sem("s2_variance")
        s_rs = sc.sem("s2_rstd")
        s_xn = sc.sem("s2_normed_rows")
        s_nd = sc.sem("s2_ready_to_add")
        s_ad = sc.sem("s2_x_added")
        s_tm = sc.sem("s2_down_thresholded")
        s_tf = sc.sem("s2_t_filled")
        s_th = sc.sem("s2_t_hi_out")
        s_tl = sc.sem("s2_t_lo_out")
        s_gf = sc.sem("s2_gate_filled")
        s_uf = sc.sem("s2_up_filled")
        s_sl = sc.sem("s2_silu")
        s_hf = sc.sem("s2_hidden")
        s_hh = sc.sem("s2_hidden_hi")
        s_hl = sc.sem("s2_hidden_lo")
        s_yf = sc.sem("s2_y_filled")
        s_yd = sc.sem("s2_y_out")
        s_fin = sc.sem("s2_final")
        s_out = sc.sem("s2_stored")

        unit, sign = octonion_table()
        ACT_UNITS = (4, 5, 6, 7)

        def width(m):
            return min(P, HID - m * P)

        def row(b, t):
            return yacc[:, bass.ds(b * TT + t, 1), :].rearrange("p a n -> p (a n)")

        def expand(eng, c, units, done):
            for i in units:
                for n, full in enumerate((tg, tu)):
                    h = i % 2 * 64
                    dst = full[h:h + 64, i // 2, c * OH:(c + 1) * OH]
                    done(eng, dst, compact[h:h + 64, n, int(unit[i, c]), :], -float(sign[i, c]))

        def run_batch(b, first, last):
            fronts = [0] * first + [b + 1] * (not last)
            pieces_at = (4, 5, 6, 8, 9, 10) if first else (0, 1, 2, 3, 4, 5, 7, 8, 9)

            with nc.Block() as block:

                @block.sync
                def _(sp):
                    if first:
                        for i, n in enumerate(("gate", "up")):
                            for h in range(2):
                                sp.dma_start(R[n][h * 64:(h + 1) * 64, :], A[f"w_{n}"]).then_inc(s_ld[i], 16)
                        sp.dma_start(R["sum"][:, :], A["w_down_once"]).then_inc(s_ld[2], 16)
                        sp.dma_start(sgn[:, :, :], A["sgn_dn"]).then_inc(s_sg, 16)
                    for i, bb in enumerate(fronts):
                        if i:
                            sp.wait_ge(s_xu, 1)
                        sp.dma_start(xb[:, :, :], x2_dram[bb].rearrange("(t p) d -> p t d", p=P)).then_inc(s_x, 16)
                    if not first:
                        sp.wait_ge(s_fin, TT)
                        sp.dma_start(out[b - 1].rearrange("(t p) d -> p t d", p=P), yb[:, :, :]).then_inc(s_out, 16)
                        sp.wait_ge(s_out, 16)

                @block.gpsimd
                def _(pool):
                    count = {"rs": 0, "nd": 0}

                    def rstd():
                        count["rs"] += 1
                        pool.wait_ge(s_ve, count["rs"])
                        pool.tensor_tensor(rs[:, :], ve[:, :], C["mhalf"][:, 0:TT], ALU.pow).then_inc(s_rs, 1)

                    def add(dst, a, c, done):
                        count["nd"] += TT
                        pool.wait_ge(s_nd, count["nd"])
                        for t in range(TT):
                            pool.tensor_tensor(dst(t), a(t), c(t), ALU.add).then_inc(done, 1)

                    def front():
                        return [rstd, lambda: add(lambda t: row(b + 1, t), lambda t: xb[:, t, :],
                                                  lambda t: nb[:, t, :], s_ad), rstd]

                    if first:
                        rstd()
                        for i in range(3):
                            pool.wait_ge(s_am, i + 1)
                            pool.partition_all_reduce(scale[:, i:i + 1], am[:, i:i + 1], P, RADD).then_inc(s_gm, 1)
                        rstd()
                        pool.wait_ge(s_sg, 16)
                        steps = dict(zip((5, 6, 9), front()))
                        for k in range(HT):
                            w = width(k)
                            x = td[0:w, k, :].rearrange("p (c o) -> p c o", c=8)
                            pool.wait_ge(s_tm, k + 1)
                            pool.tensor_tensor(x, x, sgn[0:w, k, :].unsqueeze(2).to_broadcast([w, 8, OD]),
                                               ALU.mult).then_inc(s_td, 1)
                            if k in steps:
                                steps[k]()
                    else:
                        rstd()
                        add(lambda t: yb[:, t, :], lambda t: row(b - 1, t), lambda t: yb[:, t, :], s_fin)
                        for step in front() if not last else []:
                            step()

                @block.tensor
                def _(pe):
                    def transposes(i):
                        for t in range(TT):
                            n = i * TT + t
                            pe.wait_ge(s_xn, n + 1)
                            if n >= 2:
                                pe.wait_ge(s_tl, n - 1)
                            for k in range(KT):
                                ins = pe.transpose(bank_t[n % 2][:, k * P:(k + 1) * P],
                                                     nb[:, t, k * P:(k + 1) * P], C["ident"][:, :])
                            ins.then_inc(s_tf, 1)

                    if first:
                        transposes(0)
                        pe.wait_ge(s_tl, TT)
                    for m in range(HT):
                        w = width(m)
                        if first:
                            c = (m * P + w - 1) // OH
                            pe.wait_ge(s_ev, 2 * (8 - len(ACT_UNITS)) * (c + 1))
                            pe.wait_ge(s_ea, 2 * len(ACT_UNITS) * (c + 1))
                        for bank, tern, filled in ((bank_g, tg, s_gf), (bank_u, tu, s_uf)):
                            if m >= 2:
                                pe.wait_ge(s_hf, m - 1)
                            for k in range(KT):
                                for c in range(2):
                                    ins = pe.matmul(bank[m % 2][0:w, :], tern[:, k, m * P:m * P + w],
                                                    aT[c][:, k, :], start=(k == 0 and c == 0),
                                                    stop=(k == KT - 1 and c == 1))
                            ins.then_inc(filled, 1)
                    if not last:
                        transposes(len(fronts) - 1)
                    if first:
                        pe.wait_ge(s_td, HT)
                    for t in range(TT):
                        if t >= 2:
                            pe.wait_ge(s_yd, t - 1)
                        for m in range(HT):
                            w = width(m)
                            if t == 0:
                                pe.wait_ge(s_hl, m + 1)
                            for c in range(2):
                                ins = pe.matmul(bank_y[t % 2][:, :], hT[c][0:w, m, t * P:(t + 1) * P],
                                                td[0:w, m, :], start=(m == 0 and c == 0),
                                                stop=(m == HT - 1 and c == 1))
                        ins.then_inc(s_yf, 1)

                @block.scalar
                def _(act):
                    def transposes_hi(i):
                        for t in range(TT):
                            n = i * TT + t
                            act.wait_ge(s_tf, n + 1)
                            act.activation(aT[0][:, :, t * P:(t + 1) * P],
                                           bank_t[n % 2][:, :].rearrange("p (k c) -> p k c", c=P),
                                           ACT.Copy).then_inc(s_th, 1)

                    def block_copy(eng, dst, src, s):
                        eng.activation(dst, src, ACT.Copy, scale=s).then_inc(s_ea, 1)

                    if first:
                        act.wait_ge(s_cp, 2)
                        for c in range(2):
                            expand(act, c, ACT_UNITS, block_copy)
                        transposes_hi(0)
                    for m in range(HT + 1):
                        if m < HT:
                            w = width(m)
                            act.wait_ge(s_gf, m + 1)
                            if m >= 2:
                                act.wait_ge(s_hf, m - 1)
                            act.activation(sl[0:w, m % 2, :], bank_g[m % 2][0:w, :], ACT.Silu,
                                           scale=scale[0:w, GATE:GATE + 1]).then_inc(s_sl, 1)
                        if m >= 1:
                            w = width(m - 1)
                            act.wait_ge(s_hf, m)
                            act.activation(hT[0][0:w, m - 1, :], hf[0:w, (m - 1) % 2, :],
                                           ACT.Copy).then_inc(s_hh, 1)
                        if first and m + 2 < 8:
                            expand(act, m + 2, ACT_UNITS, block_copy)
                    if not last:
                        transposes_hi(len(fronts) - 1)

                @block.vector
                def _(dve):
                    ch = Chain(dve, s_dv)
                    count = {"rs": 0, "front": 0}

                    def statistics(src, tiles=range(TT)):
                        for t in tiles:
                            ch.tick(dve.bn_stats(st[:, t, :], src(t)))
                        if TT - 1 not in tiles:
                            return
                        ch.settle()
                        for t in range(TT):
                            ch.tick(dve.bn_aggr(mv[:, t, :], st[:, t, :]))
                        ch.settle()
                        dve.tensor_scalar(ve[:, :], mv[:, :, 1], EPS, None, ALU.add).then_inc(s_ve, 1)
                        count["rs"] += 1

                    def normalise(dst, src, done):
                        dve.wait_ge(s_rs, count["rs"])
                        for t in range(TT):
                            done(dve.tensor_scalar(dst(t), src(t), mv[:, t, 0:1], rs[:, t:t + 1],
                                                   ALU.subtract, ALU.mult))

                    def to_pool(ins):
                        ins.then_inc(s_nd, 1)

                    def normed(t):
                        return nb[:, t, :]

                    def own_front():
                        def x(t):
                            return row(0, t)

                        def add():
                            normalise(normed, x, ch.tick)
                            dve.wait_ge(s_x, 16)
                            ch.settle()
                            for t in range(TT):
                                ch.tick(dve.tensor_tensor(x(t), xb[:, t, :], nb[:, t, :], ALU.add))
                            ch.settle()
                            dve.nop().then_inc(s_xu, 1)
                            statistics(x)

                        return [lambda: statistics(x), add,
                                lambda: normalise(normed, x, lambda ins: ins.then_inc(s_xn, 1))]

                    def front():
                        def x(t):
                            return row(b + 1, t)

                        def ready_to_add():
                            if first:
                                dve.wait_ge(s_tf, TT)
                            dve.wait_ge(s_x, 16 * len(fronts))
                            normalise(normed, x, to_pool)

                        def statistics_again():
                            dve.wait_ge(s_ad, TT)
                            statistics(x, (0, 1))

                        return [lambda: statistics(x, (0, 1)), lambda: statistics(x, (2, 3)), ready_to_add,
                                statistics_again, lambda: statistics(x, (2, 3)),
                                lambda: normalise(normed, x, lambda ins: ins.then_inc(s_xn, 1))]

                    def final():
                        def y(t):
                            return yb[:, t, :]

                        return [lambda: statistics(y, (0, 1)), lambda: statistics(y, (2, 3)),
                                lambda: normalise(y, y, to_pool)]

                    def transposes_lo(i):
                        for t in range(TT):
                            n = i * TT + t
                            dve.wait_ge(s_th, n + 1)
                            dve.tensor_tensor(aT[1][:, :, t * P:(t + 1) * P],
                                              bank_t[n % 2][:, :].rearrange("p (k c) -> p k c", c=P),
                                              aT[0][:, :, t * P:(t + 1) * P], ALU.subtract).then_inc(s_tl, 1)

                    def block_copy(eng, dst, src, s):
                        eng.tensor_scalar(dst, src, s, None, ALU.mult).then_inc(s_ev, 1)

                    def ternary(w, dst, i, done):
                        n = w.shape[-1]
                        p = pos[0:w.shape[0], 0:n]
                        ch.tick(dve.tensor_scalar(p, w, half[0:w.shape[0], i:i + 1], None, ALU.is_gt))
                        ch.settle()
                        done(dve.scalar_tensor_tensor(dst, w, nhalf[0:w.shape[0], i:i + 1], p, ALU.is_lt,
                                                      ALU.subtract))

                    def down(k):
                        w = width(k)
                        if k:
                            dve.wait_ge(s_tm, k)
                        ternary(raw_down[0:w, k, :], td[0:w, k, :], DOWN, lambda ins: ins.then_inc(s_tm, 1))

                    ours = tuple(i for i in range(8) if i not in ACT_UNITS)
                    if first:
                        own = own_front()
                        own[0]()
                        for i, raw in enumerate((R["gate"], R["up"], R["sum"])):
                            dve.wait_ge(s_ld[i], (32, 32, 16)[i])
                            dve.tensor_reduce(am[:, i:i + 1], raw[:, :], AX.X, ALU.add,
                                              apply_absolute_value=True).then_inc(s_am, 1)
                        dve.wait_ge(s_gm, 3)
                        ch.tick(dve.tensor_scalar(scale[:, 0:2], scale[:, 0:2], 0.5 / (OH * D), None, ALU.mult))
                        ch.tick(dve.tensor_scalar(scale[:, 2:3], scale[:, 2:3], 1.0 / (OH * D), None, ALU.mult))
                        ch.settle()
                        ch.tick(dve.tensor_scalar(half[:, :], scale[:, :], 0.5, None, ALU.mult))
                        ch.tick(dve.tensor_scalar(nhalf[:, :], scale[:, :], -0.5, None, ALU.mult))
                        ch.tick(dve.tensor_scalar(kup[:, :], scale[:, GATE:GATE + 1], 16.0, TINY, ALU.mult, ALU.max))
                        ch.settle()
                        ch.tick(dve.tensor_tensor(cdn[:, :], kup[:, :], scale[:, UPW:UPW + 1], ALU.mult))
                        ch.settle()
                        ch.tick(dve.reciprocal(kup[:, :], kup[:, :]))
                        ch.tick(dve.tensor_tensor(cdn[:, :], cdn[:, :], scale[:, DOWN:DOWN + 1], ALU.mult))
                        for i, raw in enumerate((R["gate"], R["up"])):
                            if i:
                                dve.wait_ge(s_cp, 1)
                            ternary(raw[:, :], compact[:, i, :, :].rearrange("p c o -> p (c o)"), i,
                                    lambda ins: ins.then_inc(s_cp, 1))
                        own[1]()
                        dve.wait_ge(s_cp, 2)
                        expand(dve, 0, ours, block_copy)
                        own[2]()
                        expand(dve, 1, ours, block_copy)
                        transposes_lo(0)
                    pieces = dict(zip(pieces_at, (final() if not first else []) + (front() if not last else [])))
                    for m in range(HT + 1):
                        if m < HT:
                            w = width(m)
                            dve.wait_ge(s_uf, m + 1)
                            dve.wait_ge(s_sl, m + 1)
                            if m >= 2:
                                dve.wait_ge(s_hh, m - 1)
                                dve.wait_ge(s_hl, m - 1)
                            dve.scalar_tensor_tensor(hf[0:w, m % 2, :], bank_u[m % 2][0:w, :], kup[0:w, 0:1],
                                                     sl[0:w, m % 2, :], ALU.mult, ALU.mult).then_inc(s_hf, 1)
                        if m >= 1:
                            w = width(m - 1)
                            dve.wait_ge(s_hf, m)
                            dve.wait_ge(s_hh, m)
                            dve.tensor_tensor(hT[1][0:w, m - 1, :], hf[0:w, (m - 1) % 2, :],
                                              hT[0][0:w, m - 1, :], ALU.subtract).then_inc(s_hl, 1)
                        if first and m + 2 < 8:
                            expand(dve, m + 2, ours, block_copy)
                        if first and m < HT:
                            down(m)
                        if m in pieces:
                            pieces[m]()
                    if not last:
                        transposes_lo(len(fronts) - 1)
                    if not first:
                        dve.wait_ge(s_out, 16)
                    for t in range(TT):
                        dve.wait_ge(s_yf, t + 1)
                        dve.tensor_scalar(yb[:, t, :], bank_y[t % 2][:, :], cdn[:, 0:1], None,
                                          ALU.mult).then_inc(s_yd, 1)
                    if last:
                        for t in range(TT):
                            dve.wait_ge(s_yd, t + 1)
                            ch.tick(dve.bn_stats(st[:, t, :], yb[:, t, :]))
                        ch.settle()
                        for t in range(TT):
                            ch.tick(dve.bn_aggr(mv[:, t, :], st[:, t, :]))
                        ch.settle()

            clear(nc, sc.sems)

        run_batch(0, True, False)
        with nc.Fori(1, B - 1) as b:
            run_batch(b, False, False)
        run_batch(B - 1, False, True)

        with nc.Block() as block:

            @block.sync
            def _(sp):
                for t in range(TT):
                    sp.wait_ge(s_fin, t + 1)
                    sp.dma_start(out[B - 1, t * P:(t + 1) * P, :], yb[:, t, :]).then_inc(s_out, 16)
                sp.wait_ge(s_out, 16 * TT)

            @block.gpsimd
            def _(pool):
                pool.wait_ge(s_ve, 1)
                pool.tensor_tensor(rs[:, :], ve[:, :], C["mhalf"][:, 0:TT], ALU.pow).then_inc(s_rs, 1)

            @block.vector
            def _(dve):
                dve.tensor_scalar(ve[:, :], mv[:, :, 1], EPS, None, ALU.add).then_inc(s_ve, 1)
                dve.wait_ge(s_rs, 1)
                for t in range(TT):
                    dve.tensor_scalar(yb[:, t, :], yb[:, t, :], mv[:, t, 0:1], rs[:, t:t + 1],
                                      ALU.subtract, ALU.mult).then_inc(s_yd, 1)
                for t in range(TT):
                    dve.wait_ge(s_yd, t + 1)
                    dve.tensor_tensor(yb[:, t, :], row(B - 1, t), yb[:, t, :], ALU.add).then_inc(s_fin, 1)

        clear(nc, sc.sems)


def build(nc, A, out, stages=4):
    x2_dram = nc.dram_tensor("x2_scratch", [B, S, D], F32).ap()
    fused_dram = nc.dram_tensor("fused_scratch", [D, G1 * UP], F32).ap()
    with ExitStack() as stack:
        sc = Scope(nc, stack)
        C = {"ident": sc.sb("ident", [P, P]), "mhalf": sc.sb("mhalf", [P, 8])}
        yacc = sc.sb("yacc", [P, B * TT, D])
        xT = [sc.sb("xT_hi", [P, KT, B * S], F16), sc.sb("xT_lo", [P, KT, B * S], F16)]
        with ExitStack() as first:
            s0 = Scope(nc, first)
            for n, shape, dt in (("rel", [P, S], F32), ("sel", [P, 8, P], F16), ("pairmask", [P, 2], F32),
                                 ("bias", [P, D], F32)):
                C[n] = s0.sb(n, shape, dt)
            W0 = {n: [s0.sb(f"{n}_hi", [P, KT, w], F16), s0.sb(f"{n}_lo", [P, KT, w], F16)]
                  for n, w in (("wq", D), ("wkv", P + E0), ("wo", D), ("wf", D))}
            W0["gm"] = s0.sb("gm0", [P, 4])
            with ExitStack() as second:
                ss = Scope(nc, second)
                raw = {n: ss.sb(f"raw_{n}", [P, KT, w], F32)
                       for n, w in (("wq", D), ("wkv", P + E0), ("wo", D), ("wf", D))}
                codes = ss.sb("codes", [P, KT, D], I32)
                qsc = ss.sb("qscales", [P, KT, D])
                rg = ss.sb("rg0", [P, 4])
                s_c = ss.sem("s_constants_loaded")
                fuse = FusedUpProjections(nc, ss, A, fused_dram)

                def first_loads(sp):
                    fuse.load(sp, 0)
                    fuse.load(sp, 1)

                def other_loads(sp):
                    for part in range(2, len(fuse.s_ld)):
                        fuse.load(sp, part)
                    for n in ("ident", "rel", "pairmask"):
                        sp.dma_start(C[n][:, :], A[n]).then_inc(s_c, 16)
                    sp.dma_start(C["sel"][:, :, :], A["sel"]).then_inc(s_c, 16)
                    sp.dma_start(C["bias"][:, :], A["bias"].partition_broadcast(P)).then_inc(s_c, 16)
                    fuse.store(sp)
                    sp.wait_ge(s_c, 16 * 5)

                def clear_constants(pool):
                    pool.memset(C["mhalf"][:, :], -0.5)
                    pool.memset(yacc[:, :, :], 0.0)

                def km(ap):
                    return ap.rearrange("(k p) n -> p k n", p=P)

                jobs = []
                for n, loads in (("wq", [(raw["wq"][:, :, :], km(A["wq0"]))]),
                                 ("wkv", [(raw["wkv"][:, :, 0:P], km(A["wk0"])),
                                          (raw["wkv"][:, :, P:P + E0], km(A["wv0"]))]),
                                 ("wo", [(raw["wo"][:, :, :], km(A["wo0"]))]),
                                 ("wf", [(codes[:, :, :], km(A["codes"])), (qsc[:, :, :], km(A["qscales"]))])):
                    job = [n, loads, raw[n][:, :, :], W0[n][0][:, :, :], W0[n][1][:, :, :]]
                    if n == "wf":
                        job.append((codes[:, :, :], qsc[:, :, :]))
                    jobs.append(job)
                split_matrices(nc, ss, "w0", jobs, W0["gm"], rg, {"sync": first_loads, "gpsimd": clear_constants},
                               {"sync": other_loads, "tensor": fuse.multiply, "scalar": fuse.copy})
                clear(nc, ss.sems)
            layer0(nc, A, W0, C, xT, x2_dram)
        if stages < 2:
            return
        raw_down = sc.sb("raw_down", [P, HT, D])
        s_r = sc.sem("s_down_loaded")
        full = (HT - 1) * P

        def load_down(sp):
            sp.dma_start(raw_down[:, 0:HT - 1, :],
                         A["w_down"][0:full].rearrange("(k p) n -> p k n", p=P)).then_inc(s_r, 16)
            sp.dma_start(raw_down[0:HID - full, HT - 1, :], A["w_down"][full:HID, :]).then_inc(s_r, 16)

        attention1(nc, A, C, xT, yacc, fused_dram, load_down)
        with nc.Block() as block:

            @block.vector
            def _(dve):
                dve.wait_ge(s_r, 16 * 2)

        if stages < 3:
            return
        feed_forward1(nc, A, C, raw_down, yacc, x2_dram, out)


def octonion_table():
    table = np.zeros((8, 8, 8), np.float32)
    table[0, 0, 0] = 1.0
    for i in range(1, 8):
        table[0, i, i] = table[i, 0, i] = 1.0
        table[i, i, 0] = -1.0
    for a, b, c in [(1, 2, 3), (1, 4, 5), (1, 7, 6), (2, 4, 6), (2, 5, 7), (3, 4, 7), (3, 6, 5)]:
        for x, y, z in ((a, b, c), (b, c, a), (c, a, b)):
            table[x, y, z] = 1.0
            table[y, x, z] = -1.0
    return np.abs(table).argmax(0), table.sum(0)


def constants():
    out = {"ident": np.eye(P, dtype=np.float32)}
    rel = (np.arange(S)[None, :] - (S - P) - np.arange(P)[:, None]).astype(np.float32)
    out["rel"] = np.where(rel <= 0, rel, np.float32(MASKED)).astype(np.float32)
    out["mask"] = np.where(rel <= 0, 0.0, MASKED).astype(np.float32)
    sel = np.zeros((P, 4, 2, P), np.float16)
    for r in range(4):
        for x in range(32):
            sel[32 * r + x, r, 0, [x, 64 + x]] = 1
            sel[32 * r + x, r, 1, [32 + x, 96 + x]] = 1
    out["sel"] = sel.reshape(P, 8, P)
    low = (np.arange(P) % 32 < 16).astype(np.float32)
    out["pairmask"] = np.stack([low, 1 - low], 1)
    inv_freq = 1.0 / 10000.0 ** (np.arange(0, E1, 2, dtype=np.float32) / E1)
    freqs = np.outer(np.arange(S, dtype=np.float32), inv_freq)
    emb = np.concatenate([freqs, freqs], -1).T
    cos, sin = np.cos(emb).astype(np.float32), np.sin(emb).astype(np.float32)
    sin[:E1 // 2] *= -1
    roped = (np.arange(E1) % (E1 // 2) < 32)[:, None]
    out["cosq"], out["sinq"] = cos, sin
    out["cosk"] = np.where(roped, cos, 1.0).astype(np.float32)
    out["sink"] = np.where(roped, sin, 0.0).astype(np.float32)
    sign = octonion_table()[1]
    rows = np.minimum(np.arange(HT * P), HID - 1).reshape(HT, P) // OH
    out["sgn_dn"] = np.ascontiguousarray(-sign[rows].transpose(1, 0, 2)).astype(np.float16)
    return out


def lay_out(inputs):
    a = {k: np.asarray(v) for k, v in inputs.items()}
    unit = octonion_table()[0]
    i = np.arange(8)[:, None]
    k = np.arange(8)[None, :]
    wkv = a["L0_attn_Wkv"]
    out = {
        "x": a["L0_attn_hidden_states"],
        "wq0": a["L0_attn_Wq"],
        "wk0": np.tile(wkv[:, :E0], (1, P // E0)),
        "wv0": wkv[:, E0:],
        "wo0": a["L0_attn_Wo"],
        "codes": a["L0_ffn_q_vals"].reshape(D, D).T,
        "qscales": np.repeat(a["L0_ffn_q_scales"].T, 32, axis=0),
        "bias": a["L0_ffn_bias"],
        "wq1": a["L1_attn_Wq"].reshape(G1, HG * E1, KT, P).transpose(0, 3, 2, 1),
        "wkr1": a["L1_attn_Wkr"].reshape(G1, 64, KT, P).transpose(0, 3, 2, 1),
        "wdk1": a["L1_attn_Wdk"],
        "wup1": np.concatenate([a["L1_attn_Wupk"].reshape(G1, 64, D), a["L1_attn_Wupv"].reshape(G1, E1, D)],
                               1).reshape(G1 * UP, D).T,
        "wo1": a["L1_attn_Wo"].reshape(D, G1, HG, E1).transpose(1, 3, 2, 0),
        "w_gate": a["L1_ffn_w_gate"].transpose(2, 0, 1).reshape(OD, 8 * OH),
        "w_up": a["L1_ffn_w_up"].transpose(2, 0, 1).reshape(OD, 8 * OH),
        "w_down_once": a["L1_ffn_w_down"].reshape(P, OH * D // P),
        "w_down": a["L1_ffn_w_down"][unit[i, k]].transpose(0, 3, 1, 2).reshape(HID, D),
    }
    out.update(constants())
    return {n: np.ascontiguousarray(v) for n, v in out.items()}


def declare(nc, arrays):
    return {n: nc.dram_tensor(f"in_{n}", v.shape, mybir.dt.from_np(v.dtype), kind="ExternalInput").ap()
            for n, v in arrays.items()}


def kernel(**inputs):
    import concourse.bacc as bacc
    from concourse.bass_utils import run_bass_kernel_spmd

    arrays = lay_out(inputs)
    nc = bacc.Bacc("TRN2", target_bir_lowering=False, num_devices=1)
    A = declare(nc, arrays)
    out = nc.dram_tensor("out_x", [B, S, D], F32, kind="ExternalOutput").ap()
    build(nc, A, out)
    r = run_bass_kernel_spmd(nc, [{f"in_{n}": v for n, v in arrays.items()}], core_ids=[0])
    return r.results[0]["out_x"]
```
